# Optimizing a Trainium2 kernel written in Bass

```python
import numpy as np
import jax
import jax.numpy as jnp

def _softmax(x, axis=-1):
    return jax.nn.softmax(x, axis=axis)

def _gelu(x):
    return jax.nn.gelu(x, approximate=True)

def _silu(x):
    return jax.nn.silu(x)

def _sigmoid(x):
    return jax.nn.sigmoid(x)

def _layernorm(x, axis=-1, eps=1e-05):
    m = jnp.mean(x, axis=axis, keepdims=True)
    v = jnp.var(x, axis=axis, keepdims=True)
    return (x - m) / jnp.sqrt(v + eps)

def _scatter_add(tgt, idx, src, axis=0):
    return tgt.at[idx].add(src)

def _segment_sum(src, seg, n):
    return jax.ops.segment_sum(src, seg, n)
kernel_name = 'mk_xattn_ffn_d2_seqx_r8_77def8'

def setup_inputs(seed: int=0):
    np.random.seed(seed)
    _w = jnp.asarray

    def _rec_inputs():
        import jax
        import jax.numpy as jnp
        _rk = jax.random.key(seed)
        x = 7.22e-05 + 1 * jax.random.normal(jax.random.fold_in(_rk, 1), (4, 512, 128), jnp.float32)
        _lenS = 512 - jax.random.randint(jax.random.fold_in(_rk, 7), (4,), 0, max(1, 512 // 4) + 1, jnp.int32)
        _lenS2 = 32 - jax.random.randint(jax.random.fold_in(_rk, 8), (4,), 0, max(1, 32 // 4) + 1, jnp.int32)
        _ctx_1024P = jax.random.normal(jax.random.fold_in(_rk, 11), (4, 16, 128), jnp.float32)
        _ctx_1024c = jax.random.dirichlet(jax.random.fold_in(_rk, 511), 0.3 * jnp.ones((16,), jnp.float32), (4, 32))
        _ctx_1024t = jnp.einsum('bsk,bkd->bsd', _ctx_1024c, _ctx_1024P)
        _ctx_1024t = _ctx_1024t * jax.lax.rsqrt(jnp.mean(jnp.square(_ctx_1024t)) + 1e-12) * 0.953939
        ctx_1024 = 2.81802e-05 + 1.00001 * (_ctx_1024t + 0.3 * jax.random.normal(jax.random.fold_in(_rk, 611), (4, 32, 128), jnp.float32))
        _validS = jnp.arange(512)[None, :] < _lenS[:, None]
        _validS2 = jnp.arange(32)[None, :] < _lenS2[:, None]
        _causal = jnp.tril(jnp.ones((512, 512), dtype=bool))
        mask_BxS2_bk0 = jnp.logical_not(jnp.broadcast_to(_validS2[:, :], (4, 32)))
        return (x, ctx_1024, mask_BxS2_bk0)
    x, ctx_1024, mask_BxS2_bk0 = _rec_inputs()

    def _L0_xattn_setup():
        import jax, jax.numpy as jnp
        import numpy as np
        B, NT, NM, C, H, FF = (8, 128, 256, 128, 8, 512)

        def _ln(x, g, b):
            m = x.mean(-1, keepdims=True)
            v = jnp.mean((x - m) ** 2, axis=-1, keepdims=True)
            return (x - m) / jnp.sqrt(v + 1e-05) * g + b
        key = jax.random.key(seed)
        ks = jax.random.split(key, 8)
        w = lambda k, shape, s=0.02: jax.random.normal(k, shape, dtype=jnp.float32) * s
        return {'tgt': jax.random.normal(ks[0], (B, NT, C), dtype=jnp.float32), 'memory': jax.random.normal(ks[1], (B, NM, C), dtype=jnp.float32), 'qkv_w': w(ks[2], (3 * C, C)), 'qkv_b': jnp.zeros((3 * C,), jnp.float32), 'sa_out_w': w(ks[3], (C, C)), 'sa_out_b': jnp.zeros((C,), jnp.float32), 'in_proj_w': w(ks[4], (3 * C, C)), 'in_proj_b': jnp.zeros((3 * C,), jnp.float32), 'mha_out_w': w(ks[5], (C, C)), 'mha_out_b': jnp.zeros((C,), jnp.float32), 'lin1_w': w(ks[6], (FF, C)), 'lin1_b': jnp.zeros((FF,), jnp.float32), 'lin2_w': w(ks[7], (C, FF)), 'lin2_b': jnp.zeros((C,), jnp.float32), 'ln1_g': jnp.ones((C,), jnp.float32), 'ln1_b': jnp.zeros((C,), jnp.float32), 'ln2_g': jnp.ones((C,), jnp.float32), 'ln2_b': jnp.zeros((C,), jnp.float32), 'ln3_g': jnp.ones((C,), jnp.float32), 'ln3_b': jnp.zeros((C,), jnp.float32)}
    _L0_xattn_all = _L0_xattn_setup()
    _L0_xattn_in = {k: v for k, v in _L0_xattn_all.items() if k in ('qkv_w', 'qkv_b', 'sa_out_w', 'sa_out_b', 'in_proj_w', 'in_proj_b', 'mha_out_w', 'mha_out_b', 'lin1_w', 'lin1_b', 'lin2_w', 'lin2_b', 'ln1_g', 'ln1_b', 'ln2_g', 'ln2_b', 'ln3_g', 'ln3_b')}
    del _L0_xattn_all

    def _L0_ffn_setup():
        import jax, jax.numpy as jnp
        import numpy as np
        D_MODEL = 128
        EXPERT_DIM = 128
        NUM_EXPERTS = 8
        TOP_K = 2
        B, T = (8, 512)
        key = jax.random.key(seed)
        ks = jax.random.split(key, 5)
        scale_in = 1.0 / np.sqrt(D_MODEL)
        scale_h = 1.0 / np.sqrt(EXPERT_DIM)
        return {'x': jax.random.normal(ks[0], (B, T, D_MODEL), dtype=jnp.float32), 'gate_w': jax.random.normal(ks[1], (D_MODEL, NUM_EXPERTS), dtype=jnp.float32) * scale_in, 'gate_b': jnp.zeros((NUM_EXPERTS,), dtype=jnp.float32), 'w1': jax.random.normal(ks[2], (NUM_EXPERTS, D_MODEL, EXPERT_DIM), dtype=jnp.float32) * scale_in, 'b1': jnp.zeros((NUM_EXPERTS, EXPERT_DIM), dtype=jnp.float32), 'w2': jax.random.normal(ks[3], (NUM_EXPERTS, EXPERT_DIM, D_MODEL), dtype=jnp.float32) * scale_h, 'b2': jnp.zeros((NUM_EXPERTS, D_MODEL), dtype=jnp.float32)}
    _L0_ffn_all = _L0_ffn_setup()
    _L0_ffn_in = {k: v for k, v in _L0_ffn_all.items() if k in ('gate_w', 'gate_b', 'w1', 'b1', 'w2', 'b2')}
    del _L0_ffn_all

    def _L1_xattn_setup():
        import jax, jax.numpy as jnp
        import numpy as np
        DIM, DIM_HEAD, HEADS, SCALE = (128, 64, 8, 8.0)
        INNER = DIM_HEAD * HEADS
        LN_EPS = 1e-05
        L2_EPS = 1e-12

        def layer_norm(x, w, b):
            mu = jnp.mean(x, axis=-1, keepdims=True)
            var = jnp.mean(jnp.square(x - mu), axis=-1, keepdims=True)
            return (x - mu) * jax.lax.rsqrt(var + LN_EPS) * w + b

        def l2norm(t):
            n = jnp.sqrt(jnp.sum(jnp.square(t), axis=-1, keepdims=True))
            return t / jnp.maximum(n, L2_EPS)
        key = jax.random.key(seed)
        ks = jax.random.split(key, 8)
        b, n, m = (8, 1024, 64)
        x = jax.random.normal(ks[0], (b, n, DIM), dtype=jnp.float32)
        latents = jax.random.normal(ks[1], (b, m, DIM), dtype=jnp.float32)
        mask = jax.random.randint(ks[2], (b, n), 0, 2) > 0
        Wq = jax.random.normal(ks[3], (DIM, INNER), dtype=jnp.float32) * DIM ** (-0.5)
        Wkv = jax.random.normal(ks[4], (DIM, 2 * INNER), dtype=jnp.float32) * DIM ** (-0.5)
        Wo = jax.random.normal(ks[5], (INNER, DIM), dtype=jnp.float32) * INNER ** (-0.5)
        return {'x': x, 'latents': latents, 'mask': mask, 'ln_x_w': jnp.ones((DIM,)), 'ln_x_b': jnp.zeros((DIM,)), 'ln_l_w': jnp.ones((DIM,)), 'ln_l_b': jnp.zeros((DIM,)), 'Wq': Wq, 'Wkv': Wkv, 'q_scale': jnp.ones((DIM_HEAD,)), 'k_scale': jnp.ones((DIM_HEAD,)), 'Wo': Wo, 'ln_o_w': jnp.ones((DIM,)), 'ln_o_b': jnp.zeros((DIM,))}
    _L1_xattn_all = _L1_xattn_setup()
    _L1_xattn_in = {k: v for k, v in _L1_xattn_all.items() if k in ('ln_x_w', 'ln_x_b', 'ln_l_w', 'ln_l_b', 'Wq', 'Wkv', 'q_scale', 'k_scale', 'Wo', 'ln_o_w', 'ln_o_b')}
    del _L1_xattn_all

    def _L1_ffn_setup():
        import jax, jax.numpy as jnp
        import numpy as np
        H = 128
        I = 64
        E = 32
        TOP_K = 6
        N_GROUP = 8
        TOPK_GROUP = 4
        SCALE = 2.5
        N_SHARED = 2
        SI = I * N_SHARED
        B, S = (2, 128)
        key = jax.random.key(seed)
        ks = jax.random.split(key, 8)
        x = jax.random.normal(ks[0], (B, S, H), jnp.float32)
        gate_weight = jax.random.normal(ks[1], (E, H), jnp.float32) * 0.02
        e_score_correction_bias = jax.random.normal(ks[2], (E,), jnp.float32) * 0.01
        experts_gate_up = jax.random.normal(ks[3], (E, 2 * I, H), jnp.float32) * 0.02
        experts_down = jax.random.normal(ks[4], (E, H, I), jnp.float32) * 0.02
        shared_gate_w = jax.random.normal(ks[5], (SI, H), jnp.float32) * 0.02
        shared_up_w = jax.random.normal(ks[6], (SI, H), jnp.float32) * 0.02
        shared_down_w = jax.random.normal(ks[7], (H, SI), jnp.float32) * 0.02
        return {'x': x, 'gate_weight': gate_weight, 'e_score_correction_bias': e_score_correction_bias, 'experts_gate_up': experts_gate_up, 'experts_down': experts_down, 'shared_gate_w': shared_gate_w, 'shared_up_w': shared_up_w, 'shared_down_w': shared_down_w}
    _L1_ffn_all = _L1_ffn_setup()
    _L1_ffn_in = {k: v for k, v in _L1_ffn_all.items() if k in ('gate_weight', 'e_score_correction_bias', 'experts_gate_up', 'experts_down', 'shared_gate_w', 'shared_up_w', 'shared_down_w')}
    del _L1_ffn_all
    return {'x': x, 'ctx_1024': ctx_1024, 'mask_BxS2_bk0': mask_BxS2_bk0, 'L0_xattn_qkv_w': _L0_xattn_in['qkv_w'], 'L0_xattn_qkv_b': _L0_xattn_in['qkv_b'], 'L0_xattn_sa_out_w': _L0_xattn_in['sa_out_w'], 'L0_xattn_sa_out_b': _L0_xattn_in['sa_out_b'], 'L0_xattn_in_proj_w': _L0_xattn_in['in_proj_w'], 'L0_xattn_in_proj_b': _L0_xattn_in['in_proj_b'], 'L0_xattn_mha_out_w': _L0_xattn_in['mha_out_w'], 'L0_xattn_mha_out_b': _L0_xattn_in['mha_out_b'], 'L0_xattn_lin1_w': _L0_xattn_in['lin1_w'], 'L0_xattn_lin1_b': _L0_xattn_in['lin1_b'], 'L0_xattn_lin2_w': _L0_xattn_in['lin2_w'], 'L0_xattn_lin2_b': _L0_xattn_in['lin2_b'], 'L0_xattn_ln1_g': _L0_xattn_in['ln1_g'], 'L0_xattn_ln1_b': _L0_xattn_in['ln1_b'], 'L0_xattn_ln2_g': _L0_xattn_in['ln2_g'], 'L0_xattn_ln2_b': _L0_xattn_in['ln2_b'], 'L0_xattn_ln3_g': _L0_xattn_in['ln3_g'], 'L0_xattn_ln3_b': _L0_xattn_in['ln3_b'], 'L0_ffn_gate_w': _L0_ffn_in['gate_w'], 'L0_ffn_gate_b': _L0_ffn_in['gate_b'], 'L0_ffn_w1': _L0_ffn_in['w1'], 'L0_ffn_b1': _L0_ffn_in['b1'], 'L0_ffn_w2': _L0_ffn_in['w2'], 'L0_ffn_b2': _L0_ffn_in['b2'], 'L1_xattn_ln_x_w': _L1_xattn_in['ln_x_w'], 'L1_xattn_ln_x_b': _L1_xattn_in['ln_x_b'], 'L1_xattn_ln_l_w': _L1_xattn_in['ln_l_w'], 'L1_xattn_ln_l_b': _L1_xattn_in['ln_l_b'], 'L1_xattn_Wq': _L1_xattn_in['Wq'], 'L1_xattn_Wkv': _L1_xattn_in['Wkv'], 'L1_xattn_q_scale': _L1_xattn_in['q_scale'], 'L1_xattn_k_scale': _L1_xattn_in['k_scale'], 'L1_xattn_Wo': _L1_xattn_in['Wo'], 'L1_xattn_ln_o_w': _L1_xattn_in['ln_o_w'], 'L1_xattn_ln_o_b': _L1_xattn_in['ln_o_b'], 'L1_ffn_gate_weight': _L1_ffn_in['gate_weight'], 'L1_ffn_e_score_correction_bias': _L1_ffn_in['e_score_correction_bias'], 'L1_ffn_experts_gate_up': _L1_ffn_in['experts_gate_up'], 'L1_ffn_experts_down': _L1_ffn_in['experts_down'], 'L1_ffn_shared_gate_w': _L1_ffn_in['shared_gate_w'], 'L1_ffn_shared_up_w': _L1_ffn_in['shared_up_w'], 'L1_ffn_shared_down_w': _L1_ffn_in['shared_down_w']}

def reference(x, ctx_1024, mask_BxS2_bk0, L0_xattn_qkv_w, L0_xattn_qkv_b, L0_xattn_sa_out_w, L0_xattn_sa_out_b, L0_xattn_in_proj_w, L0_xattn_in_proj_b, L0_xattn_mha_out_w, L0_xattn_mha_out_b, L0_xattn_lin1_w, L0_xattn_lin1_b, L0_xattn_lin2_w, L0_xattn_lin2_b, L0_xattn_ln1_g, L0_xattn_ln1_b, L0_xattn_ln2_g, L0_xattn_ln2_b, L0_xattn_ln3_g, L0_xattn_ln3_b, L0_ffn_gate_w, L0_ffn_gate_b, L0_ffn_w1, L0_ffn_b1, L0_ffn_w2, L0_ffn_b2, L1_xattn_ln_x_w, L1_xattn_ln_x_b, L1_xattn_ln_l_w, L1_xattn_ln_l_b, L1_xattn_Wq, L1_xattn_Wkv, L1_xattn_q_scale, L1_xattn_k_scale, L1_xattn_Wo, L1_xattn_ln_o_w, L1_xattn_ln_o_b, L1_ffn_gate_weight, L1_ffn_e_score_correction_bias, L1_ffn_experts_gate_up, L1_ffn_experts_down, L1_ffn_shared_gate_w, L1_ffn_shared_up_w, L1_ffn_shared_down_w):
    import jax
    import jax.numpy as jnp

    def _L0_xattn_ref(tgt, memory, qkv_w, qkv_b, sa_out_w, sa_out_b, in_proj_w, in_proj_b, mha_out_w, mha_out_b, lin1_w, lin1_b, lin2_w, lin2_b, ln1_g, ln1_b, ln2_g, ln2_b, ln3_g, ln3_b):
        import jax, jax.numpy as jnp
        import numpy as np
        B, NT, NM, C, H, FF = (8, 128, 256, 128, 8, 512)

        def _ln(x, g, b):
            m = x.mean(-1, keepdims=True)
            v = jnp.mean((x - m) ** 2, axis=-1, keepdims=True)
            return (x - m) / jnp.sqrt(v + 1e-05) * g + b
        Bx, N, Cx = tgt.shape
        qkv = tgt @ qkv_w.T + qkv_b
        q, k, v = jnp.split(qkv, 3, axis=-1)
        scores = jnp.einsum('bnc,bmc->bnm', q, k) * jnp.sqrt(jnp.float32(Cx))
        diag = jnp.eye(N, dtype=bool)
        scores = jnp.where(diag[None, :, :], scores, -jnp.inf)
        attn = jax.nn.softmax(scores, axis=-1)
        sa = jnp.einsum('bnm,bmc->bnc', attn, v) @ sa_out_w.T + sa_out_b
        x = _ln(tgt + sa, ln1_g, ln1_b)
        d = Cx // H
        wq, wk, wv = jnp.split(in_proj_w, 3, axis=0)
        bq, bk, bv = jnp.split(in_proj_b, 3, axis=0)
        qh = (x @ wq.T + bq).reshape(Bx, N, H, d).transpose(0, 2, 1, 3)
        kh = (memory @ wk.T + bk).reshape(Bx, -1, H, d).transpose(0, 2, 1, 3)
        vh = (memory @ wv.T + bv).reshape(Bx, -1, H, d).transpose(0, 2, 1, 3)
        a = jax.nn.softmax(jnp.einsum('bhnd,bhmd->bhnm', qh, kh) / jnp.sqrt(jnp.float32(d)), axis=-1)
        ca = jnp.einsum('bhnm,bhmd->bhnd', a, vh).transpose(0, 2, 1, 3).reshape(Bx, N, Cx)
        ca = ca @ mha_out_w.T + mha_out_b
        x = _ln(x + ca, ln2_g, ln2_b)
        ff = jax.nn.relu(x @ lin1_w.T + lin1_b) @ lin2_w.T + lin2_b
        return _ln(x + ff, ln3_g, ln3_b)

    def _L0_ffn_ref(x, gate_w, gate_b, w1, b1, w2, b2):
        import jax, jax.numpy as jnp
        import numpy as np
        D_MODEL = 128
        EXPERT_DIM = 128
        NUM_EXPERTS = 8
        TOP_K = 2
        B, T = (8, 512)
        b, t, d = x.shape
        xf = x.reshape(b * t, d)
        scores = xf @ gate_w + gate_b
        topk_s, topk_i = jax.lax.top_k(scores, TOP_K)
        n = xf.shape[0]
        comb = jnp.zeros_like(scores).at[jnp.arange(n)[:, None], topk_i].add(topk_s)
        h = jnp.maximum(jnp.einsum('nd,edh->neh', xf, w1) + b1, 0.0)
        eo = jnp.einsum('neh,ehd->ned', h, w2) + b2
        out = jnp.einsum('ne,ned->nd', comb, eo)
        return out.reshape(b, t, d)

    def _L1_xattn_ref(x, latents, mask, ln_x_w, ln_x_b, ln_l_w, ln_l_b, Wq, Wkv, q_scale, k_scale, Wo, ln_o_w, ln_o_b):
        import jax, jax.numpy as jnp
        import numpy as np
        DIM, DIM_HEAD, HEADS, SCALE = (128, 64, 8, 8.0)
        INNER = DIM_HEAD * HEADS
        LN_EPS = 1e-05
        L2_EPS = 1e-12

        def layer_norm(x, w, b):
            mu = jnp.mean(x, axis=-1, keepdims=True)
            var = jnp.mean(jnp.square(x - mu), axis=-1, keepdims=True)
            return (x - mu) * jax.lax.rsqrt(var + LN_EPS) * w + b

        def l2norm(t):
            n = jnp.sqrt(jnp.sum(jnp.square(t), axis=-1, keepdims=True))
            return t / jnp.maximum(n, L2_EPS)
        b, n, _ = x.shape
        m = latents.shape[1]
        x = layer_norm(x, ln_x_w, ln_x_b)
        latents = layer_norm(latents, ln_l_w, ln_l_b)
        q = latents @ Wq
        kv_input = jnp.concatenate([x, latents], axis=1)
        kv = kv_input @ Wkv
        k, v = jnp.split(kv, 2, axis=-1)

        def to_heads(t):
            return t.reshape(t.shape[0], t.shape[1], HEADS, DIM_HEAD).transpose(0, 2, 1, 3)
        q, k, v = map(to_heads, (q, k, v))
        q = l2norm(q) * q_scale
        k = l2norm(k) * k_scale
        sim = jnp.einsum('bhid,bhjd->bhij', q, k) * SCALE
        full_mask = jnp.concatenate([mask, jnp.ones((b, m), dtype=bool)], axis=1)[:, None, None, :]
        max_neg = -jnp.finfo(sim.dtype).max
        sim = jnp.where(full_mask, sim, max_neg)
        attn = jax.nn.softmax(sim.astype(jnp.float32), axis=-1).astype(sim.dtype)
        out = jnp.einsum('bhij,bhjd->bhid', attn, v)
        out = out.transpose(0, 2, 1, 3).reshape(b, m, INNER)
        return layer_norm(out @ Wo, ln_o_w, ln_o_b)

    def _L1_ffn_ref(x, gate_weight, e_score_correction_bias, experts_gate_up, experts_down, shared_gate_w, shared_up_w, shared_down_w):
        import jax, jax.numpy as jnp
        import numpy as np
        H = 128
        I = 64
        E = 32
        TOP_K = 6
        N_GROUP = 8
        TOPK_GROUP = 4
        SCALE = 2.5
        N_SHARED = 2
        SI = I * N_SHARED
        B, S = (2, 128)
        b, s, h = x.shape
        xf = x.reshape(-1, h)
        T = xf.shape[0]
        logits = xf.astype(jnp.float32) @ gate_weight.astype(jnp.float32).T
        scores = jax.nn.sigmoid(logits)
        sfc = scores + e_score_correction_bias[None, :]
        gs = E // N_GROUP
        group_scores = sfc.reshape(T, N_GROUP, gs).max(axis=-1)
        _, gidx = jax.lax.top_k(group_scores, TOPK_GROUP)
        gmask = jnp.zeros((T, N_GROUP), bool).at[jnp.arange(T)[:, None], gidx].set(True)
        smask = jnp.repeat(gmask, gs, axis=1)
        masked = jnp.where(smask, sfc, 0.0)
        _, topk_idx = jax.lax.top_k(masked, TOP_K)
        tw = jnp.take_along_axis(scores, topk_idx, axis=1)
        tw = tw / (tw.sum(-1, keepdims=True) + 1e-20)
        tw = (tw * SCALE).astype(xf.dtype)
        combine = jnp.zeros((T, E), xf.dtype).at[jnp.arange(T)[:, None], topk_idx].add(tw)

        def expert_step(acc, inp):
            gu, dn, c = inp
            g = xf @ gu[:I].T
            u = xf @ gu[I:].T
            o = jax.nn.silu(g) * u @ dn.T
            return (acc + c[:, None] * o, None)
        routed, _ = jax.lax.scan(expert_step, jnp.zeros_like(xf), (experts_gate_up, experts_down, combine.T))
        sh = jax.nn.silu(xf @ shared_gate_w.T) * (xf @ shared_up_w.T)
        shared_out = sh @ shared_down_w.T
        return (routed + shared_out).reshape(b, s, h)
    x = x + _L0_xattn_ref(_layernorm(x, axis=-1), ctx_1024, L0_xattn_qkv_w, L0_xattn_qkv_b, L0_xattn_sa_out_w, L0_xattn_sa_out_b, L0_xattn_in_proj_w, L0_xattn_in_proj_b, L0_xattn_mha_out_w, L0_xattn_mha_out_b, L0_xattn_lin1_w, L0_xattn_lin1_b, L0_xattn_lin2_w, L0_xattn_lin2_b, L0_xattn_ln1_g, L0_xattn_ln1_b, L0_xattn_ln2_g, L0_xattn_ln2_b, L0_xattn_ln3_g, L0_xattn_ln3_b)
    x = x + _L0_ffn_ref(_layernorm(x, axis=-1), L0_ffn_gate_w, L0_ffn_gate_b, L0_ffn_w1, L0_ffn_b1, L0_ffn_w2, L0_ffn_b2)
    x = x + _L1_xattn_ref(ctx_1024, _layernorm(x, axis=-1), mask_BxS2_bk0, L1_xattn_ln_x_w, L1_xattn_ln_x_b, L1_xattn_ln_l_w, L1_xattn_ln_l_b, L1_xattn_Wq, L1_xattn_Wkv, L1_xattn_q_scale, L1_xattn_k_scale, L1_xattn_Wo, L1_xattn_ln_o_w, L1_xattn_ln_o_b)
    x = x + _L1_ffn_ref(_layernorm(x, axis=-1), L1_ffn_gate_weight, L1_ffn_e_score_correction_bias, L1_ffn_experts_gate_up, L1_ffn_experts_down, L1_ffn_shared_gate_w, L1_ffn_shared_up_w, L1_ffn_shared_down_w)
    return x

_drawn_inputs = setup_inputs


def setup_inputs(seed=0):
    import zlib

    import numpy as np

    out = dict(_drawn_inputs(seed))
    spreads = {'L0_xattn_qkv_b': (0.0, 0.1),
     'L0_xattn_sa_out_b': (0.0, 0.1),
     'L0_xattn_in_proj_b': (0.0, 0.1),
     'L0_xattn_mha_out_b': (0.0, 0.1),
     'L0_xattn_lin1_b': (0.0, 0.1),
     'L0_xattn_lin2_b': (0.0, 0.1),
     'L0_xattn_ln1_g': (1.0, 0.2),
     'L0_xattn_ln1_b': (0.0, 0.1),
     'L0_xattn_ln2_g': (1.0, 0.2),
     'L0_xattn_ln2_b': (0.0, 0.1),
     'L0_xattn_ln3_g': (1.0, 0.2),
     'L0_xattn_ln3_b': (0.0, 0.1),
     'L0_ffn_gate_b': (0.0, 0.1),
     'L0_ffn_b1': (0.0, 0.1),
     'L0_ffn_b2': (0.0, 0.1),
     'L1_xattn_ln_x_w': (1.0, 0.6),
     'L1_xattn_ln_x_b': (0.0, 0.8),
     'L1_xattn_ln_l_w': (1.0, 0.2),
     'L1_xattn_ln_l_b': (0.0, 0.1),
     'L1_xattn_q_scale': (1.0, 0.2),
     'L1_xattn_k_scale': (1.0, 0.2),
     'L1_xattn_ln_o_w': (1.0, 0.2),
     'L1_xattn_ln_o_b': (0.0, 0.1)}
    factors = {'L1_ffn_gate_weight': 8.0,
     'L1_ffn_e_score_correction_bias': 8.0,
     'L1_ffn_experts_gate_up': 8.0,
     'L1_ffn_experts_down': 8.0,
     'L1_ffn_shared_gate_w': 8.0,
     'L1_ffn_shared_up_w': 8.0,
     'L1_ffn_shared_down_w': 8.0}
    for name, (base, spread) in spreads.items():
        noise = np.random.default_rng([zlib.crc32(name.encode()), seed]).standard_normal(out[name].shape)
        drawn = base * np.exp(spread * noise) if base else spread * noise
        out[name] = jnp.asarray(drawn.astype(out[name].dtype))
    for name, factor in factors.items():
        out[name] = (out[name] * factor).astype(out[name].dtype)
    return out
```

```python
from contextlib import ExitStack

import concourse.bass as bass
from concourse import mybir

F32 = mybir.dt.float32
U8 = mybir.dt.uint8
ALU = mybir.AluOpType
ACT = mybir.ActivationFunctionType
AX = mybir.AxisListType

P = 128
B, S, M = 4, 512, 32
NT = S // P
H0, D0 = 8, 16
FF = 512
FC = FF // P
E0 = 8
K0 = 2
H1, D1 = 8, 64
INNER = H1 * D1
PAIRS = H1 // 2
HG = P // M
E1, I1 = 32, 64
EP = E1 // 2
NG, TG, K1 = 8, 4, 6
GS = E1 // NG
ROUTE_SCALE = 2.5
SIM_SCALE = 8.0
EPS = 1e-5
L2_EPS = 1e-12
SENT = -3.0e38
PICK = 3.0e38
MASKED = 1.0e30
EXP_ROOM = 80.0
ITERS = B // 2

SLAB_A = [("ident", P), ("head_of_row", H0),
          ("sa_b", 1), ("sa_bv", 1), ("ln1_g", 1), ("ln1_b", 1), ("bq", 1), ("bk", 1), ("bv", 1), ("mha_b", 1),
          ("ln2_g", 1), ("ln2_b", 1), ("lin1_b", FC), ("lin2_b", 1), ("b1", E0), ("lnl_w", 1), ("lnl_b", 1),
          ("lnx_w", 1), ("lnx_b", 1), ("qs", 1), ("ks", 1),
          ("sa_wv", P), ("sa_oT", P), ("wqT", P), ("wkT", P), ("wvT", P), ("mha_oT", P),
          ("lin1T", FF), ("lin2T", FC * P), ("Wk", INNER), ("Wv", INNER)]
SLAB_B = [("gate_w", E0), ("w1", E0 * P), ("w2", E0 * P)]
SLAB_C = [("Wq", INNER), ("Wo", PAIRS * P)]
SLAB_D = [("route_wT", E1), ("gateT", EP * P), ("upT", EP * P), ("downT", EP * P),
          ("sh_gateT", P), ("sh_upT", P), ("sh_downT", P)]
ROWS = [("ln3_g", P), ("ln3_b", P), ("lno_w", P), ("lno_b", P), ("gate_b", E0), ("route_b", E1),
        ("qs_row", D1), ("ks_row", D1)]
LNS = 8


def width(cols):
    return sum(n for _, n in cols)


def offsets(cols):
    at, out = 0, {}
    for name, n in cols:
        out[name] = (at, n)
        at += n
    return out


def two_layer_kernel(nc, x, ctx_in, mask, slab_a, slab_b, slab_c, slab_d, rows, b2_in, sel0_in, sel1_in, out):
    with ExitStack() as stack:
        def sb(name, shape, dt=F32):
            return stack.enter_context(nc.sbuf_tensor("s_" + name, shape, dt))

        def sem(name):
            return stack.enter_context(nc.semaphore(name))

        def sem2(name):
            return [sem(f"{name}{c}") for c in range(2)]

        WA, WB, WC, WD = (sb(n, [P, width(s)]) for n, s in
                          (("WA", SLAB_A), ("WB", SLAB_B), ("WC", SLAB_C), ("WD", SLAB_D)))
        RW = sb("RW", [P, width(ROWS)])
        where = {}
        for tile_, cols in ((WA, SLAB_A), (WB, SLAB_B), (WC, SLAB_C), (WD, SLAB_D), (RW, ROWS)):
            for name, (at, n) in offsets(cols).items():
                where[name] = tile_[:, at:at + n]

        def W(name, k=None, n=P):
            return where[name] if k is None else where[name][:, k * n:(k + 1) * n]

        ident = W("ident")
        b2 = sb("b2", [E0, P])
        sel0 = sb("sel0", [E0, E0 * P])
        sel1 = sb("sel1", [E1, EP * P])
        maskb = sb("maskb", [P, B], U8)

        foldT = sb("foldT", [P, P])
        fold_b = sb("fold_b", [P, 1])
        Kb_all = sb("Kb_all", [P, B, H0 * M])
        Vp_all = sb("Vp_all", [P, B, 2, P])
        kcT_all = sb("kcT_all", [P, PAIRS, B, M])
        vc_all = sb("vc_all", [P, B, H1 // HG, D1])
        shift = sb("shift", [P, 1])
        mbias = sb("mbias", [P, B])
        prod = sb("prod", [P, D1])
        mhalf = sb("mhalf", [P, 2 * H1])
        eps_row = sb("eps_row", [P, NT])

        X = sb("X", [P, 2, NT * P])
        nrm = sb("nrm", [P, 2, NT * P])
        feat = sb("feat", [P, 2, S])
        res = sb("res", [P, 2, S])
        stat = sb("stat", [P, 2, NT, 6])
        mv = sb("mv", [P, 2, NT, 2])
        ve = sb("ve", [P, 2, NT])
        rstd = sb("rstd", [P, 2, NT])
        tmp4 = sb("tmp4", [P, 2, NT])
        Vp = sb("Vp", [P, 2, 2, P])
        kc = sb("kc", [P, 2, PAIRS, P])
        vc = sb("vc", [P, 2, H1, P])
        mb = sb("mb", [P, 2, 1])
        hmax = sb("hmax", [P, 2, NT * H0])
        hsum = sb("hsum", [P, 2, NT * H0])
        hrec = sb("hrec", [P, 2, NT * H0])
        qT = sb("qT", [P, 2, PAIRS, S])
        kT = sb("kT", [P, 2, PAIRS, S])
        vt = sb("vt", [P, 2, NT, PAIRS, 3 * D1])
        pr = sb("pr", [P, 2, 4, S])
        aT = sb("aT", [P, 2, PAIRS, S])
        ssq = sb("ssq", [P, 2, 2 * H1])
        rn = sb("rn", [P, 2, 2 * H1])
        ssc = sb("ssc", [P, 2, 2 * H1])
        rt0 = sb("rt0", [P, 2, NT, 2 * E0])
        mx = sb("mx", [P, 2, NT, 8])
        top0 = sb("top0", [P, 2, NT, 8])
        hit0 = sb("hit0", [P, 2, NT, 2 * E0])
        comb0 = sb("comb0", [P, 2, NT, E0])
        scor = sb("scor", [P, 2, NT, E1])
        sfc = sb("sfc", [P, 2, NT, E1])
        grp = sb("grp", [P, 2, NT, NG + 8])
        topg = sb("topg", [P, 2, NT, 8])
        hitg = sb("hitg", [P, 2, NT, NG + 8])
        cand = sb("cand", [P, 2, NT, E1 + 8])
        top1 = sb("top1", [P, 2, NT, 8])
        hit1 = sb("hit1", [P, 2, NT, E1 + 8])
        comb1 = sb("comb1", [P, 2, NT, E1])
        csum = sb("csum", [P, 2, NT])
        hT = [qT[:, c] for c in range(2)]
        sc = [kT[:, c, 0:2, :].rearrange("p a s -> p (a s)") for c in range(2)]
        pT = [kT[:, c, 2:4, :] for c in range(2)]
        q0T = [aT[:, c, 0, :] for c in range(2)]
        sq = [aT[:, c, 0:2, :] for c in range(2)]
        qkn = [aT[:, c, 2:4, :] for c in range(2)]
        pc = [(nrm[:, c, :], feat[:, c, :]) for c in range(2)]
        combT = [qT[0:E1, c, 3, :] for c in range(2)]
        Y = [aT[:, c, 3, :] for c in range(2)]
        ctx_tok, memT, kT0, vT0 = (aT[:, 0, 0, k * P:(k + 1) * P] for k in range(4))
        ctx_nrm, ctx_nT = (aT[:, 0, 1, k * P:(k + 1) * P] for k in range(2))
        Vb_all = vt[:, 0].rearrange("p t a d -> p (t a d)")[:, 0:B * H0 * M]
        sqc = vt[:, 1].rearrange("p t a d -> p (t a d)")[:, 0:INNER]
        kcn = vt[:, 1].rearrange("p t a d -> p (t a d)")[:, INNER:2 * INNER]
        vctx = vt[:, 1].rearrange("p t a d -> p (t a d)")[:, 2 * INNER:3 * INNER]

        PS = stack.enter_context(nc.psum_tensor("PS", [P, 8, 512], F32))
        TR, MM, SA, SB_ = 0, 1, 2, 3

        def bank(c, which):
            return PS[:, 4 * c + which, :]

        wa_in, wb_in, wc_in, wd_in, ctx_loaded, small_in = (sem(n) for n in (
            "wa_in", "wb_in", "wc_in", "wd_in", "ctx_loaded", "small_in"))
        x_loaded = sem2("x_loaded")
        stored = sem2("stored")
        y_ready = sem2("y_ready")
        su_pe, su_act, su_dve, su_pool = (sem(n) for n in ("su_pe", "su_act", "su_dve", "su_pool"))
        dve_step = sem("dve_step")
        pool_step = sem("pool_step")
        staged = sem2("staged")
        stats_ready = sem2("stats_ready")
        rstd_ready = sem2("rstd_ready")
        nrm_ready = sem2("nrm_ready")
        nrmT_psum = sem2("nrmT_psum")
        feat_ready = sem2("feat_ready")
        prod_psum = sem2("prod_psum")
        res_ready = sem2("res_ready")
        blk_ready = sem2("blk_ready")
        resT_psum = sem2("resT_psum")
        q0_psum, q0_ready = sem2("q0_psum"), sem2("q0_ready")
        score_psum, centred, exped, probs_ready, rec_ready = (sem2(n) for n in (
            "score_psum", "centred", "exped", "probs_ready", "rec_ready"))
        probT_psum, pT0_ready, pT1_ready = sem2("probT_psum"), sem2("pT0_ready"), sem2("pT1_ready")
        lin1_psum, hid_ready = sem2("lin1_psum"), sem2("hid_ready")
        gate_psum, comb_ready, combT_psum, combT_ready = (sem2(n) for n in (
            "gate_psum", "comb_ready", "combT_psum", "combT_ready"))
        h_psum, c_psum, relu_ready, gated, down_done = (sem2(n) for n in (
            "h_psum", "c_psum", "relu_ready", "gated", "down_done"))
        qkv_psum, sq_ready, ssq_ready, rn_ready, qkn_ready = (sem2(n) for n in (
            "qkv_psum", "sq_ready", "ssq_ready", "rn_ready", "qkn_ready"))
        v_ready, qT_psum, kT_psum, qT_ready, kT_ready = (sem2(n) for n in (
            "v_ready", "qT_psum", "kT_psum", "qT_ready", "kT_ready"))
        sim_psum, exp_done, pv_done, head_psum, head_ready = (sem2(n) for n in (
            "sim_psum", "exp_done", "pv_done", "head_psum", "head_ready"))
        sig_ready = sem2("sig_ready")
        g_psum, u_psum, silu_ready, u_gated, act_ready, ffn_down = (sem2(n) for n in (
            "g_psum", "u_psum", "silu_ready", "u_gated", "act_ready", "ffn_down"))

        STEPS = []
        for g in range(H1 // HG):
            STEPS.append(("ctx", g, 0))
            STEPS += [("own", h, kt) for h in range(g * HG, (g + 1) * HG) for kt in range(NT)]
        NS, NPV = len(STEPS), H1 * NT
        PLANES = EP + 1

        block = stack.enter_context(nc.Block())

        @block.sync
        def _(sp):
            sp.dma_start(ctx_tok, ctx_in.rearrange("b m f -> (b m) f")).then_inc(ctx_loaded, 16)
            sp.dma_start(WA[:, :], slab_a).then_inc(wa_in, 16)
            sp.dma_start(RW[:, :], rows[0, :].partition_broadcast(P)).then_inc(small_in, 16)
            sp.dma_start(maskb[:, :], mask).then_inc(small_in, 16)
            sp.dma_start(b2[:, :], b2_in).then_inc(small_in, 16)
            sp.dma_start(sel0[:, :], sel0_in).then_inc(small_in, 16)
            sp.dma_start(sel1[:, :], sel1_in).then_inc(small_in, 16)
            def batch(dram, b):
                return dram[bass.ds(b, 1)].rearrange("o (p t) f -> p (o t f)", p=P)

            for c in range(2):
                sp.dma_start(X[:, c, :], batch(x, c)).then_inc(x_loaded[c], 16)
            with sp.Fori(0, ITERS - 1) as i:
                for c in range(2):
                    sp.wait_ge(y_ready[c], i + 1)
                    sp.dma_start(batch(out, 2 * i + c), Y[c]).then_inc(stored[c], 16)
                for c in range(2):
                    sp.wait_ge(stored[c], 16 * (i + 1))
                    sp.dma_start(X[:, c, :], batch(x, 2 * i + 2 + c)).then_inc(x_loaded[c], 16)
            for c in range(2):
                sp.wait_ge(y_ready[c], ITERS)
                sp.dma_start(batch(out, B - 2 + c), Y[c]).then_inc(stored[c], 16)
            for c in range(2):
                sp.wait_ge(stored[c], 16 * ITERS)

        @block.tensor
        def _(pe):
            mm = nc.tensor.matmul

            def transpose_tiles(dst, src, n=NT):
                for t in range(n):
                    last = nc.tensor.transpose(dst[:, t * P:(t + 1) * P], src[:, t * P:(t + 1) * P], ident)
                return last

            pe.wait_ge(ctx_loaded, 16)
            pe.wait_ge(wa_in, 16)
            nc.tensor.transpose(PS[:, 0, 0:P], ctx_tok, ident).then_inc(su_pe, 1)
            mm(PS[:, 1, 0:P], W("sa_wv"), W("sa_oT"), start=True, stop=True).then_inc(su_pe, 1)
            mm(PS[:, 2, 0:1], W("sa_oT"), W("sa_bv"), start=True, stop=True).then_inc(su_pe, 1)
            pe.wait_ge(su_act, 1)
            mm(PS[:, 3, 0:P], W("wkT"), memT, start=True, stop=True)
            mm(PS[:, 4, 0:P], W("wvT"), memT, start=True, stop=True).then_inc(su_pe, 1)
            pe.wait_ge(su_dve, 2)
            nc.tensor.transpose(PS[:, 0, 0:P], ctx_nrm, ident).then_inc(su_pe, 1)
            pe.wait_ge(su_dve, 3)
            for b in range(B):
                for hf in range(2):
                    at = (b * 2 + hf) * P
                    last = mm(PS[:, 5 + at // 512, at % 512:at % 512 + P],
                              Vb_all[:, at:at + P], W("mha_oT"), start=True, stop=True)
            last.then_inc(su_pe, 1)
            pe.wait_ge(su_act, 3)
            mm(PS[:, 3, :], ctx_nT, W("Wk"), start=True, stop=True).then_inc(su_pe, 1)
            mm(PS[:, 4, :], ctx_nT, W("Wv"), start=True, stop=True).then_inc(su_pe, 1)
            pe.wait_ge(su_dve, 5)
            transpose_tiles(PS[:, 7, :], kcn).then_inc(su_pe, 1)
            pe.wait_ge(su_dve, 6)
            pe.wait_ge(small_in, 80)

            with pe.Fori(0, ITERS) as i:
                def tokens_to_features(c, k, dst):
                    pe.wait_ge(nrm_ready[c], i * LNS + k)
                    transpose_tiles(bank(c, dst), nrm[:, c, :]).then_inc(nrmT_psum[c], 1)

                def features_to_tokens(c, ready, k):
                    pe.wait_ge(ready, i * 3 + k)
                    transpose_tiles(bank(c, TR), res[:, c, :]).then_inc(resT_psum[c], 1)

                for c in range(2):
                    tokens_to_features(c, 1, TR)
                for c in range(2):
                    pe.wait_ge(feat_ready[c], i * 6 + 1)
                    mm(bank(c, MM), foldT[:, :], feat[:, c, :], start=True, stop=True).then_inc(prod_psum[c], 1)
                for c in range(2):
                    features_to_tokens(c, res_ready[c], 1)
                for c in range(2):
                    tokens_to_features(c, 2, MM)
                for c in range(2):
                    pe.wait_ge(feat_ready[c], i * 6 + 2)
                    mm(bank(c, SA), W("wqT"), feat[:, c, :], start=True, stop=True).then_inc(q0_psum[c], 1)
                for c in range(2):
                    pe.wait_ge(q0_ready[c], i + 1)
                    for t in range(NT):
                        at = 4 * c + SA + t // 2
                        last = mm(PS[:, at, (t % 2) * 256:(t % 2) * 256 + 256],
                                  q0T[c][:, t * P:(t + 1) * P],
                                  Kb_all[:, bass.ds(2 * i + c, 1), :].rearrange("p o n -> p (o n)"), start=True, stop=True)
                    last.then_inc(score_psum[c], 1)
                for c in range(2):
                    pe.wait_ge(probs_ready[c], i + 1)
                    for hf in range(2):
                        for t in range(NT):
                            at = t * H0 * M + hf * P
                            last = nc.tensor.transpose(bank(c, SA + hf)[:, t * P:(t + 1) * P],
                                                       sc[c][:, at:at + P], ident)
                    last.then_inc(probT_psum[c], 1)
                for c in range(2):
                    pe.wait_ge(pT0_ready[c], i + 1)
                    pe.wait_ge(staged[c], i + 1)
                    mm(bank(c, MM), Vp[:, c, 0, :], pT[c][:, 0, :], start=True, stop=False)
                    pe.wait_ge(pT1_ready[c], i + 1)
                    mm(bank(c, MM), Vp[:, c, 1, :], pT[c][:, 1, :], start=False, stop=True).then_inc(prod_psum[c], 1)
                for c in range(2):
                    features_to_tokens(c, res_ready[c], 2)
                for c in range(2):
                    tokens_to_features(c, 3, MM)
                order = (SA, SB_, TR, MM)
                for c in range(2):
                    pe.wait_ge(feat_ready[c], i * 6 + 3)
                    for k in range(FC):
                        mm(bank(c, order[k]), W("lin1T", k), feat[:, c, :], start=True, stop=True)\
                            .then_inc(lin1_psum[c], 1)
                for c in range(2):
                    for k in range(FC):
                        pe.wait_ge(hid_ready[c], i * FC + k + 1)
                        last = mm(bank(c, SA), W("lin2T", k), hT[c][:, k, :], start=(k == 0), stop=(k == FC - 1))
                    last.then_inc(prod_psum[c], 1)
                for c in range(2):
                    features_to_tokens(c, res_ready[c], 3)
                for c in range(2):
                    tokens_to_features(c, 5, MM)
                pe.wait_ge(wb_in, 16)
                for c in range(2):
                    pe.wait_ge(feat_ready[c], i * 6 + 4)
                    for t in range(NT):
                        last = mm(bank(c, SA)[:, t * E0:(t + 1) * E0], feat[:, c, t * P:(t + 1) * P], W("gate_w"),
                                  start=True, stop=True)
                    last.then_inc(gate_psum[c], 1)
                for c in range(2):
                    pe.wait_ge(comb_ready[c], i * 2 + 1)
                    for t in range(NT):
                        last = mm(bank(c, SB_)[0:E0, t * P:(t + 1) * P], comb0[:, c, t, :], ident,
                                  start=True, stop=True)
                    last.then_inc(combT_psum[c], 1)
                for c in range(2):
                    def down0(e):
                        pe.wait_ge(gated[c], i * E0 + e + 1)
                        mm(bank(c, SB_), W("w2", e), pr[:, c, 2 + e % 2, :], start=False, stop=(e == E0 - 1))\
                            .then_inc(down_done[c], 1)

                    for e in range(E0):
                        if e >= 2:
                            pe.wait_ge(relu_ready[c], i * E0 + e - 1)
                        mm(bank(c, (TR, MM)[e % 2]), W("w1", e), feat[:, c, :], start=True, stop=True)\
                            .then_inc(h_psum[c], 1)
                        if e == 0:
                            pe.wait_ge(combT_ready[c], i * 2 + 1)
                            mm(bank(c, SB_), b2[:, :], combT[c][0:E0, :], start=True, stop=False)
                        else:
                            down0(e - 1)
                        mm(bank(c, SA), sel0[:, e * P:(e + 1) * P], combT[c][0:E0, :], start=True, stop=True)\
                            .then_inc(c_psum[c], 1)
                    down0(E0 - 1)
                for c in range(2):
                    features_to_tokens(c, blk_ready[c], 1)
                for c in range(2):
                    tokens_to_features(c, 6, MM)
                pe.wait_ge(wc_in, 16)
                for t in range(NT):
                    for c in range(2):
                        lat = feat[:, c, t * P:(t + 1) * P]
                        if t == 0:
                            pe.wait_ge(feat_ready[c], i * 6 + 5)
                        else:
                            pe.wait_ge(kT_ready[c], i * NT + t)
                        mm(bank(c, MM), lat, W("Wq"), start=True, stop=True)
                        mm(bank(c, SA), lat, W("Wk"), start=True, stop=True)
                        mm(bank(c, SB_), lat, W("Wv"), start=True, stop=True).then_inc(qkv_psum[c], 1)
                    for c in range(2):
                        pe.wait_ge(qkn_ready[c], i * NT + t + 1)
                        if t > 0:
                            pe.wait_ge(qT_ready[c], i * NT + t)
                        transpose_tiles(bank(c, TR), qkn[c][:, 0, :]).then_inc(qT_psum[c], 1)
                        pe.wait_ge(v_ready[c], i * NT + t + 1)
                        transpose_tiles(bank(c, SB_), qkn[c][:, 1, :]).then_inc(kT_psum[c], 1)
                for c in range(2):
                    pe.wait_ge(qT_ready[c], (i + 1) * NT)
                    pe.wait_ge(kT_ready[c], (i + 1) * NT)

                    def values(n):
                        kind, h, kt = STEPS[n]
                        pe.wait_ge(exp_done[c], i * NS + n + 1)
                        if kind == "ctx":
                            return
                        ones_at = D1 * (h % 2)
                        if kt == 0 and h >= 2:
                            pe.wait_ge(head_ready[c], i * H1 + h - 1)
                        mm(bank(c, SA + h % 2), vt[:, c, kt, h // 2, ones_at:ones_at + P],
                           pr[:, c, (h * NT + kt) % 4, :], start=(kt == 0), stop=False).then_inc(pv_done[c], 1)
                        if kt == NT - 1:
                            mm(bank(c, SA + h % 2), vc[:, c, h, :], pc[c][h // HG],
                               start=False, stop=True).then_inc(head_psum[c], 1)

                    for n, (kind, h, kt) in enumerate(STEPS):
                        dst = bank(c, (TR, MM)[n % 2])
                        if n >= 2:
                            values(n - 2)
                        if kind == "ctx":
                            for q in range(2):
                                last = mm(dst, kc[:, c, 2 * h + q, :], qT[:, c, 2 * h + q, :],
                                          start=(q == 0), stop=(q == 1))
                        else:
                            r = D1 * (h % 2)
                            last = mm(dst, kT[r:r + D1, c, h // 2, kt * P:(kt + 1) * P], qT[r:r + D1, c, h // 2, :],
                                      start=True, stop=True)
                        last.then_inc(sim_psum[c], 1)
                    values(NS - 2)
                    values(NS - 1)
                for c in range(2):
                    pe.wait_ge(head_ready[c], (i + 1) * H1)
                    for q in range(PAIRS):
                        last = mm(bank(c, MM), W("Wo", q), aT[:, c, q, :], start=(q == 0), stop=(q == PAIRS - 1))
                    last.then_inc(prod_psum[c], 1)
                for c in range(2):
                    features_to_tokens(c, blk_ready[c], 2)
                for c in range(2):
                    tokens_to_features(c, 8, MM)
                pe.wait_ge(wd_in, 16)
                for c in range(2):
                    pe.wait_ge(feat_ready[c], i * 6 + 6)
                    for t in range(NT):
                        last = mm(bank(c, SA)[:, t * E1:(t + 1) * E1], feat[:, c, t * P:(t + 1) * P],
                                  W("route_wT"), start=True, stop=True)
                    last.then_inc(gate_psum[c], 1)
                for c in range(2):
                    pe.wait_ge(comb_ready[c], i * 2 + 2)
                    for t in range(NT):
                        last = mm(bank(c, SB_)[0:E1, t * P:(t + 1) * P], comb1[:, c, t, :], ident,
                                  start=True, stop=True)
                    last.then_inc(combT_psum[c], 1)
                for c in range(2):
                    def down1(p):
                        pe.wait_ge(act_ready[c], i * PLANES + p + 1)
                        mm(bank(c, SB_), W("downT", p) if p < EP else W("sh_downT"), pr[:, c, 2 + p % 2, :],
                           start=(p == 0), stop=(p == EP)).then_inc(ffn_down[c], 1)

                    for p in range(PLANES):
                        if p >= 1:
                            pe.wait_ge(silu_ready[c], i * PLANES + p)
                        mm(bank(c, TR), W("gateT", p) if p < EP else W("sh_gateT"), feat[:, c, :],
                           start=True, stop=True).then_inc(g_psum[c], 1)
                        if p >= 1:
                            pe.wait_ge(u_gated[c], i * EP + p)
                        mm(bank(c, MM), W("upT", p) if p < EP else W("sh_upT"), feat[:, c, :],
                           start=True, stop=True).then_inc(u_psum[c], 1)
                        if p == 0:
                            pe.wait_ge(combT_ready[c], i * 2 + 2)
                        else:
                            down1(p - 1)
                        if p < EP:
                            mm(bank(c, SA), sel1[:, p * P:(p + 1) * P], combT[c], start=True, stop=True)\
                                .then_inc(c_psum[c], 1)
                    down1(EP)
                for c in range(2):
                    features_to_tokens(c, blk_ready[c], 3)

        @block.scalar
        def _(act):
            for tile_, slab, landed in ((WB, slab_b, wb_in), (WC, slab_c, wc_in), (WD, slab_d, wd_in)):
                act.dma_start(tile_[:, :], slab).then_inc(landed, 16)

            def copy(dst, src):
                return nc.scalar.activation(dst, src, ACT.Copy)

            def affine(dst, src, scale, bias):
                return nc.scalar.activation(dst, src, ACT.Identity, bias=bias, scale=scale)

            act.wait_ge(su_pe, 1)
            copy(memT, PS[:, 0, 0:P]).then_inc(su_act, 1)
            act.wait_ge(su_pe, 2)
            copy(foldT[:, :], PS[:, 1, 0:P]).then_inc(su_act, 1)
            act.wait_ge(su_pe, 5)
            affine(ctx_nT, PS[:, 0, 0:P], W("lnx_w"), W("lnx_b")).then_inc(su_act, 1)
            act.wait_ge(su_pe, 6)
            copy(Vp_all[:, :, :, :].rearrange("p b h c -> p (b h) c"),
                 PS[:, 5:7, :].rearrange("p a (h c) -> p (a h) c", c=P)).then_inc(su_act, 1)
            act.wait_ge(su_pe, 7)
            nc.scalar.activation(sqc, PS[:, 3, :], ACT.Square).then_inc(su_act, 1)
            act.wait_ge(su_pe, 8)
            copy(vctx, PS[:, 4, :]).then_inc(su_act, 1)

            with act.Fori(0, ITERS) as i:
                def features_out(c, k, scale=None, bias=None):
                    act.wait_ge(nrmT_psum[c], i * 6 + k)
                    src = bank(c, TR if k == 1 else MM)
                    (copy(feat[:, c, :], src) if scale is None else
                     affine(feat[:, c, :], src, scale, bias)).then_inc(feat_ready[c], 1)

                def block_out(c, ready, k, which):
                    act.wait_ge(ready[c], k)
                    copy(res[:, c, :], bank(c, which)).then_inc(blk_ready[c], 1)

                for c in range(2):
                    features_out(c, 1)
                for c in range(2):
                    features_out(c, 2, W("ln1_g"), W("ln1_b"))
                for c in range(2):
                    act.wait_ge(q0_psum[c], i + 1)
                    affine(q0T[c], bank(c, SA), 1.0, W("bq")).then_inc(q0_ready[c], 1)
                for c in range(2):
                    act.wait_ge(centred[c], i + 1)
                    nc.scalar.activation(sc[c], sc[c], ACT.Exp, scale=float(D0) ** -0.5).then_inc(exped[c], 1)
                for c in range(2):
                    act.wait_ge(probT_psum[c], i + 1)
                    copy(pT[c][:, 0, :], bank(c, SA)).then_inc(pT0_ready[c], 1)
                for c in range(2):
                    features_out(c, 3, W("ln2_g"), W("ln2_b"))
                order = (SA, SB_, TR, MM)
                for c in range(2):
                    for k in range(FC):
                        act.wait_ge(lin1_psum[c], i * FC + k + 1)
                        nc.scalar.activation(hT[c][:, k, :], bank(c, order[k]), ACT.Relu,
                                             bias=W("lin1_b")[:, k:k + 1]).then_inc(hid_ready[c], 1)
                for c in range(2):
                    features_out(c, 4)
                for c in range(2):
                    act.wait_ge(combT_psum[c], i * 2 + 1)
                    copy(combT[c][0:E0, :], bank(c, SB_)[0:E0, :]).then_inc(combT_ready[c], 1)
                for c in range(2):
                    for e in range(E0):
                        act.wait_ge(h_psum[c], i * E0 + e + 1)
                        if e >= 2:
                            act.wait_ge(gated[c], i * E0 + e - 1)
                        nc.scalar.activation(pr[:, c, e % 2, :], bank(c, (TR, MM)[e % 2]), ACT.Relu,
                                             bias=W("b1")[:, e:e + 1]).then_inc(relu_ready[c], 1)
                for c in range(2):
                    block_out(c, down_done, (i + 1) * E0, SB_)
                for c in range(2):
                    features_out(c, 5, W("lnl_w"), W("lnl_b"))
                for t in range(NT):
                    for c in range(2):
                        act.wait_ge(qkv_psum[c], i * NT + t + 1)
                        if t > 0:
                            act.wait_ge(ssq_ready[c], i * NT + t)
                        nc.scalar.activation(sq[c], PS[:, 4 * c + MM:4 * c + SB_, :], ACT.Square)\
                            .then_inc(sq_ready[c], 1)
                        v4 = bank(c, SB_).rearrange("p (a h d) -> p a h d", h=2, d=D1)
                        for hh in range(2):
                            last = copy(vt[:, c, t, :, 2 * hh * D1:(2 * hh + 1) * D1], v4[:, :, hh, :])
                        last.then_inc(v_ready[c], 1)
                    for c in range(2):
                        act.wait_ge(qT_psum[c], i * NT + t + 1)
                        nc.scalar.activation(qT[:, c, :, t * P:(t + 1) * P],
                                             bank(c, TR).rearrange("p (a s) -> p a s", s=P), ACT.Copy,
                                             scale=W("qs")).then_inc(qT_ready[c], 1)
                for c in range(2):
                    for n, (kind, h, kt) in enumerate(STEPS):
                        act.wait_ge(sim_psum[c], i * NS + n + 1)
                        src = bank(c, (TR, MM)[n % 2])
                        if kind == "ctx":
                            nc.scalar.activation(pc[c][h], src, ACT.Exp, bias=mb[:, c, :],
                                                 scale=SIM_SCALE).then_inc(exp_done[c], 1)
                        else:
                            m = h * NT + kt
                            if m >= 4:
                                act.wait_ge(pv_done[c], i * NPV + m - 3)
                            nc.scalar.activation(pr[:, c, m % 4, :], src, ACT.Exp, bias=shift[:, :],
                                                 scale=SIM_SCALE).then_inc(exp_done[c], 1)
                for c in range(2):
                    block_out(c, prod_psum, (i + 1) * 4, MM)
                for c in range(2):
                    features_out(c, 6)
                for c in range(2):
                    act.wait_ge(gate_psum[c], i * 2 + 2)
                    nc.scalar.activation(scor[:, c, :, :], bank(c, SA)[:, 0:NT * E1].rearrange(
                        "p (t e) -> p t e", e=E1), ACT.Sigmoid).then_inc(sig_ready[c], 1)
                for c in range(2):
                    act.wait_ge(combT_psum[c], i * 2 + 2)
                    copy(combT[c], bank(c, SB_)[0:E1, :]).then_inc(combT_ready[c], 1)
                for c in range(2):
                    for p in range(PLANES):
                        act.wait_ge(g_psum[c], i * PLANES + p + 1)
                        if p >= 2:
                            act.wait_ge(act_ready[c], i * PLANES + p - 1)
                        nc.scalar.activation(pr[:, c, p % 2, :], bank(c, TR), ACT.Silu)\
                            .then_inc(silu_ready[c], 1)
                for c in range(2):
                    block_out(c, ffn_down, (i + 1) * PLANES, SB_)

        @block.gpsimd
        def _(pool):
            g = nc.gpsimd
            steps = [0]

            def step(ins):
                steps[0] += 1
                ins.then_inc(pool_step, 1)
                return steps[0]

            g.memset(mhalf[:, :], -0.5)
            g.memset(eps_row[:, :], EPS)
            for tile_ in (rt0, top0, grp, topg, cand, top1):
                g.memset(tile_[:, :, :, :], SENT)
            g.memset(kc[:, :, :, :], 0.0)
            k = step(g.memset(vc[:, :, :, :], 0.0))
            pool.wait_ge(pool_step, k)
            for j in range(HG):
                even = 1 - j % 2
                for c in range(2):
                    k = step(g.memset(vc[j * M:(j + 1) * M, c, j:H1:HG, even * D1:(even + 1) * D1], 1.0))
                    pool.wait_ge(pool_step, k)
            pool.wait_ge(su_dve, 1)
            k = step(g.tensor_scalar(ve[:, 0, 0:1], mv[:, 0, 0, 1:2], EPS, None, ALU.add))
            pool.wait_ge(pool_step, k)
            g.tensor_tensor(rstd[:, 0, 0:1], ve[:, 0, 0:1], mhalf[:, 0:1], ALU.pow).then_inc(su_pool, 1)
            pool.wait_ge(su_dve, 4)
            k = step(g.tensor_tensor(ssc[:, 0, 0:H1], ssq[:, 0, 0:H1], mhalf[:, 0:H1], ALU.pow))
            pool.wait_ge(pool_step, k)
            g.tensor_scalar(rn[:, 0, 0:H1], ssc[:, 0, 0:H1], 1.0 / L2_EPS, None, ALU.min).then_inc(su_pool, 1)
            pool.wait_ge(su_dve, 6)
            k = step(g.memset(vt[:, :, :, :, D1:2 * D1].rearrange("p c t a d -> p (c t a) d"), 1.0))
            pool.wait_ge(pool_step, k)
            pool.sem_clear(pool_step)
            steps[0] = 0

            with pool.Fori(0, ITERS) as i:
                def after(k):
                    pool.wait_ge(pool_step, k)

                def rsqrt_var(c, n, twice=False):
                    pool.wait_ge(stats_ready[c], i * LNS + n)
                    var = mv[:, c, :, 1]
                    after(step(g.tensor_tensor(ve[:, c, :], var, eps_row[:, 0:NT], ALU.add)))
                    ins = g.tensor_tensor(rstd[:, c, :], ve[:, c, :], mhalf[:, 0:NT], ALU.pow)
                    if twice:
                        after(step(ins))
                        after(step(g.tensor_tensor(tmp4[:, c, :], rstd[:, c, :], rstd[:, c, :], ALU.mult)))
                        after(step(g.tensor_tensor(tmp4[:, c, :], tmp4[:, c, :], var, ALU.mult)))
                        after(step(g.tensor_scalar(tmp4[:, c, :], tmp4[:, c, :], EPS, None, ALU.add)))
                        after(step(g.tensor_tensor(ve[:, c, :], tmp4[:, c, :], mhalf[:, 0:NT], ALU.pow)))
                        ins = g.tensor_tensor(rstd[:, c, :], rstd[:, c, :], ve[:, c, :], ALU.mult)
                    ins.then_inc(rstd_ready[c], 1)

                for c in range(2):
                    b = 2 * i + c
                    after(step(g.tensor_copy(Vp[:, c:c + 1, :, :].rearrange("p o h f -> p o (h f)"),
                                             Vp_all[:, bass.ds(b, 1), :, :].rearrange("p o h f -> p o (h f)"))))
                    for j in range(HG):
                        r = D1 * (j % 2)
                        after(step(g.tensor_copy(kc[r:r + D1, c, j // 2:PAIRS:2, j * M:(j + 1) * M].unsqueeze(2),
                                                 kcT_all[r:r + D1, j // 2:PAIRS:2, bass.ds(b, 1), :])))
                        after(step(g.tensor_copy(vc[j * M:(j + 1) * M, c, j:H1:HG, r:r + D1].unsqueeze(1),
                                                 vc_all[j * M:(j + 1) * M, bass.ds(b, 1), :, :])))
                    g.tensor_copy(mb[:, c, :], mbias[:, bass.ds(b, 1)]).then_inc(staged[c], 1)
                for n in (1, 2):
                    for c in range(2):
                        rsqrt_var(c, n)
                for c in range(2):
                    pool.wait_ge(rec_ready[c], i + 1)
                    p3 = sc[c].rearrange("p (g m) -> p g m", m=M)
                    g.tensor_tensor(p3, p3, hrec[:, c, :].unsqueeze(2).broadcast_to([P, NT * H0, M]), ALU.mult)\
                        .then_inc(probs_ready[c], 1)
                for n in (3, 4, 5, 6):
                    for c in range(2):
                        rsqrt_var(c, n, twice=(n == 6))
                for t in range(NT):
                    for c in range(2):
                        pool.wait_ge(ssq_ready[c], i * NT + t + 1)
                        after(step(g.tensor_tensor(ssc[:, c, :], ssq[:, c, :], mhalf[:, :], ALU.pow)))
                        g.tensor_scalar(rn[:, c, :], ssc[:, c, :], 1.0 / L2_EPS, None, ALU.min)\
                            .then_inc(rn_ready[c], 1)
                for n in (7, 8):
                    for c in range(2):
                        rsqrt_var(c, n)
                pool.wait_ge(pool_step, steps[0])
                pool.sem_clear(pool_step)

        @block.vector
        def _(dve):
            v = nc.vector
            steps = [0]

            def step(ins):
                steps[0] += 1
                ins.then_inc(dve_step, 1)
                return steps[0]

            dve.wait_ge(ctx_loaded, 16)
            k = step(v.bn_stats(stat[:, 0, 0, :], ctx_tok))
            dve.wait_ge(dve_step, k)
            v.bn_aggr(mv[:, 0, 0, :], stat[:, 0, 0, :]).then_inc(su_dve, 1)
            dve.wait_ge(su_dve, 1)
            dve.wait_ge(su_pool, 1)
            v.tensor_scalar(ctx_nrm, ctx_tok, mv[:, 0, 0, 0:1], rstd[:, 0, 0:1],
                            ALU.subtract, ALU.mult).then_inc(su_dve, 1)
            dve.wait_ge(wa_in, 16)
            dve.wait_ge(su_pe, 4)
            v.tensor_scalar(kT0, PS[:, 3, 0:P], W("bk"), None, ALU.add)
            v.tensor_scalar(vT0, PS[:, 4, 0:P], W("bv"), None, ALU.add)
            k = step(v.tensor_scalar(fold_b[:, :], PS[:, 2, 0:1], W("sa_b"), None, ALU.add))
            dve.wait_ge(dve_step, k)
            heads = W("head_of_row").unsqueeze(1).unsqueeze(3).broadcast_to([P, B, H0, M])
            for src, dst in ((kT0, Kb_all[:, :, :].rearrange("p b (h m) -> p b h m", m=M)),
                             (vT0, Vb_all.rearrange("p (b h m) -> p b h m", b=B, m=M))):
                last = v.tensor_tensor(dst, src.rearrange("p (b m) -> p b m", m=M).unsqueeze(2).broadcast_to(
                    [P, B, H0, M]), heads, ALU.mult)
            last.then_inc(su_dve, 1)
            dve.wait_ge(small_in, 80)
            k = step(v.tensor_tensor(prod[:, :], W("qs_row"), W("ks_row"), ALU.mult))
            dve.wait_ge(dve_step, k)
            k = step(v.tensor_reduce(shift[:, :], prod[:, :], AX.X, ALU.max, apply_absolute_value=True))
            dve.wait_ge(dve_step, k)
            k = step(v.tensor_scalar(shift[:, :], shift[:, :], SIM_SCALE, -EXP_ROOM, ALU.mult, ALU.add))
            dve.wait_ge(dve_step, k)
            k = step(v.tensor_scalar(shift[:, :], shift[:, :], 0.0, -1.0, ALU.max, ALU.mult))
            k2 = step(v.tensor_scalar(mbias[:, :], maskb[:, :], 1.0, MASKED, ALU.subtract, ALU.mult))
            dve.wait_ge(dve_step, k2)
            k = step(v.tensor_scalar(mbias[:, :], mbias[:, :], shift[:, :], None, ALU.add))
            dve.wait_ge(dve_step, k)
            dve.wait_ge(su_act, 5)
            v.tensor_reduce(ssq[:, 0, 0:H1], sqc.rearrange("p (h d) -> p h d", d=D1), AX.X, ALU.add)\
                .then_inc(su_dve, 1)
            dve.wait_ge(su_pool, 2)
            v.tensor_tensor(kcn.rearrange("p (h d) -> p h d", d=D1), PS[:, 3, :].rearrange(
                "p (h d) -> p h d", d=D1), rn[:, 0, 0:H1].unsqueeze(2).broadcast_to([P, H1, D1]), ALU.mult)\
                .then_inc(su_dve, 1)
            dve.wait_ge(su_act, 6)
            vh = vctx.rearrange("p (h d) -> p h d", d=D1)
            for b in range(B):
                for j in range(HG):
                    v.tensor_copy(vc_all[j * M:(j + 1) * M, b, :, :], vh[b * M:(b + 1) * M, j:H1:HG, :])
            dve.wait_ge(su_pe, 9)
            v.tensor_scalar(kcT_all[:, :, :, :].rearrange("p a b m -> p (a b m)"), PS[:, 7, :], W("ks"), None,
                            ALU.mult).then_inc(su_dve, 1)
            dve.wait_ge(su_dve, 6)
            dve.wait_ge(dve_step, steps[0])
            dve.sem_clear(dve_step)
            steps[0] = 0

            with dve.Fori(0, ITERS) as i:
                def after(k):
                    dve.wait_ge(dve_step, k)

                def tile_of(c, src, t):
                    return src[:, c, t * P:(t + 1) * P] if src is X else bank(c, TR)[:, t * P:(t + 1) * P]

                def layer_norm(n, src, wait, token_affine=None):
                    marks = []
                    for c in range(2):
                        wait(c)
                        for t in range(NT):
                            last = v.bn_stats(stat[:, c, t, :], tile_of(c, src, t))
                        marks.append(step(last))
                    for c in range(2):
                        after(marks[c])
                        for t in range(NT):
                            last = v.bn_aggr(mv[:, c, t, :], stat[:, c, t, :])
                        last.then_inc(stats_ready[c], 1)
                    for c in range(2):
                        dve.wait_ge(stats_ready[c], i * LNS + n)
                        dve.wait_ge(rstd_ready[c], i * LNS + n)
                        for t in range(NT):
                            last = v.tensor_scalar(nrm[:, c, t * P:(t + 1) * P], tile_of(c, src, t),
                                                   mv[:, c, t, 0:1], rstd[:, c, t:t + 1], ALU.subtract, ALU.mult)
                        last.then_inc(nrm_ready[c], 1)
                    if token_affine:
                        gain, bias = token_affine
                        r3 = [nrm[:, c, :].rearrange("p (t f) -> p t f", f=P) for c in range(2)]
                        row = [W(nm).unsqueeze(1).broadcast_to([P, NT, P]) for nm in (gain, bias)]
                        marks = []
                        for c in range(2):
                            dve.wait_ge(nrm_ready[c], i * LNS + n)
                            marks.append(step(v.tensor_tensor(r3[c], r3[c], row[0], ALU.mult)))
                        for c in range(2):
                            after(marks[c])
                            marks[c] = step(v.tensor_tensor(r3[c], r3[c], row[1], ALU.add))
                        for c in range(2):
                            after(marks[c])
                            marks[c] = step(v.tensor_tensor(X[:, c, :], X[:, c, :], nrm[:, c, :], ALU.add))
                        for c in range(2):
                            after(marks[c])

                def returned(k):
                    return lambda c: dve.wait_ge(resT_psum[c], i * 6 + k)

                def add_residual(c, k, which, bias):
                    dve.wait_ge(prod_psum[c], i * 4 + k)
                    v.scalar_tensor_tensor(res[:, c, :], bank(c, which), bias, feat[:, c, :], ALU.add, ALU.add)\
                        .then_inc(res_ready[c], 1)

                def add_block(k):
                    marks = []
                    for c in range(2):
                        dve.wait_ge(resT_psum[c], i * 6 + k)
                        marks.append(step(v.tensor_tensor(X[:, c, :], bank(c, TR), X[:, c, :], ALU.add)))
                    for c in range(2):
                        after(marks[c])

                def pick(k, values, n, top):
                    hit = hit0 if values is rt0 else hitg if values is grp else hit1
                    marks = []
                    for c in range(2):
                        for t in range(NT):
                            last = v.max(mx[:, c, t, :], values[:, c, t, 0:n])
                        marks.append(step(last))
                    for c in range(2):
                        after(marks[c])
                        marks[c] = step(v.tensor_copy(top[:, c, :, 0:k], mx[:, c, :, 0:k]))
                    for c in range(2):
                        after(marks[c])
                        for t in range(NT):
                            last = v.match_replace(hit[:, c, t, 0:n + 8 - k], top[:, c, t, :],
                                                   values[:, c, t, 0:n + 8 - k], PICK)
                        marks[c] = step(last)
                    return marks

                layer_norm(1, X, lambda c: dve.wait_ge(x_loaded[c], 16 * (i + 1)))
                for c in range(2):
                    add_residual(c, 1, MM, fold_b[:, :])
                layer_norm(2, PS, returned(1))
                for c in range(2):
                    dve.wait_ge(score_psum[c], i + 1)
                    s3 = PS[:, 4 * c + SA:4 * c + SA + 2, :].rearrange("p a (g m) -> p (a g) m", m=M)
                    k = step(v.tensor_reduce(hmax[:, c, :], s3, AX.X, ALU.max))
                    after(k)
                    v.tensor_tensor(sc[c].rearrange("p (g m) -> p g m", m=M), s3,
                                    hmax[:, c, :].unsqueeze(2).broadcast_to([P, NT * H0, M]), ALU.subtract)\
                        .then_inc(centred[c], 1)
                for c in range(2):
                    dve.wait_ge(exped[c], i + 1)
                    k = step(v.tensor_reduce(hsum[:, c, :], sc[c].rearrange("p (g m) -> p g m", m=M), AX.X, ALU.add))
                    after(k)
                    v.reciprocal(hrec[:, c, :], hsum[:, c, :]).then_inc(rec_ready[c], 1)
                for c in range(2):
                    dve.wait_ge(probT_psum[c], i + 1)
                    v.tensor_copy(pT[c][:, 1, :], bank(c, SB_)).then_inc(pT1_ready[c], 1)
                for c in range(2):
                    add_residual(c, 2, MM, W("mha_b"))
                layer_norm(3, PS, returned(2))
                for c in range(2):
                    add_residual(c, 3, SA, W("lin2_b"))
                layer_norm(4, PS, returned(3), ("ln3_g", "ln3_b"))
                layer_norm(5, X, lambda c: None)
                marks = []
                for c in range(2):
                    dve.wait_ge(gate_psum[c], i * 2 + 1)
                    marks.append(step(v.tensor_tensor(
                        rt0[:, c, :, 0:E0], bank(c, SA)[:, 0:NT * E0].rearrange("p (t e) -> p t e", e=E0),
                        W("gate_b").unsqueeze(1).broadcast_to([P, NT, E0]), ALU.add)))
                after(marks[1])
                marks = pick(K0, rt0, E0, top0)
                for c in range(2):
                    after(marks[c])
                    v.scalar_tensor_tensor(comb0[:, c, :, :], hit0[:, c, :, 0:E0], PICK, rt0[:, c, :, 0:E0],
                                           ALU.is_ge, ALU.mult).then_inc(comb_ready[c], 1)
                for c in range(2):
                    for e in range(E0):
                        dve.wait_ge(relu_ready[c], i * E0 + e + 1)
                        dve.wait_ge(c_psum[c], i * (E0 + EP) + e + 1)
                        if e >= 2:
                            dve.wait_ge(down_done[c], i * E0 + e - 1)
                        v.tensor_tensor(pr[:, c, 2 + e % 2, :], bank(c, SA), pr[:, c, e % 2, :], ALU.mult)\
                            .then_inc(gated[c], 1)
                add_block(4)
                layer_norm(6, X, lambda c: None)
                for t in range(NT):
                    for c in range(2):
                        dve.wait_ge(sq_ready[c], i * NT + t + 1)
                        v.tensor_reduce(ssq[:, c, :], sq[c].rearrange("p a (h d) -> p (a h) d", d=D1), AX.X, ALU.add)\
                            .then_inc(ssq_ready[c], 1)
                    for c in range(2):
                        dve.wait_ge(rn_ready[c], i * NT + t + 1)
                        for a in range(2):
                            last = v.tensor_tensor(
                                qkn[c][:, a, :].rearrange("p (h d) -> p h d", d=D1),
                                bank(c, (MM, SA)[a]).rearrange("p (h d) -> p h d", d=D1),
                                rn[:, c, a * H1:(a + 1) * H1].unsqueeze(2).broadcast_to([P, H1, D1]), ALU.mult)
                        last.then_inc(qkn_ready[c], 1)
                    for c in range(2):
                        dve.wait_ge(kT_psum[c], i * NT + t + 1)
                        v.tensor_scalar(kT[:, c, :, t * P:(t + 1) * P], bank(c, SB_).rearrange(
                            "p (a s) -> p a s", s=P), W("ks"), None, ALU.mult).then_inc(kT_ready[c], 1)
                for c in range(2):
                    for h in range(H1):
                        dve.wait_ge(head_psum[c], i * H1 + h + 1)
                        o = bank(c, SA + h % 2)
                        r, d = D1 * (h % 2), D1 * (1 - h % 2)
                        after(step(v.reciprocal(res[r:r + D1, c, :], o[d:d + D1, :])))
                        v.tensor_tensor(aT[r:r + D1, c, h // 2, :], o[r:r + D1, :], res[r:r + D1, c, :], ALU.mult)\
                            .then_inc(head_ready[c], 1)
                layer_norm(7, PS, returned(5), ("lno_w", "lno_b"))
                layer_norm(8, X, lambda c: None)
                marks = []
                for c in range(2):
                    dve.wait_ge(sig_ready[c], i + 1)
                    marks.append(step(v.tensor_tensor(sfc[:, c, :, :], scor[:, c, :, :],
                                                      W("route_b").unsqueeze(1).broadcast_to([P, NT, E1]), ALU.add)))
                for c in range(2):
                    after(marks[c])
                    marks[c] = step(v.tensor_reduce(grp[:, c, :, 0:NG], sfc[:, c, :, :].rearrange(
                        "p t (g s) -> p t g s", s=GS), AX.X, ALU.max))
                after(marks[1])
                marks = pick(TG, grp, NG, topg)
                for c in range(2):
                    after(marks[c])
                    marks[c] = step(v.tensor_scalar(hitg[:, c, :, 0:NG], hitg[:, c, :, 0:NG], PICK, None, ALU.is_ge))
                for c in range(2):
                    after(marks[c])
                    marks[c] = step(v.tensor_tensor(
                        cand[:, c, :, 0:E1].rearrange("p t (g s) -> p t g s", s=GS),
                        sfc[:, c, :, :].rearrange("p t (g s) -> p t g s", s=GS),
                        hitg[:, c, :, 0:NG].unsqueeze(3).broadcast_to([P, NT, NG, GS]), ALU.mult))
                after(marks[1])
                marks = pick(K1, cand, E1, top1)
                for c in range(2):
                    after(marks[c])
                    marks[c] = step(v.scalar_tensor_tensor(comb1[:, c, :, :], hit1[:, c, :, 0:E1], PICK,
                                                           scor[:, c, :, :], ALU.is_ge, ALU.mult))
                for c in range(2):
                    after(marks[c])
                    marks[c] = step(v.tensor_reduce(csum[:, c, :], comb1[:, c, :, :], AX.X, ALU.add))
                for c in range(2):
                    after(marks[c])
                    marks[c] = step(v.tensor_scalar(csum[:, c, :], csum[:, c, :], 1e-20, None, ALU.add))
                for c in range(2):
                    after(marks[c])
                    marks[c] = step(v.reciprocal(csum[:, c, :], csum[:, c, :]))
                for c in range(2):
                    after(marks[c])
                    marks[c] = step(v.tensor_scalar(csum[:, c, :], csum[:, c, :], ROUTE_SCALE, None, ALU.mult))
                for c in range(2):
                    after(marks[c])
                    v.tensor_tensor(comb1[:, c, :, :], comb1[:, c, :, :], csum[:, c, :].unsqueeze(2).broadcast_to(
                        [P, NT, E1]), ALU.mult).then_inc(comb_ready[c], 1)
                for c in range(2):
                    for p in range(PLANES):
                        dve.wait_ge(silu_ready[c], i * PLANES + p + 1)
                        dve.wait_ge(u_psum[c], i * PLANES + p + 1)
                        if p >= 2:
                            dve.wait_ge(ffn_down[c], i * PLANES + p - 1)
                        if p == EP:
                            v.tensor_tensor(pr[:, c, 2 + p % 2, :], bank(c, MM), pr[:, c, p % 2, :], ALU.mult)\
                                .then_inc(act_ready[c], 1)
                            continue
                        v.tensor_tensor(pr[:, c, p % 2, :], bank(c, MM), pr[:, c, p % 2, :], ALU.mult)\
                            .then_inc(u_gated[c], 1)
                        dve.wait_ge(u_gated[c], i * EP + p + 1)
                        dve.wait_ge(c_psum[c], i * (E0 + EP) + E0 + p + 1)
                        v.tensor_tensor(pr[:, c, 2 + p % 2, :], bank(c, SA), pr[:, c, p % 2, :], ALU.mult)\
                            .then_inc(act_ready[c], 1)
                for c in range(2):
                    dve.wait_ge(resT_psum[c], i * 6 + 6)
                    v.tensor_tensor(Y[c], bank(c, TR), X[:, c, :], ALU.add).then_inc(y_ready[c], 1)
                dve.wait_ge(dve_step, steps[0])
                dve.sem_clear(dve_step)


def kernel(**inputs):
    import numpy as np
    import concourse.bacc as bacc
    from concourse.bass_utils import run_bass_kernel_spmd

    a = {k: np.asarray(v) for k, v in inputs.items()}
    f32 = np.float32

    def col(v):
        return np.ascontiguousarray(np.asarray(v).reshape(-1, P).T)

    def chunks(m):
        return m.reshape(-1, P, m.shape[1]).transpose(1, 0, 2).reshape(P, -1)

    rows_ = np.arange(P)
    qkv_w, qkv_b, in_w, in_b = (a["L0_xattn_" + n] for n in ("qkv_w", "qkv_b", "in_proj_w", "in_proj_b"))
    gu = a["L1_ffn_experts_gate_up"]
    part = {
        "ident": np.eye(P, dtype=f32),
        "head_of_row": (rows_[:, None] // D0 == np.arange(H0)[None]).astype(f32),
        "sa_b": col(a["L0_xattn_sa_out_b"]), "sa_bv": col(qkv_b[2 * P:]),
        "ln1_g": col(a["L0_xattn_ln1_g"]), "ln1_b": col(a["L0_xattn_ln1_b"]),
        "bq": col(in_b[:P]), "bk": col(in_b[P:2 * P]), "bv": col(in_b[2 * P:]),
        "mha_b": col(a["L0_xattn_mha_out_b"]),
        "ln2_g": col(a["L0_xattn_ln2_g"]), "ln2_b": col(a["L0_xattn_ln2_b"]),
        "lin1_b": col(a["L0_xattn_lin1_b"]), "lin2_b": col(a["L0_xattn_lin2_b"]),
        "b1": col(a["L0_ffn_b1"]),
        "lnl_w": col(a["L1_xattn_ln_l_w"]), "lnl_b": col(a["L1_xattn_ln_l_b"]),
        "lnx_w": col(a["L1_xattn_ln_x_w"]), "lnx_b": col(a["L1_xattn_ln_x_b"]),
        "qs": col(np.tile(a["L1_xattn_q_scale"], 2)), "ks": col(np.tile(a["L1_xattn_k_scale"], 2)),
        "sa_wv": qkv_w[2 * P:], "sa_oT": a["L0_xattn_sa_out_w"].T,
        "wqT": in_w[:P].T, "wkT": in_w[P:2 * P].T, "wvT": in_w[2 * P:].T,
        "mha_oT": a["L0_xattn_mha_out_w"].T,
        "lin1T": a["L0_xattn_lin1_w"].T, "lin2T": chunks(a["L0_xattn_lin2_w"].T),
        "Wk": a["L1_xattn_Wkv"][:, :INNER], "Wv": a["L1_xattn_Wkv"][:, INNER:],
        "gate_w": a["L0_ffn_gate_w"],
        "w1": a["L0_ffn_w1"].transpose(1, 0, 2).reshape(P, -1), "w2": a["L0_ffn_w2"].transpose(1, 0, 2).reshape(P, -1),
        "Wq": a["L1_xattn_Wq"], "Wo": chunks(a["L1_xattn_Wo"]),
        "route_wT": a["L1_ffn_gate_weight"].T,
        "gateT": gu[:, :I1].reshape(E1 * I1, P).T, "upT": gu[:, I1:].reshape(E1 * I1, P).T,
        "downT": chunks(a["L1_ffn_experts_down"].transpose(0, 2, 1).reshape(E1 * I1, P)),
        "sh_gateT": a["L1_ffn_shared_gate_w"].T, "sh_upT": a["L1_ffn_shared_up_w"].T,
        "sh_downT": a["L1_ffn_shared_down_w"].T,
        "ln3_g": a["L0_xattn_ln3_g"], "ln3_b": a["L0_xattn_ln3_b"],
        "lno_w": a["L1_xattn_ln_o_w"], "lno_b": a["L1_xattn_ln_o_b"],
        "gate_b": a["L0_ffn_gate_b"], "route_b": a["L1_ffn_e_score_correction_bias"],
        "qs_row": a["L1_xattn_q_scale"], "ks_row": a["L1_xattn_k_scale"],
    }
    slab = [np.ascontiguousarray(np.concatenate([part[n] for n, _ in s], axis=1)) for s in
            (SLAB_A, SLAB_B, SLAB_C, SLAB_D)]
    rows = np.concatenate([part[n] for n, _ in ROWS])[None]
    mask = np.ascontiguousarray(np.tile(a["mask_BxS2_bk0"].T, (HG, 1)))
    sel0 = (np.arange(E0)[:, None, None] == np.arange(E0)[None, :, None]) * np.ones((1, 1, P))
    sel1 = (np.arange(E1)[:, None] == np.repeat(np.arange(E1), I1)[None])
    arrays = {
        "x": a["x"], "ctx": a["ctx_1024"], "mask": mask, "slab_a": slab[0], "slab_b": slab[1],
        "slab_c": slab[2], "slab_d": slab[3], "rows": rows, "b2": a["L0_ffn_b2"],
        "sel0": sel0.reshape(E0, -1).astype(f32), "sel1": sel1.astype(f32),
    }
    nc = bacc.Bacc("TRN2", target_bir_lowering=False, num_devices=1)
    arrays = {k: np.ascontiguousarray(v) for k, v in arrays.items()}
    args = [nc.dram_tensor(k, v.shape, mybir.dt.from_np(v.dtype), kind="ExternalInput").ap()
            for k, v in arrays.items()]
    args.append(nc.dram_tensor("out", (B, S, P), F32, kind="ExternalOutput").ap())
    nc.disable_value_cache = True
    two_layer_kernel(nc, *args)
    return run_bass_kernel_spmd(nc, [arrays], core_ids=[0]).results[0]["out"]
```

```python
from contextlib import ExitStack

import concourse.bass as bass
from concourse import mybir

F32, F16, BF16, U8 = mybir.dt.float32, mybir.dt.float16, mybir.dt.bfloat16, mybir.dt.uint8
ALU = mybir.AluOpType
ACT = mybir.ActivationFunctionType
AX = mybir.AxisListType

P = 128
B, S, M = 4, 512, 32
NT = S // P
H0, D0 = 8, 16
FF = 512
FC = FF // P
E0, K0 = 8, 2
H1, D1 = 8, 64
INNER = H1 * D1
PAIRS = H1 // 2
HG = P // M
E1, I1 = 32, 64
EP = E1 // 2
PLANES = EP + 1
NG, TG, K1 = 8, 4, 6
GS = E1 // NG
ROUTE_SCALE = 2.5
SIM_SCALE = 8.0
EPS = 1e-5
L2_EPS = 1e-12
SENT = -3.0e38
PICK = 3.0e38
MASKED = 1.0e30
EXP_ROOM = 80.0
WS = 2.0 ** 10
AS = 2.0 ** 6
DS = 1.0 / (WS * AS)
QS = 2.0 ** 8
LNS = (6, 2)
PARTS = 3

SLAB_A = [("ident", P), ("head_of_row", H0),
          ("sa_b", 1), ("sa_bv", 1), ("ln1_g", 1), ("ln1_b", 1), ("bq", 1), ("bk", 1), ("bv", 1), ("mha_b", 1),
          ("ln2_g", 1), ("ln2_b", 1), ("lnl_w", 1), ("lnl_b", 1), ("lin1_b", FC), ("lin2_b", 1), ("b1", E0),
          ("lnx_w", 1), ("lnx_b", 1),
          ("sa_wv", P), ("sa_oT", P), ("wqT", P), ("wkT", P), ("wvT", P), ("mha_oT", P)]
SLAB_B = [("lin2T", FC * P), ("gate_w", E0), ("w2", E0 * P), ("Wo", PAIRS * P),
          ("route_wT", E1), ("downT", EP * P), ("sh_downT", P)]
SLAB_S = [("lin1T", FF), ("w1", E0 * P), ("Wk", INNER), ("Wv", INNER), ("Wq", INNER)]
SLAB_G = [("gateT", EP * P), ("upT", EP * P)]
SLAB_H = [("sh_gateT", P), ("sh_upT", P)]
ROWS = [("ln3_g", P), ("ln3_b", P), ("lno_w", P), ("lno_b", P), ("gate_b", E0), ("route_b", E1),
        ("qs_row", D1), ("ks_row", D1)]

LAYER0 = (["x_stats", "x_norm", "x_turn", "fold", "fold_back", "n1_norm", "n1_turn", "q0", "scores", "exp0",
           "probs", "probs_turn", "ca", "ca_back", "n2_norm", "n2_turn"] + [("lin1", k) for k in range(FC)] +
          ["lin2", "lin2_back", "n3_norm", "y_stats", "y_norm", "y_turn", "gate0", "comb0_turn"] +
          [("expert", e) for e in range(E0)] + ["moe_out", "moe_back", "lat_norm", "lat_turn"])
ATTN = []
for _g in range(H1 // HG):
    ATTN.append(("ctx", _g, 0))
    ATTN += [("own", _h, _kt) for _h in range(_g * HG, (_g + 1) * HG) for _kt in range(NT)]
NS = len(ATTN)
LAG = 2
TILES = [[("qk_rows", 0)], [], [("v_rows", 0), ("l2norm", 0)]]
for _k in range(1, NT):
    TILES += [[("halves", _k - 1), ("qk_rows", _k)], [("turn_A", _k - 1)],
              [("turn_B", _k - 1), ("v_rows", _k), ("l2norm", _k)]]
TILES += [[("halves", NT - 1)], [("turn_A", NT - 1)], [("turn_B", NT - 1)]]
LAYER1 = ([("attn", n) for n in range(NS + LAG + 2)] +
          ["wo", "wo_back", "no_norm", "z_stats", "z_norm", "z_turn", "route", "route_pick", "comb1_turn"] +
          [("ffn", p) for p in range(PLANES)] + ["ffn_out", "ffn_back"])


EARLY = [0, 0, 3, 4, 5, 5, 8, 9, 10, 11, 12, 15, 16, 18, 18, 21, 22, 23, 24, 25, 26, 27, 27, 28, 29, 32, 33, 36]
LATE = [("attn", NS + LAG), ("attn", NS + LAG + 1), "wo", "wo_back", "no_norm", "z_stats", "z_turn", "route",
        "route_pick", "route_pick", ("ffn", 0), ("ffn", 2)]


def merged():
    at = {}

    def put(after, stream, steps):
        at.setdefault(after, []).extend((stream, s) for s in steps)

    experts = LAYER0.index(("expert", 0))
    for at_attn, step in zip(EARLY, LAYER0[:experts], strict=True):
        put(("attn", at_attn), 0, [step])
    for after, step in zip(LATE, LAYER0[experts:], strict=True):
        put(after, 0, [step])
    for p, steps in zip(range(3, PLANES), TILES[:-1], strict=True):
        put(("ffn", p), 2, steps)
    put("ffn_back", 2, TILES[-1])
    return [s for x in LAYER1 for s in [(1, x)] + at.get(x, [])]


BODY = merged()


def width(cols):
    return sum(n for _, n in cols)


def offsets(cols):
    at, out = 0, {}
    for name, n in cols:
        out[name] = (at, n)
        at += n
    return out


def two_layer_kernel(nc, x, ctx_in, mask, slab_a, slab_b, slab_s, slab_g, slab_h, rows, b2_in, sel0_in, sel1_in,
                     out):
    with ExitStack() as stack:
        def sb(name, shape, dt=F32):
            return stack.enter_context(nc.sbuf_tensor("s_" + name, shape, dt))

        def sem(name):
            return stack.enter_context(nc.semaphore(name))

        def sem2(name):
            return [sem(f"{name}_layer{hf}") for hf in range(2)]

        X0 = sb("X0", [P, NT * P])
        X = sb("X", [P, 2, NT * P])
        Y = sb("Y", [P, NT * P])
        nrm = sb("nrm", [P, 2, NT * P])
        feat = sb("feat", [P, 2, S])
        res = sb("res", [P, 2, S])
        stat = sb("stat", [P, 2, NT, 6])
        mv = sb("mv", [P, 2, NT, 2])
        ve = sb("ve", [P, 2, NT])
        rstd = sb("rstd", [P, 2, NT])
        tmp4 = sb("tmp4", [P, NT])
        xh, xl, lath, latl, zh, zl = (sb(n, [P, S], F16) for n in ("xh", "xl", "lath", "latl", "zh", "zl"))
        soft = sb("soft", [P, 4, S])
        sc = soft[:, 0:2, :].rearrange("p a s -> p (a s)")
        pT = soft[:, 2:4, :]
        hT = soft
        hmax, hsum, hrec = (sb(n, [P, NT * H0]) for n in ("hmax", "hsum", "hrec"))
        er = sb("er", [P, 4, S])
        q0T = er[:, 3, :]
        rt0 = sb("rt0", [P, NT, 2 * E0])
        mx0, top0 = (sb(n, [P, NT, 8]) for n in ("mx0", "top0"))
        hit0 = sb("hit0", [P, NT, 2 * E0])
        comb0 = sb("comb0", [P, NT, E0])
        part0 = sb("part0", [P, NT, PARTS, E0], BF16)
        comb0T = sb("comb0T", [PARTS * E0, S], BF16)
        q16 = sb("q16", [P, H1, 2 * D1], F16)
        k16 = sb("k16", [P, H1, 3 * D1], F16)
        big = sb("big", [P, 3, H1, S], F16)
        qT, kA, kB = (big[:, k, :, :] for k in range(3))
        vt = sb("vt", [P, NT, PAIRS, 3 * D1])
        pr = sb("pr", [P, NT, S])
        qk = pr[:, 0:2, :]
        aT = sb("aT", [P, PAIRS, S])
        ssq, rn, nn = (sb(n, [P, 2 * H1]) for n in ("ssq", "rn", "nn"))
        sq = aT[:, 0:2, :]
        scor, sfc, comb1 = (sb(n, [P, NT, E1]) for n in ("scor", "sfc", "comb1"))
        grp, hitg = (sb(n, [P, NT, NG + 8]) for n in ("grp", "hitg"))
        cand, hit1 = (sb(n, [P, NT, E1 + 8]) for n in ("cand", "hit1"))
        mx1, topg, top1 = (sb(n, [P, NT, 8]) for n in ("mx1", "topg", "top1"))
        csum = sb("csum", [P, NT])
        part1 = sb("part1", [P, NT, PARTS, E1], BF16)
        comb1T = sb("comb1T", [PARTS * E1, S], BF16)
        fr = sb("fr", [P, 4, S])
        pc = fr[:, 0:2, :]
        on = fr[:, 2:4, :]
        den = [res[:, 1, :], feat[:, 1, :]]

        WA, WB = sb("WA", [P, width(SLAB_A)]), sb("WB", [P, width(SLAB_B)])
        RW = sb("RW", [P, width(ROWS)])
        WH = sb("WH", [P, width(SLAB_H)])
        halves = sb("halves", [P, 2, width(SLAB_S) + width(SLAB_G) + width(SLAB_H)], F16)
        WSP = vt[:, :, :, :].rearrange("p t a d -> p (t a d)")[:, 0:width(SLAB_S)]
        WG = big[:, :, :, :].rearrange("p k h s -> p (k h s)").bitcast(F32)[:, 0:width(SLAB_G)]
        where = {}
        for tile_, cols in ((WA, SLAB_A), (WB, SLAB_B), (RW, ROWS), (WSP, SLAB_S), (WG, SLAB_G), (WH, SLAB_H)):
            for name, (at, n) in offsets(cols).items():
                where[name] = tile_[:, at:at + n]
        split_at = offsets(SLAB_S + SLAB_G + SLAB_H)

        def W(name, k=None, n=P):
            return where[name] if k is None else where[name][:, k * n:(k + 1) * n]

        def W16(name, part, k=0, n=P):
            at = split_at[name][0] + k * n
            return halves[:, part, at:at + n]

        PIECES = [("lin1T", 0, FF), ("w1", 0, E0 * P), ("Wk", 0, INNER), ("Wv", 0, INNER), ("Wq", 0, INNER)]
        PIECES += [(nm, k * 1024, 1024) for nm in ("gateT", "upT") for k in range(EP * P // 1024)]
        PIECES += [("sh_gateT", 0, P), ("sh_upT", 0, P)]

        ident = W("ident")
        id16 = sb("id16", [P, P], F16)
        idb = sb("idb", [P, P], BF16)
        scaled = sb("scaled", [P, 4])
        b2 = sb("b2", [PARTS * E0, P])
        b2r = sb("b2r", [PARTS * E0, P])
        b2p = sb("b2p", [PARTS * E0, PARTS, P], BF16)
        sel0 = sb("sel0", [PARTS * E0, E0 * P], BF16)
        sel1 = sb("sel1", [PARTS * E1, EP * P], BF16)
        maskb = sb("maskb", [P, B], U8)

        foldT = sb("foldT", [P, P])
        fold_b = sb("fold_b", [P, 1])
        Kb_all = sb("Kb_all", [P, B, H0 * M])
        Vp_all = sb("Vp_all", [P, B, 2, P])
        Vp = sb("Vp", [P, 2, P])
        kc_all = sb("kc_all", [P, 2, H1, B, M], F16)
        kc = sb("kc", [P, 2, H1, P], F16)
        vc_all = sb("vc_all", [P, B, H1 // HG, D1])
        vc = sb("vc", [P, H1, P])
        shift = sb("shift", [P, 1])
        mbias = sb("mbias", [P, B])
        mb = sb("mb", [P, 1])
        qks_row = sb("qks_row", [P, D1])
        mhalf = sb("mhalf", [P, 2 * H1])
        eps_row = sb("eps_row", [P, NT])
        ctx_tok, memT, kT0, vT0 = (aT[:, 0, k * P:(k + 1) * P] for k in range(4))
        ctx_nrm, ctx_nT = (aT[:, 1, k * P:(k + 1) * P] for k in range(2))
        Vb_all = er[:, 0:2, :].rearrange("p a s -> p (a s)")
        sqc, vctx, kcn = fr[:, 0, :], fr[:, 1, :], fr[:, 2, :]

        PS = stack.enter_context(nc.psum_tensor("PS", [P, 8, 512], F32))
        TR, MM, SA, SB_ = 0, 1, 2, 3

        def bank(hf, which):
            return PS[:, 4 * hf + which, :]

        ctx_loaded, wa_in, ws_in, wb_in, wg_in, small_in = (sem(n) for n in (
            "ctx_loaded", "wa_in", "ws_in", "wb_in", "wg_in", "small_in"))
        x_loaded, x0_free, y_ready, stored = (sem(n) for n in ("x_loaded", "x0_free", "y_ready", "stored"))
        su_pe, su_act, su_dve, su_pool = (sem(n) for n in ("su_pe", "su_act", "su_dve", "su_pool"))
        high_done, low_done = sem("high_done"), sem("low_done")
        dve_step, pool_step = sem("dve_step"), sem("pool_step")
        staged0, staged1 = sem("staged0"), sem("staged1")
        stats_ready, rstd_ready, nrm_ready, nrmT_psum, feat_ready, split_ready = (sem2(n) for n in (
            "stats_ready", "rstd_ready", "nrm_ready", "nrmT_psum", "feat_ready", "split_ready"))
        prod_psum, res_ready, resT_psum = (sem2(n) for n in ("prod_psum", "res_ready", "resT_psum"))
        q0_psum, q0_ready, score_psum, centred, exped, rec_ready, probs_ready, probT_psum, pT0_ready, pT1_ready = (
            sem(n) for n in ("q0_psum", "q0_ready", "score_psum", "centred", "exped", "rec_ready", "probs_ready",
                             "probT_psum", "pT0_ready", "pT1_ready"))
        lin1_psum, hid_ready = sem("lin1_psum"), sem("hid_ready")
        gate_psum, comb_ready, combT_psum, combT_ready = (sem2(n) for n in (
            "gate_psum", "comb_ready", "combT_psum", "combT_ready"))
        h_psum, w0_psum, relu_ready, gated, down_done, moe_ready = (sem(n) for n in (
            "h_psum", "w0_psum", "relu_ready", "gated", "down_done", "moe_ready"))
        x_moved = sem("x_moved")
        qk_psum, v_psum, sq_ready, ssq_ready, rn_ready, qk_used, low_ready = (sem(n) for n in (
            "qk_psum", "v_psum", "sq_ready", "ssq_ready", "rn_ready", "qk_used", "low_ready"))
        high_qk = sem("high_qk")
        v_ready, qT_psum, kA_psum, kB_psum, qT_ready, kA_ready, kB_ready = (sem(n) for n in (
            "v_ready", "qT_psum", "kA_psum", "kB_psum", "qT_ready", "kA_ready", "kB_ready"))
        sim_psum, exp_done, pv_done, head_psum, head_out, pair_ready = (sem(n) for n in (
            "sim_psum", "exp_done", "pv_done", "head_psum", "head_out", "pair_ready"))
        wo_ready, sig_ready = sem("wo_ready"), sem("sig_ready")
        g_psum, u_psum, w1_psum, silu_ready, u_gated, act_ready, ffn_down, ffn_ready = (sem(n) for n in (
            "g_psum", "u_psum", "w1_psum", "silu_ready", "u_gated", "act_ready", "ffn_down", "ffn_ready"))

        block = stack.enter_context(nc.Block())

        @block.sync
        def _(sp):
            def batch(dram, b):
                return dram[bass.ds(b, 1)].rearrange("o (p t) f -> p (o t f)", p=P)

            sp.dma_start(ctx_tok, ctx_in.rearrange("b m f -> (b m) f")).then_inc(ctx_loaded, 16)
            sp.dma_start(WA[:, :], slab_a).then_inc(wa_in, 16)
            sp.dma_start(X0[:, :], batch(x, 0)).then_inc(x_loaded, 16)
            sp.dma_start(WSP, slab_s).then_inc(ws_in, 16)
            sp.dma_start(RW[:, :], rows[0, :].partition_broadcast(P)).then_inc(small_in, 16)
            sp.dma_start(maskb[:, :], mask).then_inc(small_in, 16)
            sp.dma_start(b2[:, :], b2_in).then_inc(small_in, 16)
            sp.dma_start(sel0[:, :], sel0_in).then_inc(small_in, 16)
            sp.dma_start(sel1[:, :], sel1_in).then_inc(small_in, 16)
            sp.dma_start(WB[:, :], slab_b).then_inc(wb_in, 16)
            sp.dma_start(WG, slab_g).then_inc(wg_in, 16)
            sp.dma_start(WH[:, :], slab_h).then_inc(wg_in, 16)
            sp.wait_ge(x0_free, 1)
            sp.dma_start(X0[:, :], batch(x, 1)).then_inc(x_loaded, 16)
            with sp.Fori(0, B - 2) as i:
                sp.wait_ge(y_ready, i + 1)
                sp.dma_start(batch(out, i), Y[:, :]).then_inc(stored, 16)
                sp.wait_ge(x0_free, i + 2)
                sp.wait_ge(stored, 16 * (i + 1))
                sp.dma_start(X0[:, :], batch(x, i + 2)).then_inc(x_loaded, 16)
            for b in (B - 2, B - 1):
                sp.wait_ge(y_ready, b + 1)
                sp.dma_start(batch(out, b), Y[:, :]).then_inc(stored, 16)
            sp.wait_ge(stored, 16 * B)

        @block.tensor
        def _(pe):
            mm = nc.tensor.matmul

            def turn(dst, src):
                for t in range(NT):
                    last = nc.tensor.transpose(dst[:, t * P:(t + 1) * P], src[:, t * P:(t + 1) * P], ident)
                return last

            def mm3(dst, stat_parts, mov_parts, start=True, stop=True):
                mm(dst, stat_parts[0], mov_parts[0], start=start, stop=False)
                mm(dst, stat_parts[0], mov_parts[1], start=False, stop=False)
                return mm(dst, stat_parts[1], mov_parts[0], start=False, stop=stop)

            pe.wait_ge(ctx_loaded, 16)
            pe.wait_ge(wa_in, 16)
            nc.tensor.transpose(PS[:, 4, 0:P], ctx_tok, ident).then_inc(su_pe, 1)
            mm(PS[:, 5, 0:P], W("sa_wv"), W("sa_oT"), start=True, stop=True).then_inc(su_pe, 1)
            mm(PS[:, 6, 0:1], W("sa_oT"), W("sa_bv"), start=True, stop=True).then_inc(su_pe, 1)
            pe.wait_ge(su_act, 1)
            mm(PS[:, 7, 0:P], W("wkT"), memT, start=True, stop=True)
            mm(PS[:, 7, P:2 * P], W("wvT"), memT, start=True, stop=True).then_inc(su_pe, 1)
            pe.wait_ge(su_dve, 2)
            nc.tensor.transpose(PS[:, 4, 0:P], ctx_nrm, ident).then_inc(su_pe, 1)
            pe.wait_ge(su_dve, 3)
            pe.wait_ge(su_act, 2)
            for k in range(2 * B):
                last = mm(PS[:, 5 + k // 4, k % 4 * P:(k % 4 + 1) * P], Vb_all[:, k * P:(k + 1) * P], W("mha_oT"),
                          start=True, stop=True)
            last.then_inc(su_pe, 1)
            pe.wait_ge(ws_in, 16)
            pe.wait_ge(su_act, 3)
            mm(PS[:, 7, :], ctx_nT, W("Wk"), start=True, stop=True).then_inc(su_pe, 1)
            mm(PS[:, 4, :], ctx_nT, W("Wv"), start=True, stop=True).then_inc(su_pe, 1)
            pe.wait_ge(su_dve, 5)
            pe.wait_ge(su_act, 4)
            for s in range(2):
                dst = PS[:, 5 + s, :].bitcast(F16).rearrange("p (h k) -> p h k", k=P)
                for h in range(H1):
                    last = nc.tensor.transpose(dst[:, h, :], k16[:, h, s * D1:s * D1 + P], id16[:, :])
            last.then_inc(su_pe, 1)

            def layer0(step, b):
                name, k = step if isinstance(step, tuple) else (step, 0)

                def tokens_to_features(n, turned, dst):
                    pe.wait_ge(nrm_ready[0], b * LNS[0] + n)
                    turn(bank(0, dst), nrm[:, 0, :]).then_inc(nrmT_psum[0], 1)

                def features_to_tokens(n):
                    pe.wait_ge(res_ready[0], b * 3 + n)
                    turn(bank(0, TR), res[:, 0, :]).then_inc(resT_psum[0], 1)

                if name == "x_turn":
                    tokens_to_features(1, 1, MM)
                elif name == "fold":
                    pe.wait_ge(feat_ready[0], b * 5 + 1)
                    pe.wait_ge(su_act, 2)
                    mm(bank(0, SA), foldT[:, :], feat[:, 0, :], start=True, stop=True).then_inc(prod_psum[0], 1)
                elif name == "fold_back":
                    features_to_tokens(1)
                elif name == "n1_turn":
                    tokens_to_features(2, 2, MM)
                elif name == "q0":
                    pe.wait_ge(feat_ready[0], b * 5 + 2)
                    mm(bank(0, SA), W("wqT"), feat[:, 0, :], start=True, stop=True).then_inc(q0_psum, 1)
                elif name == "scores":
                    pe.wait_ge(q0_ready, b + 1)
                    for t in range(NT):
                        last = mm(PS[:, SA + t // 2, (t % 2) * 256:(t % 2) * 256 + 256], q0T[:, t * P:(t + 1) * P],
                                  Kb_all[:, bass.ds(b, 1), :].rearrange("p o n -> p (o n)"), start=True, stop=True)
                    last.then_inc(score_psum, 1)
                elif name == "probs_turn":
                    pe.wait_ge(probs_ready, b + 1)
                    for half in range(2):
                        for t in range(NT):
                            at = t * H0 * M + half * P
                            last = nc.tensor.transpose(bank(0, SA + half)[:, t * P:(t + 1) * P], sc[:, at:at + P],
                                                       ident)
                    last.then_inc(probT_psum, 1)
                elif name == "ca":
                    pe.wait_ge(pT0_ready, b + 1)
                    pe.wait_ge(staged0, b + 1)
                    mm(bank(0, MM), Vp[:, 0, :], pT[:, 0, :], start=True, stop=False)
                    pe.wait_ge(pT1_ready, b + 1)
                    mm(bank(0, MM), Vp[:, 1, :], pT[:, 1, :], start=False, stop=True).then_inc(prod_psum[0], 1)
                elif name == "ca_back":
                    features_to_tokens(2)
                elif name == "n2_turn":
                    tokens_to_features(3, 3, MM)
                elif name == "lin1":
                    if k == 0:
                        pe.wait_ge(split_ready[0], b * 3 + 1)
                        pe.wait_ge(low_done, 1)
                    mm3(bank(0, (SA, SB_, TR, MM)[k]), [W16("lin1T", s, k) for s in range(2)],
                        [xh[:, :], xl[:, :]]).then_inc(lin1_psum, 1)
                elif name == "lin2":
                    pe.wait_ge(wb_in, 16)
                    for j in range(FC):
                        pe.wait_ge(hid_ready, b * FC + j + 1)
                        last = mm(bank(0, SA), W("lin2T", j), hT[:, j, :], start=(j == 0), stop=(j == FC - 1))
                    last.then_inc(prod_psum[0], 1)
                elif name == "lin2_back":
                    features_to_tokens(3)
                elif name == "y_turn":
                    tokens_to_features(5, 4, MM)
                elif name == "gate0":
                    pe.wait_ge(feat_ready[0], b * 5 + 4)
                    for t in range(NT):
                        last = mm(bank(0, SA)[:, t * E0:(t + 1) * E0], feat[:, 0, t * P:(t + 1) * P], W("gate_w"),
                                  start=True, stop=True)
                    last.then_inc(gate_psum[0], 1)
                elif name == "comb0_turn":
                    pe.wait_ge(comb_ready[0], b + 1)
                    dst = bank(0, SB_).bitcast(BF16)
                    for t in range(NT):
                        last = nc.tensor.transpose(dst[0:PARTS * E0, t * P:(t + 1) * P],
                                                   part0[:, t, :, :].rearrange("p k e -> p (k e)"), idb[:, :])
                    last.then_inc(combT_psum[0], 1)
                elif name in ("expert", "moe_out"):
                    e = k if name == "expert" else E0
                    if e < E0:
                        if e == 0:
                            pe.wait_ge(split_ready[0], b * 3 + 2)
                            pe.wait_ge(low_done, 2)
                        if e >= 2:
                            pe.wait_ge(relu_ready, b * E0 + e - 1)
                        mm3(bank(0, (TR, MM)[e % 2]), [W16("w1", s, e) for s in range(2)],
                            [xh[:, :], xl[:, :]]).then_inc(h_psum, 1)
                    if e == 0:
                        pe.wait_ge(combT_ready[0], b + 1)
                        pe.wait_ge(su_dve, 7)
                        for s in range(PARTS):
                            mm(bank(0, SB_), b2p[:, s, :], comb0T[:, :], start=(s == 0), stop=False)
                    else:
                        pe.wait_ge(gated, b * E0 + e)
                        mm(bank(0, SB_), W("w2", e - 1), er[:, 2 + (e - 1) % 2, :], start=False, stop=(e == E0))\
                            .then_inc(down_done, 1)
                    if e < E0:
                        mm(bank(0, SA), sel0[:, e * P:(e + 1) * P], comb0T[:, :], start=True, stop=True)\
                            .then_inc(w0_psum, 1)
                elif name == "moe_back":
                    pe.wait_ge(moe_ready, b + 1)
                    turn(bank(0, TR), res[:, 0, :]).then_inc(resT_psum[0], 1)
                elif name == "lat_turn":
                    tokens_to_features(6, 5, MM)

            def tiles(step, b):
                name, k = step
                n = b * NT + k + 1
                lat = [z[:, k * P:(k + 1) * P] for z in (lath, latl)]

                def turn16(which, src, at):
                    dst = bank(0, which).bitcast(F16).rearrange("p (h k) -> p h k", k=P)
                    for h in range(H1):
                        last = nc.tensor.transpose(dst[:, h, :], src[:, h, at:at + P], id16[:, :])
                    return last

                if name == "qk_rows":
                    if k == 0:
                        pe.wait_ge(split_ready[0], b * 3 + 3)
                        pe.wait_ge(low_done, len(PIECES))
                    else:
                        pe.wait_ge(qk_used, n - 1)
                    mm3(bank(0, MM), lat, [W16("Wq", s, 0, INNER) for s in range(2)])
                    mm3(bank(0, SA), lat, [W16("Wk", s, 0, INNER) for s in range(2)]).then_inc(qk_psum, 1)
                elif name == "v_rows":
                    if k > 0:
                        pe.wait_ge(kA_ready, n - 1)
                    mm3(bank(0, SB_), lat, [W16("Wv", s, 0, INNER) for s in range(2)]).then_inc(v_psum, 1)
                elif name == "turn_A":
                    pe.wait_ge(low_ready, n)
                    if k > 0:
                        pe.wait_ge(kB_ready, n - 1)
                    turn16(TR, q16, 0).then_inc(qT_psum, 1)
                    pe.wait_ge(v_ready, n)
                    turn16(SB_, k16, 0).then_inc(kA_psum, 1)
                elif name == "turn_B":
                    pe.wait_ge(qT_ready, n)
                    turn16(TR, k16, D1).then_inc(kB_psum, 1)

            def layer1(step, b):
                name, k = step if isinstance(step, tuple) else (step, 0)

                def values(n):
                    kind, h, kt = ATTN[n]
                    pe.wait_ge(exp_done, b * NS + n + 1)
                    if kind == "ctx":
                        return
                    if kt == 0 and h >= 2:
                        pe.wait_ge(head_out, b * H1 + h - 1)
                    mm(bank(1, SA + h % 2), vt[:, kt, h // 2, D1 * (h % 2):D1 * (h % 2) + P], pr[:, kt, :],
                       start=(kt == 0), stop=False).then_inc(pv_done, 1)
                    if kt == NT - 1:
                        mm(bank(1, SA + h % 2), vc[:, h, :], pc[:, h // HG, :], start=False, stop=True)\
                            .then_inc(head_psum, 1)

                if name == "attn":
                    if k == 0:
                        pe.wait_ge(qT_ready, b * NT + NT)
                        pe.wait_ge(kA_ready, b * NT + NT)
                        pe.wait_ge(kB_ready, b * NT + NT)
                        pe.wait_ge(staged1, b + 1)
                    if LAG <= k < NS + LAG:
                        values(k - LAG)
                    if k < NS:
                        kind, h, kt = ATTN[k]
                        dst = bank(1, (TR, MM)[k % 2])
                        if kind == "ctx":
                            for j in range(HG):
                                for s in range(2):
                                    last = mm(dst, kc[:, s, h * HG + j, :], qT[:, h * HG + j, :],
                                              start=(j + s == 0), stop=(j + s == HG))
                        else:
                            mm(dst, kA[:, h, kt * P:(kt + 1) * P], qT[:, h, :], start=True, stop=False)
                            last = mm(dst, kB[:, h, kt * P:(kt + 1) * P], qT[:, h, :], start=False, stop=True)
                        last.then_inc(sim_psum, 1)
                elif name == "wo":
                    for q in range(PAIRS):
                        if q >= PAIRS - 2:
                            pe.wait_ge(pair_ready, b * PAIRS + q + 1)
                        last = mm(bank(1, MM), W("Wo", q), aT[:, q, :], start=(q == 0), stop=(q == PAIRS - 1))
                    last.then_inc(prod_psum[1], 1)
                elif name == "wo_back":
                    pe.wait_ge(wo_ready, b + 1)
                    turn(bank(1, TR), res[:, 1, :]).then_inc(resT_psum[1], 1)
                elif name == "z_turn":
                    pe.wait_ge(nrm_ready[1], b * LNS[1] + 2)
                    turn(bank(1, MM), nrm[:, 1, :]).then_inc(nrmT_psum[1], 1)
                elif name == "route":
                    pe.wait_ge(feat_ready[1], b + 1)
                    for t in range(NT):
                        last = mm(bank(1, SA)[:, t * E1:(t + 1) * E1], feat[:, 1, t * P:(t + 1) * P], W("route_wT"),
                                  start=True, stop=True)
                    last.then_inc(gate_psum[1], 1)
                elif name == "comb1_turn":
                    pe.wait_ge(comb_ready[1], b + 1)
                    dst = bank(1, SB_).bitcast(BF16)
                    for t in range(NT):
                        last = nc.tensor.transpose(dst[0:PARTS * E1, t * P:(t + 1) * P],
                                                   part1[:, t, :, :].rearrange("p k e -> p (k e)"), idb[:, :])
                    last.then_inc(combT_psum[1], 1)
                elif name in ("ffn", "ffn_out"):
                    p = k if name == "ffn" else PLANES
                    if p < PLANES:
                        if p == 0:
                            pe.wait_ge(split_ready[1], b + 1)
                        else:
                            pe.wait_ge(silu_ready, b * PLANES + p)
                        src = [W16("gateT" if p < EP else "sh_gateT", s, p % EP) for s in range(2)]
                        mm3(bank(1, TR), src, [zh[:, :], zl[:, :]]).then_inc(g_psum, 1)
                        if p >= 1:
                            pe.wait_ge(u_gated, b * EP + p)
                        src = [W16("upT" if p < EP else "sh_upT", s, p % EP) for s in range(2)]
                        mm3(bank(1, MM), src, [zh[:, :], zl[:, :]]).then_inc(u_psum, 1)
                    if p == 0:
                        pe.wait_ge(combT_ready[1], b + 1)
                    else:
                        pe.wait_ge(act_ready, b * PLANES + p)
                        mm(bank(1, SB_), W("downT", p - 1) if p <= EP else W("sh_downT"),
                           fr[:, 2 + (p - 1) % 2, :], start=(p == 1), stop=(p == PLANES)).then_inc(ffn_down, 1)
                    if p < EP:
                        mm(bank(1, SA), sel1[:, p * P:(p + 1) * P], comb1T[:, :], start=True, stop=True)\
                            .then_inc(w1_psum, 1)
                elif name == "ffn_back":
                    pe.wait_ge(ffn_ready, b + 1)
                    turn(bank(1, TR), res[:, 1, :]).then_inc(resT_psum[1], 1)

            pe.wait_ge(su_dve, 6)
            pe.wait_ge(small_in, 80)
            for step in LAYER0:
                layer0(step, 0)
            for step in sum(TILES, []):
                tiles(step, 0)
            with pe.Fori(0, B - 1) as i:
                for stream, step in BODY:
                    (layer0, layer1, tiles)[stream](step, i if stream == 1 else i + 1)
            for step in LAYER1:
                layer1(step, B - 1)

        @block.scalar
        def _(act):
            def copy(dst, src, scale=1.0):
                return nc.scalar.activation(dst, src, ACT.Copy, scale=scale)

            def affine(dst, src, scale, bias):
                return nc.scalar.activation(dst, src, ACT.Identity, bias=bias, scale=scale)

            act.wait_ge(su_pe, 1)
            copy(memT, PS[:, 4, 0:P]).then_inc(su_act, 1)
            act.wait_ge(su_pe, 2)
            copy(foldT[:, :], PS[:, 5, 0:P]).then_inc(su_act, 1)
            act.wait_ge(su_pe, 5)
            affine(ctx_nT, PS[:, 4, 0:P], W("lnx_w"), W("lnx_b")).then_inc(su_act, 1)
            act.wait_ge(su_pe, 6)
            copy(Vp_all[:, :, :, :].rearrange("p b h c -> p (b h) c"),
                 PS[:, 5:7, :].rearrange("p a (h c) -> p (a h) c", c=P)).then_inc(su_act, 1)
            act.wait_ge(su_pe, 7)
            nc.scalar.activation(sqc, PS[:, 7, :], ACT.Square).then_inc(su_act, 1)
            act.wait_ge(su_pe, 8)
            copy(vctx, PS[:, 4, :]).then_inc(su_act, 1)

            def split_high(n):
                nm, c0, cols = PIECES[n]
                if nm in dict(SLAB_G) or nm in dict(SLAB_H):
                    act.wait_ge(wg_in, 32)
                else:
                    act.wait_ge(ws_in, 16)
                at = split_at[nm][0] + c0
                copy(halves[:, 0, at:at + cols], W(nm)[:, c0:c0 + cols], WS).then_inc(high_done, 1)

            def layer0(step, b):
                name, k = step if isinstance(step, tuple) else (step, 0)

                def features_out(n, scale=None, bias=None, scaled_at=None, high=None):
                    act.wait_ge(nrmT_psum[0], b * 5 + n)
                    src, dst = bank(0, MM), feat[:, 0, :]
                    last = copy(dst, src) if scale is None else affine(dst, src, scale, bias)
                    if high is not None:
                        last = copy(high, src, AS) if scale is None else \
                            affine(high, src, scaled[:, scaled_at:scaled_at + 1],
                                   scaled[:, scaled_at + 1:scaled_at + 2])
                    last.then_inc(feat_ready[0], 1)

                if name == "x_turn":
                    features_out(1)
                elif name == "n1_turn":
                    features_out(2, W("ln1_g"), W("ln1_b"))
                elif name == "q0":
                    act.wait_ge(q0_psum, b + 1)
                    affine(q0T[:, :], bank(0, SA), 1.0, W("bq")).then_inc(q0_ready, 1)
                elif name == "exp0":
                    act.wait_ge(centred, b + 1)
                    nc.scalar.activation(sc, sc, ACT.Exp, scale=float(D0) ** -0.5).then_inc(exped, 1)
                elif name == "probs_turn":
                    act.wait_ge(probT_psum, b + 1)
                    copy(pT[:, 0, :], bank(0, SA)).then_inc(pT0_ready, 1)
                elif name == "n2_turn":
                    features_out(3, W("ln2_g"), W("ln2_b"), 0, xh[:, :])
                elif name == "lin1":
                    act.wait_ge(lin1_psum, b * FC + k + 1)
                    nc.scalar.activation(hT[:, k, :], bank(0, (SA, SB_, TR, MM)[k]), ACT.Relu,
                                         bias=W("lin1_b")[:, k:k + 1], scale=DS).then_inc(hid_ready, 1)
                elif name == "y_turn":
                    features_out(4, high=xh[:, :])
                elif name == "comb0_turn":
                    act.wait_ge(combT_psum[0], b + 1)
                    copy(comb0T[:, :], bank(0, SB_).bitcast(BF16)[0:PARTS * E0, 0:S]).then_inc(combT_ready[0], 1)
                elif name == "expert":
                    act.wait_ge(h_psum, b * E0 + k + 1)
                    if k >= 2:
                        act.wait_ge(gated, b * E0 + k - 1)
                    nc.scalar.activation(er[:, k % 2, :], bank(0, (TR, MM)[k % 2]), ACT.Relu,
                                         bias=W("b1")[:, k:k + 1], scale=DS).then_inc(relu_ready, 1)
                elif name == "moe_out":
                    act.wait_ge(down_done, b * E0 + E0)
                    copy(res[:, 0, :], bank(0, SB_)).then_inc(moe_ready, 1)
                elif name == "lat_turn":
                    features_out(5, W("lnl_w"), W("lnl_b"), 2, lath[:, :])

            def tiles(step, b):
                name, k = step
                n = b * NT + k + 1
                at = slice(k * P, (k + 1) * P)
                if name == "qk_rows":
                    act.wait_ge(qk_psum, n)
                    if k > 0:
                        act.wait_ge(ssq_ready, n - 1)
                    nc.scalar.activation(sq, PS[:, MM:SB_, :], ACT.Square).then_inc(sq_ready, 1)
                elif name == "v_rows":
                    act.wait_ge(v_psum, n)
                    v4 = bank(0, SB_).rearrange("p (a h d) -> p a h d", h=2, d=D1)
                    for hh in range(2):
                        last = copy(vt[:, k, :, 2 * hh * D1:(2 * hh + 1) * D1], v4[:, :, hh, :], DS)
                    last.then_inc(v_ready, 1)
                elif name == "turn_A":
                    act.wait_ge(qT_psum, n)
                    copy(qT[:, :, at], bank(0, TR).bitcast(F16).rearrange("p (h k) -> p h k", k=P))\
                        .then_inc(qT_ready, 1)
                    act.wait_ge(kA_psum, n)
                    copy(kA[:, :, at], bank(0, SB_).bitcast(F16).rearrange("p (h k) -> p h k", k=P))\
                        .then_inc(kA_ready, 1)

            def layer1(step, b):
                name, k = step if isinstance(step, tuple) else (step, 0)
                if name == "attn":
                    if k < NS:
                        kind, h, kt = ATTN[k]
                        act.wait_ge(sim_psum, b * NS + k + 1)
                        src = bank(1, (TR, MM)[k % 2])
                        scale = SIM_SCALE / (QS * QS)
                        if kind == "ctx":
                            nc.scalar.activation(pc[:, h, :], src, ACT.Exp, bias=mb[:, :], scale=scale)\
                                .then_inc(exp_done, 1)
                        else:
                            if h > 0:
                                act.wait_ge(pv_done, b * H1 * NT + (h - 1) * NT + kt + 1)
                            nc.scalar.activation(pr[:, kt, :], src, ACT.Exp, bias=shift[:, :], scale=scale)\
                                .then_inc(exp_done, 1)
                    if k >= LAG and k - LAG < NS:
                        kind, h, kt = ATTN[k - LAG]
                        if kind == "own" and kt == NT - 1:
                            act.wait_ge(head_psum, b * H1 + h + 1)
                            if h >= 4:
                                act.wait_ge(pair_ready, b * PAIRS + h // 2 - 1)
                            own, other = (slice(D1 * j, D1 * j + D1) for j in (h % 2, 1 - h % 2))
                            copy(den[h // 2 % 2][own, :], bank(1, SA + h % 2)[other, :])
                            copy(on[own, h // 2 % 2, :], bank(1, SA + h % 2)[own, :]).then_inc(head_out, 1)
                elif name == "wo":
                    act.wait_ge(prod_psum[1], b + 1)
                    copy(res[:, 1, :], bank(1, MM)).then_inc(wo_ready, 1)
                elif name == "z_turn":
                    act.wait_ge(nrmT_psum[1], b + 1)
                    copy(feat[:, 1, :], bank(1, MM))
                    copy(zh[:, :], bank(1, MM), AS).then_inc(feat_ready[1], 1)
                elif name == "route":
                    act.wait_ge(gate_psum[1], b + 1)
                    nc.scalar.activation(scor[:, :, :], bank(1, SA)[:, 0:NT * E1].rearrange(
                        "p (t e) -> p t e", e=E1), ACT.Sigmoid).then_inc(sig_ready, 1)
                elif name == "comb1_turn":
                    act.wait_ge(combT_psum[1], b + 1)
                    copy(comb1T[:, :], bank(1, SB_).bitcast(BF16)[0:PARTS * E1, 0:S]).then_inc(combT_ready[1], 1)
                elif name == "ffn":
                    act.wait_ge(g_psum, b * PLANES + k + 1)
                    if k >= 2:
                        act.wait_ge(act_ready, b * PLANES + k - 1)
                    nc.scalar.activation(fr[:, k % 2, :], bank(1, TR), ACT.Silu, scale=DS).then_inc(silu_ready, 1)
                elif name == "ffn_out":
                    act.wait_ge(ffn_down, b * PLANES + PLANES)
                    copy(res[:, 1, :], bank(1, SB_)).then_inc(ffn_ready, 1)

            for n, step in enumerate(LAYER0):
                layer0(step, 0)
                if n % 2 and n // 2 < len(PIECES):
                    split_high(n // 2)
            for step in sum(TILES, []):
                tiles(step, 0)
            with act.Fori(0, B - 1) as i:
                for stream, step in BODY:
                    (layer0, layer1, tiles)[stream](step, i if stream == 1 else i + 1)
            for step in LAYER1:
                layer1(step, B - 1)

        @block.gpsimd
        def _(pool):
            g = nc.gpsimd
            steps = [0]

            def then(ins):
                steps[0] += 1
                ins.then_inc(pool_step, 1)
                pool.wait_ge(pool_step, steps[0])

            g.memset(mhalf[:, :], -0.5)
            g.memset(eps_row[:, :], EPS)
            for tile_ in (rt0, top0, grp, topg, cand, top1):
                g.memset(tile_[:, :, :], SENT)
            g.memset(kc[:, :, :, :], 0.0)
            then(g.memset(vc[:, :, :], 0.0))
            for j in range(HG):
                r = D1 * (1 - j % 2)
                then(g.memset(vc[j * M:(j + 1) * M, j:H1:HG, r:r + D1], 1.0))
            pool.wait_ge(su_dve, 1)
            then(g.tensor_scalar(ve[:, 0, 0:1], mv[:, 0, 0, 1:2], EPS, None, ALU.add))
            g.tensor_tensor(rstd[:, 0, 0:1], ve[:, 0, 0:1], mhalf[:, 0:1], ALU.pow).then_inc(su_pool, 1)
            pool.wait_ge(su_dve, 4)
            then(g.tensor_tensor(nn[:, 0:H1], ssq[:, 0:H1], mhalf[:, 0:H1], ALU.pow))
            g.tensor_scalar(rn[:, 0:H1], nn[:, 0:H1], 1.0 / L2_EPS, QS, ALU.min, ALU.mult)\
                .then_inc(su_pool, 1)
            pool.wait_ge(su_dve, 6)
            then(g.tensor_copy(mb[:, :], mbias[:, 0:1]))
            pool.sem_clear(pool_step)
            steps[0] = 0

            def rsqrt_var(hf, b, n, twice=False):
                pool.wait_ge(stats_ready[hf], b * LNS[hf] + n)
                var = mv[:, hf, :, 1]
                then(g.tensor_tensor(ve[:, hf, :], var, eps_row[:, :], ALU.add))
                ins = g.tensor_tensor(rstd[:, hf, :], ve[:, hf, :], mhalf[:, 0:NT], ALU.pow)
                if twice:
                    then(ins)
                    then(g.tensor_tensor(tmp4[:, :], rstd[:, hf, :], rstd[:, hf, :], ALU.mult))
                    then(g.tensor_tensor(tmp4[:, :], tmp4[:, :], var, ALU.mult))
                    then(g.tensor_tensor(tmp4[:, :], tmp4[:, :], eps_row[:, :], ALU.add))
                    then(g.tensor_tensor(ve[:, hf, :], tmp4[:, :], mhalf[:, 0:NT], ALU.pow))
                    ins = g.tensor_tensor(rstd[:, hf, :], rstd[:, hf, :], ve[:, hf, :], ALU.mult)
                ins.then_inc(rstd_ready[hf], 1)

            def layer0(step, b):
                norms = {"x_stats": 1, "fold_back": 2, "ca_back": 3, "lin2_back": 4, "y_stats": 5, "moe_back": 6}
                if step in norms:
                    rsqrt_var(0, b, norms[step], twice=(step == "moe_back"))
                elif step == "n1_norm":
                    g.tensor_copy(Vp[:, :, :].rearrange("p h f -> p (h f)").unsqueeze(1),
                                  Vp_all[:, bass.ds(b, 1), :, :].rearrange("p o h f -> p o (h f)"))\
                        .then_inc(staged0, 1)
                elif step == "probs":
                    pool.wait_ge(rec_ready, b + 1)
                    p3 = sc.rearrange("p (g m) -> p g m", m=M)
                    g.tensor_tensor(p3, p3, hrec[:, :].unsqueeze(2).broadcast_to([P, NT * H0, M]), ALU.mult)\
                        .then_inc(probs_ready, 1)

            def tiles(step, b):
                name, k = step
                if name == "qk_rows":
                    pool.wait_ge(ssq_ready, b * NT + k + 1)
                    then(g.tensor_tensor(nn[:, :], ssq[:, :], mhalf[:, :], ALU.pow))
                    g.tensor_scalar(rn[:, :], nn[:, :], DS / L2_EPS, QS, ALU.min, ALU.mult).then_inc(rn_ready, 1)
                    then(g.tensor_copy(kc[:, :, k:H1:HG, k * M:(k + 1) * M].rearrange("p s g m -> p (s g) m")
                                       .unsqueeze(2),
                                       kc_all[:, :, k:H1:HG, bass.ds(b, 1), :].rearrange("p s g o m -> p (s g) o m")))
                    r = D1 * (k % 2)
                    then(g.tensor_copy(vc[k * M:(k + 1) * M, k:H1:HG, r:r + D1].unsqueeze(1),
                                       vc_all[k * M:(k + 1) * M, bass.ds(b, 1), :, :]))
                    if k == NT - 1:
                        g.tensor_copy(mb[:, :], mbias[:, bass.ds(b, 1)]).then_inc(staged1, 1)

            def layer1(step, b):
                name, k = step if isinstance(step, tuple) else (step, 0)
                if name == "wo_back":
                    rsqrt_var(1, b, 1)
                elif name == "z_stats":
                    rsqrt_var(1, b, 2)

            def end_of_pass():
                pool.wait_ge(pool_step, steps[0])
                pool.sem_clear(pool_step)
                steps[0] = 0

            for step in LAYER0:
                layer0(step, 0)
            pool.wait_ge(low_done, len(PIECES))
            then(g.memset(vt[:, :, :, D1:2 * D1].rearrange("p t a d -> p (t a) d"), 1.0))
            for step in sum(TILES, []):
                tiles(step, 0)
            end_of_pass()
            with pool.Fori(0, B - 1) as i:
                for stream, step in BODY:
                    (layer0, layer1, tiles)[stream](step, i if stream == 1 else i + 1)
                end_of_pass()
            for step in LAYER1:
                layer1(step, B - 1)

        @block.vector
        def _(dve):
            v = nc.vector
            steps = [0]

            def then(ins):
                steps[0] += 1
                ins.then_inc(dve_step, 1)
                dve.wait_ge(dve_step, steps[0])

            def three_parts(parts, value, rest):
                then(v.tensor_copy(parts[0], value))
                then(v.tensor_tensor(rest, value, parts[0], ALU.subtract))
                then(v.tensor_copy(parts[1], rest))
                then(v.tensor_tensor(rest, rest, parts[1], ALU.subtract))
                return v.tensor_copy(parts[2], rest)

            dve.wait_ge(ctx_loaded, 16)
            then(v.bn_stats(stat[:, 0, 0, :], ctx_tok))
            v.bn_aggr(mv[:, 0, 0, :], stat[:, 0, 0, :]).then_inc(su_dve, 1)
            dve.wait_ge(su_dve, 1)
            dve.wait_ge(su_pool, 1)
            v.tensor_scalar(ctx_nrm, ctx_tok, mv[:, 0, 0, 0:1], rstd[:, 0, 0:1],
                            ALU.subtract, ALU.mult).then_inc(su_dve, 1)
            dve.wait_ge(wa_in, 16)
            v.tensor_copy(id16[:, :], ident)
            v.tensor_copy(idb[:, :], ident)
            at = offsets(SLAB_A)["ln2_g"][0]
            v.tensor_scalar(scaled[:, :], WA[:, at:at + 4], AS, None, ALU.mult)
            dve.wait_ge(su_pe, 4)
            v.tensor_scalar(kT0, PS[:, 7, 0:P], W("bk"), None, ALU.add)
            v.tensor_scalar(vT0, PS[:, 7, P:2 * P], W("bv"), None, ALU.add)
            then(v.tensor_scalar(fold_b[:, :], PS[:, 6, 0:1], W("sa_b"), None, ALU.add))
            heads = W("head_of_row").unsqueeze(1).unsqueeze(3).broadcast_to([P, B, H0, M])
            for src, dst in ((kT0, Kb_all[:, :, :].rearrange("p b (h m) -> p b h m", m=M)),
                             (vT0, Vb_all.rearrange("p (b h m) -> p b h m", b=B, m=M))):
                last = v.tensor_tensor(dst, src.rearrange("p (b m) -> p b m", m=M).unsqueeze(2).broadcast_to(
                    [P, B, H0, M]), heads, ALU.mult)
            last.then_inc(su_dve, 1)
            dve.wait_ge(su_act, 5)
            v.tensor_reduce(ssq[:, 0:H1], sqc.rearrange("p (h d) -> p h d", d=D1), AX.X, ALU.add)\
                .then_inc(su_dve, 1)
            dve.wait_ge(su_pool, 2)
            k3 = kcn.rearrange("p (h d) -> p h d", d=D1)
            then(v.tensor_tensor(k3, PS[:, 7, :].rearrange("p (h d) -> p h d", d=D1),
                                 rn[:, 0:H1].unsqueeze(2).broadcast_to([P, H1, D1]), ALU.mult))
            v.tensor_copy(k16[:, :, 2 * D1:3 * D1], k3)
            then(v.tensor_copy(k16[:, :, 0:D1], k3))
            v.tensor_tensor(k16[:, :, D1:2 * D1], k3, k16[:, :, 0:D1], ALU.subtract).then_inc(su_dve, 1)
            dve.wait_ge(su_act, 6)
            vh = vctx.rearrange("p (h d) -> p h d", d=D1)
            for b in range(B):
                for j in range(HG):
                    v.tensor_copy(vc_all[j * M:(j + 1) * M, b, :, :], vh[b * M:(b + 1) * M, j:H1:HG, :])
            dve.wait_ge(small_in, 80)
            then(v.tensor_tensor(qks_row[:, :], W("qs_row"), W("ks_row"), ALU.mult))
            then(v.tensor_reduce(shift[:, :], qks_row[:, :], AX.X, ALU.max, apply_absolute_value=True))
            then(v.tensor_scalar(shift[:, :], shift[:, :], SIM_SCALE, -EXP_ROOM, ALU.mult, ALU.add))
            v.tensor_scalar(mbias[:, :], maskb[:, :], 1.0, MASKED, ALU.subtract, ALU.mult)
            then(v.tensor_scalar(shift[:, :], shift[:, :], 0.0, -1.0, ALU.max, ALU.mult))
            then(v.tensor_scalar(mbias[:, :], mbias[:, :], shift[:, :], None, ALU.add))
            dve.wait_ge(su_pe, 9)
            for s in range(2):
                last = v.tensor_copy(kc_all[:, s, :, :, :].rearrange("p h b m -> p (h b m)"),
                                     PS[:, 5 + s, :].bitcast(F16))
            last.then_inc(su_dve, 1)
            three_parts([b2p[:, s, :] for s in range(PARTS)], b2[:, :], b2r[:, :]).then_inc(su_dve, 1)
            dve.wait_ge(su_dve, 7)

            def end_of_pass():
                dve.wait_ge(dve_step, steps[0])
                dve.sem_clear(dve_step)
                steps[0] = 0

            def split_low(n):
                nm, c0, cols = PIECES[n]
                at = split_at[nm][0] + c0
                dve.wait_ge(high_done, n + 1)
                v.scalar_tensor_tensor(halves[:, 1, at:at + cols], W(nm)[:, c0:c0 + cols], WS,
                                       halves[:, 0, at:at + cols], ALU.mult, ALU.subtract).then_inc(low_done, 1)

            def by_tile(src):
                return [src[:, t * P:(t + 1) * P] for t in range(NT)]

            def stats(hf, src):
                for t in range(NT):
                    last = v.bn_stats(stat[:, hf, t, :], by_tile(src)[t])
                then(last)
                for t in range(NT):
                    last = v.bn_aggr(mv[:, hf, t, :], stat[:, hf, t, :])
                last.then_inc(stats_ready[hf], 1)

            def normalise(hf, b, n, src):
                dve.wait_ge(stats_ready[hf], b * LNS[hf] + n)
                dve.wait_ge(rstd_ready[hf], b * LNS[hf] + n)
                for t in range(NT):
                    last = v.tensor_scalar(nrm[:, hf, t * P:(t + 1) * P], by_tile(src)[t], mv[:, hf, t, 0:1],
                                           rstd[:, hf, t:t + 1], ALU.subtract, ALU.mult)
                last.then_inc(nrm_ready[hf], 1)

            def token_affine(hf, b, n, gain, bias, base):
                r3 = nrm[:, hf, :].rearrange("p (t f) -> p t f", f=P)
                row = [W(nm).unsqueeze(1).broadcast_to([P, NT, P]) for nm in (gain, bias)]
                dve.wait_ge(nrm_ready[hf], b * LNS[hf] + n)
                then(v.tensor_tensor(r3, r3, row[0], ALU.mult))
                then(v.tensor_tensor(r3, r3, row[1], ALU.add))
                return v.tensor_tensor(X[:, hf, :], base, nrm[:, hf, :], ALU.add)

            def add_residual(b, n, which, bias):
                dve.wait_ge(prod_psum[0], b * 3 + n)
                v.scalar_tensor_tensor(res[:, 0, :], bank(0, which), bias, feat[:, 0, :], ALU.add, ALU.add)\
                    .then_inc(res_ready[0], 1)

            def low_part(hf, dst, high, ready):
                dve.wait_ge(feat_ready[hf], ready)
                v.scalar_tensor_tensor(dst, feat[:, hf, :], AS, high, ALU.mult, ALU.subtract)\
                    .then_inc(split_ready[hf], 1)

            def pick(k, values, n, mx, top, hit):
                for t in range(NT):
                    last = v.max(mx[:, t, :], values[:, t, 0:n])
                then(last)
                then(v.tensor_copy(top[:, :, 0:k], mx[:, :, 0:k]))
                for t in range(NT):
                    last = v.match_replace(hit[:, t, 0:n + 8 - k], top[:, t, :], values[:, t, 0:n + 8 - k], PICK)
                then(last)

            def layer0(step, b):
                name, k = step if isinstance(step, tuple) else (step, 0)
                if name == "x_stats":
                    dve.wait_ge(x_loaded, 16 * (b + 1))
                    stats(0, X0)
                elif name == "x_norm":
                    normalise(0, b, 1, X0)
                elif name == "fold":
                    add_residual(b, 1, SA, fold_b[:, :])
                elif name == "fold_back":
                    dve.wait_ge(resT_psum[0], b * 4 + 1)
                    stats(0, bank(0, TR))
                elif name == "n1_norm":
                    normalise(0, b, 2, bank(0, TR))
                elif name == "scores":
                    dve.wait_ge(score_psum, b + 1)
                    s3 = PS[:, SA:SA + 2, :].rearrange("p a (g m) -> p (a g) m", m=M)
                    then(v.tensor_reduce(hmax[:, :], s3, AX.X, ALU.max))
                    v.tensor_tensor(sc.rearrange("p (g m) -> p g m", m=M), s3,
                                    hmax[:, :].unsqueeze(2).broadcast_to([P, NT * H0, M]), ALU.subtract)\
                        .then_inc(centred, 1)
                elif name == "exp0":
                    dve.wait_ge(exped, b + 1)
                    then(v.tensor_reduce(hsum[:, :], sc.rearrange("p (g m) -> p g m", m=M), AX.X, ALU.add))
                    v.reciprocal(hrec[:, :], hsum[:, :]).then_inc(rec_ready, 1)
                elif name == "probs_turn":
                    dve.wait_ge(probT_psum, b + 1)
                    v.tensor_copy(pT[:, 1, :], bank(0, SB_)).then_inc(pT1_ready, 1)
                elif name == "ca":
                    add_residual(b, 2, MM, W("mha_b"))
                elif name == "ca_back":
                    dve.wait_ge(resT_psum[0], b * 4 + 2)
                    stats(0, bank(0, TR))
                elif name == "n2_norm":
                    normalise(0, b, 3, bank(0, TR))
                elif name == "n2_turn":
                    low_part(0, xl[:, :], xh[:, :], b * 5 + 3)
                elif name == "lin2":
                    add_residual(b, 3, SA, W("lin2_b"))
                elif name == "lin2_back":
                    dve.wait_ge(resT_psum[0], b * 4 + 3)
                    stats(0, bank(0, TR))
                elif name == "n3_norm":
                    normalise(0, b, 4, bank(0, TR))
                    token_affine(0, b, 4, "ln3_g", "ln3_b", X0[:, :]).then_inc(x0_free, 1)
                elif name == "y_stats":
                    dve.wait_ge(x0_free, b + 1)
                    stats(0, X[:, 0, :])
                elif name == "y_norm":
                    normalise(0, b, 5, X[:, 0, :])
                elif name == "y_turn":
                    low_part(0, xl[:, :], xh[:, :], b * 5 + 4)
                elif name == "gate0":
                    dve.wait_ge(gate_psum[0], b + 1)
                    then(v.tensor_tensor(rt0[:, :, 0:E0], bank(0, SA)[:, 0:NT * E0].rearrange(
                        "p (t e) -> p t e", e=E0), W("gate_b").unsqueeze(1).broadcast_to([P, NT, E0]), ALU.add))
                    pick(K0, rt0, E0, mx0, top0, hit0)
                    then(v.scalar_tensor_tensor(comb0[:, :, :], hit0[:, :, 0:E0], PICK, rt0[:, :, 0:E0],
                                                ALU.is_ge, ALU.mult))
                    three_parts([part0[:, :, s, :] for s in range(PARTS)], comb0[:, :, :], hit0[:, :, 0:E0])\
                        .then_inc(comb_ready[0], 1)
                elif name == "expert":
                    dve.wait_ge(relu_ready, b * E0 + k + 1)
                    dve.wait_ge(w0_psum, b * E0 + k + 1)
                    if k >= 2:
                        dve.wait_ge(down_done, b * E0 + k - 1)
                    v.tensor_tensor(er[:, 2 + k % 2, :], bank(0, SA), er[:, k % 2, :], ALU.mult).then_inc(gated, 1)
                elif name == "moe_back":
                    dve.wait_ge(resT_psum[0], b * 4 + 4)
                    then(v.tensor_tensor(X[:, 0, :], bank(0, TR), X[:, 0, :], ALU.add))
                    stats(0, X[:, 0, :])
                elif name == "lat_norm":
                    normalise(0, b, 6, X[:, 0, :])
                elif name == "lat_turn":
                    low_part(0, latl[:, :], lath[:, :], b * 5 + 5)

            def next_residual():
                then(v.tensor_copy(X[:, 1, :], X[:, 0, :]))

            def tiles(step, b):
                name, k = step
                n = b * NT + k + 1
                q3, k3 = (qk[:, a, :].rearrange("p (h d) -> p h d", d=D1) for a in range(2))
                if name == "qk_rows":
                    dve.wait_ge(sq_ready, n)
                    v.tensor_reduce(ssq[:, :], sq.rearrange("p a (h d) -> p (a h) d", d=D1), AX.X, ALU.add)\
                        .then_inc(ssq_ready, 1)
                elif name == "l2norm":
                    dve.wait_ge(rn_ready, n)
                    for a in range(2):
                        last = v.tensor_tensor(
                            (q3, k3)[a], bank(0, (MM, SA)[a]).rearrange("p (h d) -> p h d", d=D1),
                            rn[:, a * H1:(a + 1) * H1].unsqueeze(2).broadcast_to([P, H1, D1]), ALU.mult)
                    last.then_inc(qk_used, 1)
                elif name == "halves":
                    dve.wait_ge(qk_used, n)
                    if k > 0:
                        dve.wait_ge(kB_psum, n - 1)
                    v.tensor_copy(k16[:, :, 2 * D1:3 * D1], k3)
                    v.tensor_copy(k16[:, :, 0:D1], k3)
                    then(v.tensor_tensor(q3, q3, qks_row[:, :].unsqueeze(1).broadcast_to([P, H1, D1]), ALU.mult))
                    v.tensor_tensor(k16[:, :, D1:2 * D1], k3, k16[:, :, 0:D1], ALU.subtract)
                    then(v.tensor_copy(q16[:, :, 0:D1], q3))
                    v.tensor_tensor(q16[:, :, D1:2 * D1], q3, q16[:, :, 0:D1], ALU.subtract).then_inc(low_ready, 1)
                elif name == "turn_B":
                    dve.wait_ge(kB_psum, n)
                    v.tensor_copy(kB[:, :, k * P:(k + 1) * P], bank(0, TR).bitcast(F16).rearrange(
                        "p (h k) -> p h k", k=P)).then_inc(kB_ready, 1)

            s4 = sfc[:, :, :].rearrange("p t (g s) -> p t g s", s=GS)

            def layer1(step, b):
                name, k = step if isinstance(step, tuple) else (step, 0)
                if name == "attn":
                    n = k - LAG - 1
                    if 0 <= n < NS and ATTN[n][0] == "own" and ATTN[n][1] % 2 and ATTN[n][2] == NT - 1:
                        h = ATTN[n][1]
                        dve.wait_ge(head_out, b * H1 + h + 1)
                        rec = den[h // 2 % 2]
                        then(v.reciprocal(rec, rec))
                        v.tensor_tensor(aT[:, h // 2, :], on[:, h // 2 % 2, :], rec, ALU.mult)\
                            .then_inc(pair_ready, 1)
                elif name == "wo_back":
                    dve.wait_ge(resT_psum[1], b * 2 + 1)
                    stats(1, bank(1, TR))
                elif name == "no_norm":
                    normalise(1, b, 1, bank(1, TR))
                    then(token_affine(1, b, 1, "lno_w", "lno_b", X[:, 1, :]))
                elif name == "z_stats":
                    stats(1, X[:, 1, :])
                elif name == "z_norm":
                    normalise(1, b, 2, X[:, 1, :])
                elif name == "z_turn":
                    low_part(1, zl[:, :], zh[:, :], b + 1)
                elif name == "route":
                    dve.wait_ge(sig_ready, b + 1)
                    then(v.tensor_tensor(sfc[:, :, :], scor[:, :, :], W("route_b").unsqueeze(1).broadcast_to(
                        [P, NT, E1]), ALU.add))
                    then(v.tensor_reduce(grp[:, :, 0:NG], s4, AX.X, ALU.max))
                    pick(TG, grp, NG, mx1, topg, hitg)
                elif name == "route_pick":
                    then(v.tensor_scalar(hitg[:, :, 0:NG], hitg[:, :, 0:NG], PICK, None, ALU.is_ge))
                    then(v.tensor_tensor(cand[:, :, 0:E1].rearrange("p t (g s) -> p t g s", s=GS), s4,
                                         hitg[:, :, 0:NG].unsqueeze(3).broadcast_to([P, NT, NG, GS]), ALU.mult))
                    pick(K1, cand, E1, mx1, top1, hit1)
                    then(v.scalar_tensor_tensor(comb1[:, :, :], hit1[:, :, 0:E1], PICK, scor[:, :, :],
                                                ALU.is_ge, ALU.mult))
                    then(v.tensor_reduce(csum[:, :], comb1[:, :, :], AX.X, ALU.add))
                    then(v.tensor_scalar(csum[:, :], csum[:, :], 1e-20, None, ALU.add))
                    then(v.reciprocal(csum[:, :], csum[:, :]))
                    then(v.tensor_scalar(csum[:, :], csum[:, :], ROUTE_SCALE, None, ALU.mult))
                    then(v.tensor_tensor(comb1[:, :, :], comb1[:, :, :], csum[:, :].unsqueeze(2).broadcast_to(
                        [P, NT, E1]), ALU.mult))
                    three_parts([part1[:, :, s, :] for s in range(PARTS)], comb1[:, :, :], hit1[:, :, 0:E1])\
                        .then_inc(comb_ready[1], 1)
                elif name == "ffn":
                    dve.wait_ge(silu_ready, b * PLANES + k + 1)
                    dve.wait_ge(u_psum, b * PLANES + k + 1)
                    if k >= 2:
                        dve.wait_ge(ffn_down, b * PLANES + k - 1)
                    shared = k == EP
                    ins = v.scalar_tensor_tensor(fr[:, (2 if shared else 0) + k % 2, :], bank(1, MM), DS,
                                                 fr[:, k % 2, :], ALU.mult, ALU.mult)
                    if shared:
                        ins.then_inc(act_ready, 1)
                    else:
                        ins.then_inc(u_gated, 1)
                        dve.wait_ge(u_gated, b * EP + k + 1)
                        dve.wait_ge(w1_psum, b * EP + k + 1)
                        v.tensor_tensor(fr[:, 2 + k % 2, :], bank(1, SA), fr[:, k % 2, :], ALU.mult)\
                            .then_inc(act_ready, 1)
                elif name == "ffn_back":
                    dve.wait_ge(resT_psum[1], b * 2 + 2)
                    last = isinstance(b, int) and b == B - 1
                    if last:
                        dve.wait_ge(stored, 16 * (B - 1))
                    v.tensor_tensor(Y[:, :], bank(1, TR), X[:, 1, :], ALU.add).then_inc(y_ready, 1)
                    if not last:
                        dve.wait_ge(y_ready, b + 1)
                        next_residual()

            end_of_pass()
            for n, step in enumerate(LAYER0):
                layer0(step, 0)
                if n % 2 and n // 2 < len(PIECES):
                    split_low(n // 2)
            for step in sum(TILES, []):
                tiles(step, 0)
            next_residual()
            end_of_pass()
            with dve.Fori(0, B - 1) as i:
                for stream, step in BODY:
                    (layer0, layer1, tiles)[stream](step, i if stream == 1 else i + 1)
                end_of_pass()
            for step in LAYER1:
                layer1(step, B - 1)


def kernel(**inputs):
    import ml_dtypes
    import numpy as np
    import concourse.bacc as bacc
    from concourse.bass_utils import run_bass_kernel_spmd

    a = {k: np.asarray(v) for k, v in inputs.items()}
    f32, bf16 = np.float32, ml_dtypes.bfloat16

    def col(v):
        return np.ascontiguousarray(np.asarray(v).reshape(-1, P).T)

    def chunks(m):
        return m.reshape(-1, P, m.shape[1]).transpose(1, 0, 2).reshape(P, -1)

    qkv_w, qkv_b, in_w, in_b = (a["L0_xattn_" + n] for n in ("qkv_w", "qkv_b", "in_proj_w", "in_proj_b"))
    gu = a["L1_ffn_experts_gate_up"]
    part = {
        "ident": np.eye(P, dtype=f32),
        "head_of_row": (np.arange(P)[:, None] // D0 == np.arange(H0)[None]).astype(f32),
        "sa_b": col(a["L0_xattn_sa_out_b"]), "sa_bv": col(qkv_b[2 * P:]),
        "ln1_g": col(a["L0_xattn_ln1_g"]), "ln1_b": col(a["L0_xattn_ln1_b"]),
        "bq": col(in_b[:P]), "bk": col(in_b[P:2 * P]), "bv": col(in_b[2 * P:]),
        "mha_b": col(a["L0_xattn_mha_out_b"]),
        "ln2_g": col(a["L0_xattn_ln2_g"]), "ln2_b": col(a["L0_xattn_ln2_b"]),
        "lin1_b": col(a["L0_xattn_lin1_b"]), "lin2_b": col(a["L0_xattn_lin2_b"]),
        "b1": col(a["L0_ffn_b1"]),
        "lnl_w": col(a["L1_xattn_ln_l_w"]), "lnl_b": col(a["L1_xattn_ln_l_b"]),
        "lnx_w": col(a["L1_xattn_ln_x_w"]), "lnx_b": col(a["L1_xattn_ln_x_b"]),
        "sa_wv": qkv_w[2 * P:], "sa_oT": a["L0_xattn_sa_out_w"].T,
        "wqT": in_w[:P].T, "wkT": in_w[P:2 * P].T, "wvT": in_w[2 * P:].T,
        "mha_oT": a["L0_xattn_mha_out_w"].T,
        "lin1T": a["L0_xattn_lin1_w"].T, "lin2T": chunks(a["L0_xattn_lin2_w"].T),
        "Wk": a["L1_xattn_Wkv"][:, :INNER], "Wv": a["L1_xattn_Wkv"][:, INNER:],
        "gate_w": a["L0_ffn_gate_w"],
        "w1": a["L0_ffn_w1"].transpose(1, 0, 2).reshape(P, -1), "w2": a["L0_ffn_w2"].transpose(1, 0, 2).reshape(P, -1),
        "Wq": a["L1_xattn_Wq"], "Wo": chunks(a["L1_xattn_Wo"]),
        "route_wT": a["L1_ffn_gate_weight"].T,
        "gateT": gu[:, :I1].reshape(E1 * I1, P).T, "upT": gu[:, I1:].reshape(E1 * I1, P).T,
        "downT": chunks(a["L1_ffn_experts_down"].transpose(0, 2, 1).reshape(E1 * I1, P)),
        "sh_gateT": a["L1_ffn_shared_gate_w"].T, "sh_upT": a["L1_ffn_shared_up_w"].T,
        "sh_downT": a["L1_ffn_shared_down_w"].T,
        "ln3_g": a["L0_xattn_ln3_g"], "ln3_b": a["L0_xattn_ln3_b"],
        "lno_w": a["L1_xattn_ln_o_w"], "lno_b": a["L1_xattn_ln_o_b"],
        "gate_b": a["L0_ffn_gate_b"], "route_b": a["L1_ffn_e_score_correction_bias"],
        "qs_row": a["L1_xattn_q_scale"], "ks_row": a["L1_xattn_k_scale"],
    }
    slabs = [np.concatenate([part[n] for n, _ in s], axis=1) for s in (SLAB_A, SLAB_B, SLAB_S, SLAB_G, SLAB_H)]
    sel0 = np.arange(E0)[:, None] == np.repeat(np.arange(E0), P)[None]
    sel1 = np.arange(E1)[:, None] == np.repeat(np.arange(E1), I1)[None]
    arrays = {
        "x": a["x"], "ctx": a["ctx_1024"], "mask": np.tile(a["mask_BxS2_bk0"].T, (HG, 1)),
        **dict(zip(("slab_a", "slab_b", "slab_s", "slab_g", "slab_h"), slabs)),
        "rows": np.concatenate([part[n] for n, _ in ROWS])[None], "b2": np.tile(a["L0_ffn_b2"], (PARTS, 1)),
        "sel0": np.tile(sel0, (PARTS, 1)).astype(bf16), "sel1": np.tile(sel1, (PARTS, 1)).astype(bf16),
    }
    nc = bacc.Bacc("TRN2", target_bir_lowering=False, num_devices=1)
    nc.disable_value_cache = True
    arrays = {k: np.ascontiguousarray(v) for k, v in arrays.items()}
    args = [nc.dram_tensor(k, v.shape, mybir.dt.from_np(v.dtype), kind="ExternalInput").ap()
            for k, v in arrays.items()]
    args.append(nc.dram_tensor("out", (B, S, P), F32, kind="ExternalOutput").ap())
    two_layer_kernel(nc, *args)
    return run_bass_kernel_spmd(nc, [arrays], core_ids=[0]).results[0]["out"]
```

```python
from contextlib import ExitStack

import concourse.bass as bass
from concourse import mybir

F32, F16, BF16, U8 = mybir.dt.float32, mybir.dt.float16, mybir.dt.bfloat16, mybir.dt.uint8
ALU = mybir.AluOpType
ACT = mybir.ActivationFunctionType
AX = mybir.AxisListType

P = 128
B, S, M = 4, 512, 32
NT = S // P
H0, D0 = 8, 16
FF = 512
FC = FF // P
E0, K0 = 8, 2
H1, D1 = 8, 64
INNER = H1 * D1
PAIRS = H1 // 2
HG = P // M
E1, I1 = 32, 64
EP = E1 // 2
PLANES = EP + 1
NG, TG, K1 = 8, 4, 6
GS = E1 // NG
ROUTE_SCALE = 2.5
SIM_SCALE = 8.0
EPS = 1e-5
L2_EPS = 1e-12
SENT = -3.0e38
PICK = 3.0e38
MASKED = 1.0e30
EXP_ROOM = 80.0
WS = 2.0 ** 10
AS = 2.0 ** 6
DS = 1.0 / (WS * AS)
QS = 2.0 ** 8
LNS = (6, 2)
TURNS = 5
PARTS = 3

SLAB_A = [("ident", P), ("head_of_row", H0),
          ("sa_b", 1), ("sa_bv", 1), ("ln1_g", 1), ("ln1_b", 1), ("bq", 1), ("bk", 1), ("bv", 1), ("mha_b", 1),
          ("ln2_g", 1), ("ln2_b", 1), ("lnl_w", 1), ("lnl_b", 1), ("lin1_b", FC), ("lin2_b", 1), ("b1", E0),
          ("lnx_w", 1), ("lnx_b", 1),
          ("sa_wv", P), ("sa_oT", P), ("wqT", P), ("wkT", P), ("wvT", P), ("mha_oT", P)]
SLAB_B = [("lin2T", FC * P), ("gate_w", E0), ("w2", E0 * P), ("Wo", PAIRS * P),
          ("route_wT", E1), ("downT", EP * P), ("sh_downT", P)]
SLAB_S = [("lin1T", FF), ("w1", E0 * P), ("Wk", INNER), ("Wv", INNER), ("Wq", INNER)]
SLAB_G = [("gateT", EP * P), ("upT", EP * P)]
SLAB_H = [("sh_gateT", P), ("sh_upT", P)]
ROWS = [("ln3_g", P), ("ln3_b", P), ("lno_w", P), ("lno_b", P), ("gate_b", E0), ("route_b", E1),
        ("qs_row", D1), ("ks_row", D1)]

LAYER0 = (["x_stats", "x_norm", "x_turn", "fold", "fold_back", "n1_norm", "n1_turn", "q0", "scores", "exp0",
           "probs", "probs_turn", "ca", "ca_back", "n2_norm", "n2_turn"] + [("lin1", k) for k in range(FC)] +
          ["lin2", "lin2_back", "n3_norm", "y_stats", "y_norm", "y_turn", "gate0", "comb0_turn"] +
          [("expert", e) for e in range(E0)] + ["moe_out", "moe_back", "lat_norm", "lat_turn"])
ATTN = []
for _g in range(H1 // HG):
    ATTN.append(("ctx", _g, 0))
    ATTN += [("own", _h, _kt) for _h in range(_g * HG, (_g + 1) * HG) for _kt in range(NT)]
NS = len(ATTN)
LAG = 2
TILES = [[("qk_rows", 0)], [], [("v_rows", 0), ("l2norm", 0)]]
for _k in range(1, NT):
    TILES += [[("halves", _k - 1), ("qk_rows", _k)], [("turn_A", _k - 1)],
              [("turn_B", _k - 1), ("v_rows", _k), ("l2norm", _k)]]
TILES += [[("halves", NT - 1)], [("turn_A", NT - 1)], [("turn_B", NT - 1)]]
PAIR_AT = [16, 26, 31, 36]
LAYER1 = ([("attn", n) for n in range(NS + LAG + 2)] +
          ["wo", "wo_back", "no_norm", "z_stats", "z_norm", "z_turn", "route", "route_pick", "comb1_turn"] +
          [("ffn", p) for p in range(PLANES)] + ["ffn_out", "ffn_back"])


EARLY = [0, 2, 3, 4, 5, 8, 8, 9, 10, 11, 11, 15, 16, 17, 18, 20, 21, 23, 24, 25, 26, 27, 27, 29, 30, 32, 34,
         35]
TILES_AT = [3, 3, 5, 6, 7, 8, 9, 10, 11, 12, 13, 13, 14, 16]
LATE = [("attn", NS + LAG + 1), "wo", "wo_back", "z_stats", "z_stats", "z_norm", "z_turn", "route", "route",
        "route_pick", ("ffn", 1), ("ffn", 2)]


BEHIND = {"n1_norm": [("split", 0), ("set_up", 1)], "q0": [("set_up", 2)], "probs": [("split", 1)],
          "n2_norm": [("set_up", 3)], ("lin1", 0): [("split", 2)], ("lin1", 2): [("split", 3)],
          ("lin1", 3): [("set_up", 4)], ("expert", 0): [("split", 4), ("split", 5)],
          ("expert", 1): [("split", 6)], ("expert", 2): [("split", 7)],
          ("expert", 4): [("split", 8), ("split", 9), ("split", 10)], ("expert", 6): [("set_up", 5)]}
PROLOGUE = [("set_up", 0)] + [s for step in LAYER0 for s in [step] + BEHIND.get(step, [])]


def merged():
    at = {}

    def put(after, stream, steps):
        at.setdefault(after, []).extend((stream, s) for s in steps)

    experts = LAYER0.index(("expert", 0))
    for at_attn, step in zip(EARLY, LAYER0[:experts], strict=True):
        put(("attn", at_attn), 0, [step])
    for after, step in zip(LATE, LAYER0[experts:], strict=True):
        put(after, 0, [step])
    for p, steps in zip(TILES_AT, TILES[:-1], strict=True):
        put(("ffn", p), 2, steps)
    put("ffn_back", 2, TILES[-1])
    return [s for x in LAYER1 for s in [(1, x)] + at.get(x, [])]


BODY = merged()


def width(cols):
    return sum(n for _, n in cols)


def offsets(cols):
    at, out = 0, {}
    for name, n in cols:
        out[name] = (at, n)
        at += n
    return out


def two_layer_kernel(nc, x, ctx_in, mask, slab_a, slab_b, slab_s, slab_g, slab_h, rows, b2_in, sel0_in, sel1_in,
                     out):
    with ExitStack() as stack:
        def sb(name, shape, dt=F32):
            return stack.enter_context(nc.sbuf_tensor("s_" + name, shape, dt))

        def sem(name):
            return stack.enter_context(nc.semaphore(name))

        def sem2(name):
            return [sem(f"{name}_layer{hf}") for hf in range(2)]

        X0 = sb("X0", [P, NT * P])
        X = sb("X", [P, 2, NT * P])
        Y = sb("Y", [P, NT * P])
        nrm = sb("nrm", [P, 2, NT * P])
        feat = sb("feat", [P, 2, S])
        res = sb("res", [P, 2, S])
        stat = sb("stat", [P, 2, NT, 6])
        mv = sb("mv", [P, 2, NT, 2])
        ve = sb("ve", [P, 2, NT])
        rstd = sb("rstd", [P, 2, NT])
        tmp4 = sb("tmp4", [P, NT])
        xh, xl, lath, latl, zh, zl = (sb(n, [P, S], F16) for n in ("xh", "xl", "lath", "latl", "zh", "zl"))
        soft = sb("soft", [P, 4, S])
        sc = soft[:, 0:2, :].rearrange("p a s -> p (a s)")
        pT = soft[:, 2:4, :]
        hT = soft
        hmax, hsum, hrec = (sb(n, [P, NT * H0]) for n in ("hmax", "hsum", "hrec"))
        er = sb("er", [P, 4, S])
        q0T = er[:, 3, :]
        rt0 = sb("rt0", [P, NT, 2 * E0])
        mx0, top0 = (sb(n, [P, NT, 8]) for n in ("mx0", "top0"))
        hit0 = sb("hit0", [P, NT, 2 * E0])
        comb0 = sb("comb0", [P, NT, E0])
        part0 = sb("part0", [P, NT, PARTS, E0], BF16)
        comb0T = sb("comb0T", [PARTS * E0, S], BF16)
        q16 = sb("q16", [P, H1, 2 * D1], F16)
        k16 = sb("k16", [P, H1, 2 * D1], F16)
        big = sb("big", [P, 3, H1, S], F16)
        qT, kA, kB = (big[:, k, :, :] for k in range(3))
        vt = sb("vt", [P, NT, PAIRS, 3 * D1])
        pr = sb("pr", [P, NT, S])
        qk = pr[:, 0:2, :]
        aT = sb("aT", [P, PAIRS, S])
        ssq, rn, nn = (sb(n, [P, 2 * H1]) for n in ("ssq", "rn", "nn"))
        sq = aT[:, 0:2, :]
        scor, sfc, comb1 = (sb(n, [P, NT, E1]) for n in ("scor", "sfc", "comb1"))
        grp, hitg = (sb(n, [P, NT, NG + 8]) for n in ("grp", "hitg"))
        cand, hit1 = (sb(n, [P, NT, E1 + 8]) for n in ("cand", "hit1"))
        mx1, topg, top1 = (sb(n, [P, NT, 8]) for n in ("mx1", "topg", "top1"))
        csum = sb("csum", [P, NT])
        part1 = sb("part1", [P, NT, PARTS, E1], BF16)
        comb1T = sb("comb1T", [PARTS * E1, S], BF16)
        fr = sb("fr", [P, 4, S])
        pc = fr[:, 0:2, :]
        on = fr[:, 2:4, :]
        den = [res[:, 1, :], feat[:, 1, :]]

        WA, WB = sb("WA", [P, width(SLAB_A)]), sb("WB", [P, width(SLAB_B)])
        RW = sb("RW", [P, width(ROWS)])
        WH = sb("WH", [P, width(SLAB_H)])
        halves = sb("halves", [P, 2, width(SLAB_S) + width(SLAB_G) + width(SLAB_H)], F16)
        WSP = vt[:, :, :, :].rearrange("p t a d -> p (t a d)")[:, 0:width(SLAB_S)]
        WG = big[:, :, :, :].rearrange("p k h s -> p (k h s)").bitcast(F32)[:, 0:width(SLAB_G)]
        where = {}
        for tile_, cols in ((WA, SLAB_A), (WB, SLAB_B), (RW, ROWS), (WSP, SLAB_S), (WG, SLAB_G), (WH, SLAB_H)):
            for name, (at, n) in offsets(cols).items():
                where[name] = tile_[:, at:at + n]
        split_at = offsets(SLAB_S + SLAB_G + SLAB_H)

        def W(name, k=None, n=P):
            return where[name] if k is None else where[name][:, k * n:(k + 1) * n]

        def W16(name, part, k=0, n=P):
            at = split_at[name][0] + k * n
            return halves[:, part, at:at + n]

        PIECES = [("lin1T", 0, FF), ("w1", 0, E0 * P), ("Wk", 0, INNER), ("Wv", 0, INNER), ("Wq", 0, INNER)]
        PIECES += [(nm, k * 1024, 1024) for nm in ("gateT", "upT") for k in range(EP * P // 1024)]
        PIECES += [("sh_gateT", 0, P), ("sh_upT", 0, P)]

        ident = W("ident")
        id16 = sb("id16", [P, P], F16)
        idb = sb("idb", [P, P], BF16)
        scaled = sb("scaled", [P, 4])
        b2 = sb("b2", [PARTS * E0, P])
        b2r = sb("b2r", [PARTS * E0, P])
        b2p = sb("b2p", [PARTS * E0, PARTS, P], BF16)
        sel0 = sb("sel0", [PARTS * E0, E0 * P], BF16)
        sel1 = sb("sel1", [PARTS * E1, EP * P], BF16)
        maskb = sb("maskb", [P, B], U8)

        foldT = sb("foldT", [P, P])
        fold_b = sb("fold_b", [P, 1])
        Kb_all = sb("Kb_all", [P, B, H0 * M])
        Vp_all = sb("Vp_all", [P, B, 2, P])
        Vp = sb("Vp", [P, 2, P])
        kc_all = sb("kc_all", [P, 2, H1, B, M], F16)
        kc = sb("kc", [P, 2, H1, P], F16)
        vc_all = sb("vc_all", [P, B, H1 // HG, D1])
        vc = sb("vc", [P, H1, P])
        shift = sb("shift", [P, 1])
        mbias = sb("mbias", [P, B])
        mb = sb("mb", [P, 1])
        qks_row = sb("qks_row", [P, D1])
        mhalf = sb("mhalf", [P, 2 * H1])
        eps_row = sb("eps_row", [P, NT])
        ctx_tok, memT, kT0, vT0 = (aT[:, 0, k * P:(k + 1) * P] for k in range(4))
        ctx_nrm, ctx_nT = (aT[:, 1, k * P:(k + 1) * P] for k in range(2))
        Vb_all = er[:, 0:2, :].rearrange("p a s -> p (a s)")
        sqc, vctx, kcn = fr[:, 0, :], fr[:, 1, :], fr[:, 2, :]

        PS = stack.enter_context(nc.psum_tensor("PS", [P, 8, 512], F32))
        TR, MM, SA, SB_ = 0, 1, 2, 3

        def bank(hf, which):
            return PS[:, 4 * hf + which, :]

        ctx_loaded, wa_in, ws_in, wb_in, wg_in, small_in = (sem(n) for n in (
            "ctx_loaded", "wa_in", "ws_in", "wb_in", "wg_in", "small_in"))
        x_loaded, x0_free, y_ready, stored = (sem(n) for n in ("x_loaded", "x0_free", "y_ready", "stored"))
        su_pe, su_act, su_dve, su_pool = (sem(n) for n in ("su_pe", "su_act", "su_dve", "su_pool"))
        b2_ready = sem("b2_ready")
        high_done, low_done = sem("high_done"), sem("low_done")
        dve_step, pool_step = sem("dve_step"), sem("pool_step")
        staged0, staged1 = sem("staged0"), sem("staged1")
        stats_ready, rstd_ready, nrm_ready, nrmT_psum, feat_ready, split_ready = (sem2(n) for n in (
            "stats_ready", "rstd_ready", "nrm_ready", "nrmT_psum", "feat_ready", "split_ready"))
        prod_psum, res_ready, resT_psum = (sem2(n) for n in ("prod_psum", "res_ready", "resT_psum"))
        q0_psum, q0_ready, score_psum, centred, exped, rec_ready, probs_ready, probT_psum, pT0_ready, pT1_ready = (
            sem(n) for n in ("q0_psum", "q0_ready", "score_psum", "centred", "exped", "rec_ready", "probs_ready",
                             "probT_psum", "pT0_ready", "pT1_ready"))
        lin1_psum, hid_ready = sem("lin1_psum"), sem("hid_ready")
        gate_psum, comb_ready, combT_psum, combT_ready = (sem2(n) for n in (
            "gate_psum", "comb_ready", "combT_psum", "combT_ready"))
        h_psum, w0_psum, relu_ready, gated, down_done, moe_ready = (sem(n) for n in (
            "h_psum", "w0_psum", "relu_ready", "gated", "down_done", "moe_ready"))
        qk_psum, v_psum, sq_ready, ssq_ready, rn_ready, qk_used, low_ready = (sem(n) for n in (
            "qk_psum", "v_psum", "sq_ready", "ssq_ready", "rn_ready", "qk_used", "low_ready"))
        v_ready, qT_psum, kT_psum, qT_ready, kA_ready, kB_ready = (sem(n) for n in (
            "v_ready", "qT_psum", "kT_psum", "qT_ready", "kA_ready", "kB_ready"))
        sim_psum, exp_done, pv_done, head_psum, head_out, pair_ready = (sem(n) for n in (
            "sim_psum", "exp_done", "pv_done", "head_psum", "head_out", "pair_ready"))
        wo_ready, sig_ready = sem("wo_ready"), sem("sig_ready")
        g_psum, u_psum, w1_psum, silu_ready, u_gated, act_ready, ffn_down, ffn_ready = (sem(n) for n in (
            "g_psum", "u_psum", "w1_psum", "silu_ready", "u_gated", "act_ready", "ffn_down", "ffn_ready"))

        block = stack.enter_context(nc.Block())

        @block.sync
        def _(sp):
            def batch(dram, b):
                return dram[bass.ds(b, 1)].rearrange("o (p t) f -> p (o t f)", p=P)

            sp.dma_start(ctx_tok, ctx_in.rearrange("b m f -> (b m) f")).then_inc(ctx_loaded, 16)
            sp.dma_start(WA[:, :], slab_a).then_inc(wa_in, 16)
            sp.dma_start(X0[:, :], batch(x, 0)).then_inc(x_loaded, 16)
            sp.dma_start(WSP, slab_s).then_inc(ws_in, 16)
            sp.dma_start(RW[:, :], rows[0, :].partition_broadcast(P)).then_inc(small_in, 16)
            sp.dma_start(maskb[:, :], mask).then_inc(small_in, 16)
            sp.dma_start(b2[:, :], b2_in).then_inc(small_in, 16)
            sp.dma_start(sel0[:, :], sel0_in).then_inc(small_in, 16)
            sp.dma_start(sel1[:, :], sel1_in).then_inc(small_in, 16)
            sp.dma_start(WB[:, :], slab_b).then_inc(wb_in, 16)
            sp.dma_start(WG, slab_g).then_inc(wg_in, 16)
            sp.dma_start(WH[:, :], slab_h).then_inc(wg_in, 16)
            sp.wait_ge(x0_free, 1)
            sp.dma_start(X0[:, :], batch(x, 1)).then_inc(x_loaded, 16)
            with sp.Fori(0, B - 2) as i:
                sp.wait_ge(y_ready, i + 1)
                sp.dma_start(batch(out, i), Y[:, :]).then_inc(stored, 16)
                sp.wait_ge(x0_free, i + 2)
                sp.wait_ge(stored, 16 * (i + 1))
                sp.dma_start(X0[:, :], batch(x, i + 2)).then_inc(x_loaded, 16)
            for b in (B - 2, B - 1):
                sp.wait_ge(y_ready, b + 1)
                sp.dma_start(batch(out, b), Y[:, :]).then_inc(stored, 16)
            sp.wait_ge(stored, 16 * B)

        @block.tensor
        def _(pe):
            mm = nc.tensor.matmul

            def turn(dst, src):
                for t in range(NT):
                    last = nc.tensor.transpose(dst[:, t * P:(t + 1) * P], src[:, t * P:(t + 1) * P], ident)
                return last

            def mm3(dst, stat_parts, mov_parts, start=True, stop=True):
                mm(dst, stat_parts[0], mov_parts[0], start=start, stop=False)
                mm(dst, stat_parts[0], mov_parts[1], start=False, stop=False)
                return mm(dst, stat_parts[1], mov_parts[0], start=False, stop=stop)

            def set_up(part):
                if part == 0:
                    pe.wait_ge(ctx_loaded, 16)
                    pe.wait_ge(wa_in, 16)
                    nc.tensor.transpose(PS[:, 4, 0:P], ctx_tok, ident).then_inc(su_pe, 1)
                    mm(PS[:, 5, 0:P], W("sa_wv"), W("sa_oT"), start=True, stop=True).then_inc(su_pe, 1)
                    mm(PS[:, 6, 0:1], W("sa_oT"), W("sa_bv"), start=True, stop=True).then_inc(su_pe, 1)
                    pe.wait_ge(su_act, 1)
                    mm(PS[:, 7, 0:P], W("wkT"), memT, start=True, stop=True)
                    mm(PS[:, 7, P:2 * P], W("wvT"), memT, start=True, stop=True).then_inc(su_pe, 1)
                    pe.wait_ge(su_dve, 2)
                    nc.tensor.transpose(PS[:, 4, 0:P], ctx_nrm, ident).then_inc(su_pe, 1)
                elif part == 2:
                    pe.wait_ge(su_dve, 3)
                    pe.wait_ge(su_act, 2)
                    for k in range(2 * B):
                        last = mm(PS[:, 5 + k // 4, k % 4 * P:(k % 4 + 1) * P], Vb_all[:, k * P:(k + 1) * P],
                                  W("mha_oT"), start=True, stop=True)
                    last.then_inc(su_pe, 1)
                elif part == 3:
                    pe.wait_ge(ws_in, 16)
                    pe.wait_ge(su_act, 3)
                    mm(PS[:, 7, :], ctx_nT, W("Wk"), start=True, stop=True).then_inc(su_pe, 1)
                    mm(PS[:, 4, :], ctx_nT, W("Wv"), start=True, stop=True).then_inc(su_pe, 1)
                elif part == 4:
                    pe.wait_ge(small_in, 80)
                elif part == 5:
                    pe.wait_ge(su_dve, 5)
                    pe.wait_ge(su_act, 4)
                    dst = PS[:, 5, :].bitcast(F16).rearrange("p (h k) -> p h k", k=P)
                    for h in range(H1):
                        last = nc.tensor.transpose(dst[:, h, :], k16[:, h, :], id16[:, :])
                    last.then_inc(su_pe, 1)

            def layer0(step, b):
                name, k = step if isinstance(step, tuple) else (step, 0)

                def tokens_to_features(n, dst):
                    pe.wait_ge(nrm_ready[0], b * TURNS + n)
                    turn(bank(0, dst), nrm[:, 0, :]).then_inc(nrmT_psum[0], 1)

                def features_to_tokens(n):
                    pe.wait_ge(res_ready[0], b * 3 + n)
                    turn(bank(0, TR), res[:, 0, :]).then_inc(resT_psum[0], 1)

                if name == "x_turn":
                    tokens_to_features(1, MM)
                elif name == "fold":
                    pe.wait_ge(feat_ready[0], b * TURNS + 1)
                    pe.wait_ge(su_act, 2)
                    mm(bank(0, SA), foldT[:, :], feat[:, 0, :], start=True, stop=True).then_inc(prod_psum[0], 1)
                elif name == "fold_back":
                    features_to_tokens(1)
                elif name == "n1_turn":
                    tokens_to_features(2, MM)
                elif name == "q0":
                    pe.wait_ge(feat_ready[0], b * TURNS + 2)
                    mm(bank(0, SA), W("wqT"), feat[:, 0, :], start=True, stop=True).then_inc(q0_psum, 1)
                elif name == "scores":
                    pe.wait_ge(q0_ready, b + 1)
                    for t in range(NT):
                        last = mm(PS[:, SA + t // 2, (t % 2) * 256:(t % 2) * 256 + 256], q0T[:, t * P:(t + 1) * P],
                                  Kb_all[:, bass.ds(b, 1), :].rearrange("p o n -> p (o n)"), start=True, stop=True)
                    last.then_inc(score_psum, 1)
                elif name == "probs_turn":
                    pe.wait_ge(probs_ready, b + 1)
                    for half in range(2):
                        for t in range(NT):
                            at = t * H0 * M + half * P
                            last = nc.tensor.transpose(bank(0, SA + half)[:, t * P:(t + 1) * P], sc[:, at:at + P],
                                                       ident)
                    last.then_inc(probT_psum, 1)
                elif name == "ca":
                    pe.wait_ge(pT0_ready, b + 1)
                    pe.wait_ge(staged0, b + 1)
                    mm(bank(0, MM), Vp[:, 0, :], pT[:, 0, :], start=True, stop=False)
                    pe.wait_ge(pT1_ready, b + 1)
                    mm(bank(0, MM), Vp[:, 1, :], pT[:, 1, :], start=False, stop=True).then_inc(prod_psum[0], 1)
                elif name == "ca_back":
                    features_to_tokens(2)
                elif name == "n2_turn":
                    tokens_to_features(3, MM)
                elif name == "lin1":
                    if k == 0:
                        pe.wait_ge(split_ready[0], b * 3 + 1)
                        pe.wait_ge(low_done, 1)
                    mm3(bank(0, (SA, SB_, TR, MM)[k]), [W16("lin1T", s, k) for s in range(2)],
                        [xh[:, :], xl[:, :]]).then_inc(lin1_psum, 1)
                elif name == "lin2":
                    pe.wait_ge(wb_in, 16)
                    for j in range(FC):
                        pe.wait_ge(hid_ready, b * FC + j + 1)
                        last = mm(bank(0, SA), W("lin2T", j), hT[:, j, :], start=(j == 0), stop=(j == FC - 1))
                    last.then_inc(prod_psum[0], 1)
                elif name == "lin2_back":
                    features_to_tokens(3)
                elif name == "y_turn":
                    tokens_to_features(4, MM)
                elif name == "gate0":
                    pe.wait_ge(feat_ready[0], b * TURNS + 4)
                    for t in range(NT):
                        last = mm(bank(0, SA)[:, t * E0:(t + 1) * E0], feat[:, 0, t * P:(t + 1) * P], W("gate_w"),
                                  start=True, stop=True)
                    last.then_inc(gate_psum[0], 1)
                elif name == "comb0_turn":
                    pe.wait_ge(comb_ready[0], b + 1)
                    dst = bank(0, SB_).bitcast(BF16)
                    for t in range(NT):
                        last = nc.tensor.transpose(dst[0:PARTS * E0, t * P:(t + 1) * P],
                                                   part0[:, t, :, :].rearrange("p k e -> p (k e)"), idb[:, :])
                    last.then_inc(combT_psum[0], 1)
                elif name in ("expert", "moe_out"):
                    e = k if name == "expert" else E0
                    if e < E0:
                        if e == 0:
                            pe.wait_ge(split_ready[0], b * 3 + 2)
                            pe.wait_ge(low_done, 2)
                        if e >= 2:
                            pe.wait_ge(relu_ready, b * E0 + e - 1)
                        mm3(bank(0, (TR, MM)[e % 2]), [W16("w1", s, e) for s in range(2)],
                            [xh[:, :], xl[:, :]]).then_inc(h_psum, 1)
                    if e == 0:
                        pe.wait_ge(combT_ready[0], b + 1)
                        pe.wait_ge(b2_ready, 1)
                        for s in range(PARTS):
                            mm(bank(0, SB_), b2p[:, s, :], comb0T[:, :], start=(s == 0), stop=False)
                    else:
                        pe.wait_ge(gated, b * E0 + e)
                        mm(bank(0, SB_), W("w2", e - 1), er[:, 2 + (e - 1) % 2, :], start=False, stop=(e == E0))\
                            .then_inc(down_done, 1)
                    if e < E0:
                        mm(bank(0, SA), sel0[:, e * P:(e + 1) * P], comb0T[:, :], start=True, stop=True)\
                            .then_inc(w0_psum, 1)
                elif name == "moe_back":
                    pe.wait_ge(moe_ready, b + 1)
                    turn(bank(0, TR), res[:, 0, :]).then_inc(resT_psum[0], 1)
                elif name == "lat_turn":
                    tokens_to_features(5, MM)

            def tiles(step, b):
                name, k = step
                n = b * NT + k + 1
                lat = [z[:, k * P:(k + 1) * P] for z in (lath, latl)]

                def turn16(which, src):
                    dst = bank(0, which).bitcast(F16).rearrange("p (h k) -> p h k", k=P)
                    for h in range(H1):
                        last = nc.tensor.transpose(dst[:, h, :], src[:, h, :], id16[:, :])
                    return last

                if name == "qk_rows":
                    if k == 0:
                        pe.wait_ge(split_ready[0], b * 3 + 3)
                        pe.wait_ge(low_done, len(PIECES))
                    else:
                        pe.wait_ge(qk_used, n - 1)
                    mm3(bank(0, MM), lat, [W16("Wq", s, 0, INNER) for s in range(2)])\
                        .then_inc(qk_psum, 1)
                    mm3(bank(0, SA), lat, [W16("Wk", s, 0, INNER) for s in range(2)]).then_inc(qk_psum, 1)
                elif name == "v_rows":
                    if k > 0:
                        pe.wait_ge(kA_ready, n - 1)
                    mm3(bank(0, SB_), lat, [W16("Wv", s, 0, INNER) for s in range(2)]).then_inc(v_psum, 1)
                elif name == "turn_A":
                    pe.wait_ge(low_ready, n)
                    if k > 0:
                        pe.wait_ge(qT_ready, n - 1)
                    turn16(TR, q16).then_inc(qT_psum, 1)
                    pe.wait_ge(v_ready, n)
                    turn16(SB_, k16).then_inc(kT_psum, 1)

            def layer1(step, b):
                name, k = step if isinstance(step, tuple) else (step, 0)

                def values(n):
                    kind, h, kt = ATTN[n]
                    pe.wait_ge(exp_done, b * NS + n + 1)
                    if kind == "ctx":
                        return
                    if kt == 0 and h >= 2:
                        pe.wait_ge(head_out, b * H1 + h - 1)
                    mm(bank(1, SA + h % 2), vt[:, kt, h // 2, D1 * (h % 2):D1 * (h % 2) + P], pr[:, kt, :],
                       start=(kt == 0), stop=False).then_inc(pv_done, 1)
                    if kt == NT - 1:
                        mm(bank(1, SA + h % 2), vc[:, h, :], pc[:, h // HG, :], start=False, stop=True)\
                            .then_inc(head_psum, 1)

                if name == "attn":
                    if k == 0:
                        pe.wait_ge(qT_ready, b * NT + NT)
                        pe.wait_ge(kA_ready, b * NT + NT)
                        pe.wait_ge(kB_ready, b * NT + NT)
                        pe.wait_ge(staged1, b + 1)
                    if LAG <= k < NS + LAG:
                        values(k - LAG)
                    if k < NS:
                        kind, h, kt = ATTN[k]
                        dst = bank(1, (TR, MM)[k % 2])
                        if kind == "ctx":
                            for j in range(HG):
                                for s in range(2):
                                    last = mm(dst, kc[:, s, h * HG + j, :], qT[:, h * HG + j, :],
                                              start=(j + s == 0), stop=(j + s == HG))
                        else:
                            mm(dst, kA[:, h, kt * P:(kt + 1) * P], qT[:, h, :], start=True, stop=False)
                            last = mm(dst, kB[:, h, kt * P:(kt + 1) * P], qT[:, h, :], start=False, stop=True)
                        last.then_inc(sim_psum, 1)
                elif name == "wo":
                    for q in range(PAIRS):
                        if q >= PAIRS - 2:
                            pe.wait_ge(pair_ready, b * PAIRS + q + 1)
                        last = mm(bank(1, MM), W("Wo", q), aT[:, q, :], start=(q == 0), stop=(q == PAIRS - 1))
                    last.then_inc(prod_psum[1], 1)
                elif name == "wo_back":
                    pe.wait_ge(wo_ready, b + 1)
                    turn(bank(1, TR), res[:, 1, :]).then_inc(resT_psum[1], 1)
                elif name == "z_turn":
                    pe.wait_ge(nrm_ready[1], b + 1)
                    turn(bank(1, MM), nrm[:, 1, :]).then_inc(nrmT_psum[1], 1)
                elif name == "route":
                    pe.wait_ge(feat_ready[1], b + 1)
                    for t in range(NT):
                        last = mm(bank(1, SA)[:, t * E1:(t + 1) * E1], feat[:, 1, t * P:(t + 1) * P], W("route_wT"),
                                  start=True, stop=True)
                    last.then_inc(gate_psum[1], 1)
                elif name == "comb1_turn":
                    pe.wait_ge(comb_ready[1], b + 1)
                    dst = bank(1, SB_).bitcast(BF16)
                    for t in range(NT):
                        last = nc.tensor.transpose(dst[0:PARTS * E1, t * P:(t + 1) * P],
                                                   part1[:, t, :, :].rearrange("p k e -> p (k e)"), idb[:, :])
                    last.then_inc(combT_psum[1], 1)
                elif name in ("ffn", "ffn_out"):
                    p = k if name == "ffn" else PLANES
                    if p < PLANES:
                        if p == 0:
                            pe.wait_ge(split_ready[1], b + 1)
                        else:
                            pe.wait_ge(silu_ready, b * PLANES + p)
                        src = [W16("gateT" if p < EP else "sh_gateT", s, p % EP) for s in range(2)]
                        mm3(bank(1, TR), src, [zh[:, :], zl[:, :]]).then_inc(g_psum, 1)
                        if p >= 1:
                            pe.wait_ge(u_gated, b * EP + p)
                        src = [W16("upT" if p < EP else "sh_upT", s, p % EP) for s in range(2)]
                        mm3(bank(1, MM), src, [zh[:, :], zl[:, :]]).then_inc(u_psum, 1)
                    if p == 0:
                        pe.wait_ge(combT_ready[1], b + 1)
                    else:
                        pe.wait_ge(act_ready, b * PLANES + p)
                        mm(bank(1, SB_), W("downT", p - 1) if p <= EP else W("sh_downT"),
                           fr[:, 2 + (p - 1) % 2, :], start=(p == 1), stop=(p == PLANES)).then_inc(ffn_down, 1)
                    if p < EP:
                        mm(bank(1, SA), sel1[:, p * P:(p + 1) * P], comb1T[:, :], start=True, stop=True)\
                            .then_inc(w1_psum, 1)
                elif name == "ffn_back":
                    pe.wait_ge(ffn_ready, b + 1)
                    turn(bank(1, TR), res[:, 1, :]).then_inc(resT_psum[1], 1)

            for step in PROLOGUE:
                if step[0] == "set_up":
                    set_up(step[1])
                elif step[0] != "split":
                    layer0(step, 0)
            for step in sum(TILES, []):
                tiles(step, 0)
            with pe.Fori(0, B - 1) as i:
                for stream, step in BODY:
                    (layer0, layer1, tiles)[stream](step, i if stream == 1 else i + 1)
            for step in LAYER1:
                layer1(step, B - 1)

        @block.scalar
        def _(act):
            def copy(dst, src, scale=1.0):
                return nc.scalar.activation(dst, src, ACT.Copy, scale=scale)

            def affine(dst, src, scale, bias):
                return nc.scalar.activation(dst, src, ACT.Identity, bias=bias, scale=scale)

            def set_up(part):
                if part == 0:
                    act.wait_ge(su_pe, 1)
                    copy(memT, PS[:, 4, 0:P]).then_inc(su_act, 1)
                    act.wait_ge(su_pe, 2)
                    copy(foldT[:, :], PS[:, 5, 0:P]).then_inc(su_act, 1)
                    act.wait_ge(su_pe, 5)
                    affine(ctx_nT, PS[:, 4, 0:P], W("lnx_w"), W("lnx_b")).then_inc(su_act, 1)
                elif part == 2:
                    act.wait_ge(su_pe, 6)
                    copy(Vp_all[:, :, :, :].rearrange("p b h c -> p (b h) c"),
                         PS[:, 5:7, :].rearrange("p a (h c) -> p (a h) c", c=P)).then_inc(su_act, 1)
                elif part == 3:
                    act.wait_ge(su_pe, 7)
                    nc.scalar.activation(sqc, PS[:, 7, :], ACT.Square).then_inc(su_act, 1)
                    act.wait_ge(su_pe, 8)
                    copy(vctx, PS[:, 4, :]).then_inc(su_act, 1)

            def split_high(n):
                nm, c0, cols = PIECES[n]
                if nm in dict(SLAB_G) or nm in dict(SLAB_H):
                    act.wait_ge(wg_in, 32)
                else:
                    act.wait_ge(ws_in, 16)
                at = split_at[nm][0] + c0
                copy(halves[:, 0, at:at + cols], W(nm)[:, c0:c0 + cols], WS).then_inc(high_done, 1)

            def layer0(step, b):
                name, k = step if isinstance(step, tuple) else (step, 0)

                def features_out(n, scale=None, bias=None, scaled_at=None, high=None):
                    act.wait_ge(nrmT_psum[0], b * TURNS + n)
                    src, dst = bank(0, MM), feat[:, 0, :]
                    last = copy(dst, src) if scale is None else affine(dst, src, scale, bias)
                    if high is not None:
                        last = copy(high, src, AS) if scale is None else \
                            affine(high, src, scaled[:, scaled_at:scaled_at + 1],
                                   scaled[:, scaled_at + 1:scaled_at + 2])
                    last.then_inc(feat_ready[0], 1)

                if name == "x_turn":
                    features_out(1)
                elif name == "n1_turn":
                    features_out(2, W("ln1_g"), W("ln1_b"))
                elif name == "q0":
                    act.wait_ge(q0_psum, b + 1)
                    affine(q0T[:, :], bank(0, SA), 1.0, W("bq")).then_inc(q0_ready, 1)
                elif name == "exp0":
                    act.wait_ge(centred, b + 1)
                    nc.scalar.activation(sc, sc, ACT.Exp, scale=float(D0) ** -0.5).then_inc(exped, 1)
                elif name == "probs_turn":
                    act.wait_ge(probT_psum, b + 1)
                    copy(pT[:, 0, :], bank(0, SA)).then_inc(pT0_ready, 1)
                elif name == "n2_turn":
                    features_out(3, W("ln2_g"), W("ln2_b"), 0, xh[:, :])
                elif name == "lin1":
                    act.wait_ge(lin1_psum, b * FC + k + 1)
                    nc.scalar.activation(hT[:, k, :], bank(0, (SA, SB_, TR, MM)[k]), ACT.Relu,
                                         bias=W("lin1_b")[:, k:k + 1], scale=DS).then_inc(hid_ready, 1)
                elif name == "y_turn":
                    features_out(4, high=xh[:, :])
                elif name == "comb0_turn":
                    act.wait_ge(combT_psum[0], b + 1)
                    copy(comb0T[:, :], bank(0, SB_).bitcast(BF16)[0:PARTS * E0, 0:S]).then_inc(combT_ready[0], 1)
                elif name == "expert":
                    act.wait_ge(h_psum, b * E0 + k + 1)
                    if k >= 2:
                        act.wait_ge(gated, b * E0 + k - 1)
                    nc.scalar.activation(er[:, k % 2, :], bank(0, (TR, MM)[k % 2]), ACT.Relu,
                                         bias=W("b1")[:, k:k + 1], scale=DS).then_inc(relu_ready, 1)
                elif name == "moe_out":
                    act.wait_ge(down_done, b * E0 + E0)
                    copy(res[:, 0, :], bank(0, SB_)).then_inc(moe_ready, 1)
                elif name == "lat_turn":
                    features_out(5, W("lnl_w"), W("lnl_b"), 2, lath[:, :])

            def tiles(step, b):
                name, k = step
                n = b * NT + k + 1
                at = slice(k * P, (k + 1) * P)
                if name == "qk_rows":
                    if k > 0:
                        act.wait_ge(ssq_ready, 2 * (n - 1))
                    for a in range(2):
                        act.wait_ge(qk_psum, 2 * (n - 1) + a + 1)
                        nc.scalar.activation(sq[:, a, :], bank(0, (MM, SA)[a]), ACT.Square).then_inc(sq_ready, 1)
                elif name == "v_rows":
                    act.wait_ge(v_psum, n)
                    v4 = bank(0, SB_).rearrange("p (a h d) -> p a h d", h=2, d=D1)
                    for hh in range(2):
                        last = copy(vt[:, k, :, 2 * hh * D1:(2 * hh + 1) * D1], v4[:, :, hh, :], DS)
                    last.then_inc(v_ready, 1)
                elif name == "turn_A":
                    act.wait_ge(kT_psum, n)
                    copy(kA[:, :, at], bank(0, SB_).bitcast(F16).rearrange("p (h k) -> p h k", k=P))\
                        .then_inc(kA_ready, 1)

            def layer1(step, b):
                name, k = step if isinstance(step, tuple) else (step, 0)
                if name == "attn":
                    if k < NS:
                        kind, h, kt = ATTN[k]
                        act.wait_ge(sim_psum, b * NS + k + 1)
                        src = bank(1, (TR, MM)[k % 2])
                        scale = SIM_SCALE / (QS * QS)
                        if kind == "ctx":
                            nc.scalar.activation(pc[:, h, :], src, ACT.Exp, bias=mb[:, :], scale=scale)\
                                .then_inc(exp_done, 1)
                        else:
                            if h > 0:
                                act.wait_ge(pv_done, b * H1 * NT + (h - 1) * NT + kt + 1)
                            nc.scalar.activation(pr[:, kt, :], src, ACT.Exp, bias=shift[:, :], scale=scale)\
                                .then_inc(exp_done, 1)
                    if k >= LAG and k - LAG < NS:
                        kind, h, kt = ATTN[k - LAG]
                        if kind == "own" and kt == NT - 1:
                            act.wait_ge(head_psum, b * H1 + h + 1)
                            if h >= 4:
                                act.wait_ge(pair_ready, b * PAIRS + h // 2 - 1)
                            own, other = (slice(D1 * j, D1 * j + D1) for j in (h % 2, 1 - h % 2))
                            copy(den[h // 2 % 2][own, :], bank(1, SA + h % 2)[other, :])
                            copy(on[own, h // 2 % 2, :], bank(1, SA + h % 2)[own, :]).then_inc(head_out, 1)
                elif name == "wo":
                    act.wait_ge(prod_psum[1], b + 1)
                    copy(res[:, 1, :], bank(1, MM)).then_inc(wo_ready, 1)
                elif name == "z_turn":
                    act.wait_ge(nrmT_psum[1], b + 1)
                    copy(feat[:, 1, :], bank(1, MM))
                    copy(zh[:, :], bank(1, MM), AS).then_inc(feat_ready[1], 1)
                elif name == "route":
                    act.wait_ge(gate_psum[1], b + 1)
                    nc.scalar.activation(scor[:, :, :], bank(1, SA)[:, 0:NT * E1].rearrange(
                        "p (t e) -> p t e", e=E1), ACT.Sigmoid).then_inc(sig_ready, 1)
                elif name == "comb1_turn":
                    act.wait_ge(combT_psum[1], b + 1)
                    copy(comb1T[:, :], bank(1, SB_).bitcast(BF16)[0:PARTS * E1, 0:S]).then_inc(combT_ready[1], 1)
                elif name == "ffn":
                    act.wait_ge(g_psum, b * PLANES + k + 1)
                    if k >= 2:
                        act.wait_ge(act_ready, b * PLANES + k - 1)
                    nc.scalar.activation(fr[:, k % 2, :], bank(1, TR), ACT.Silu, scale=DS).then_inc(silu_ready, 1)
                elif name == "ffn_out":
                    act.wait_ge(ffn_down, b * PLANES + PLANES)
                    copy(res[:, 1, :], bank(1, SB_)).then_inc(ffn_ready, 1)

            for step in PROLOGUE:
                if step[0] == "set_up":
                    set_up(step[1])
                elif step[0] == "split":
                    split_high(step[1])
                else:
                    layer0(step, 0)
            for step in sum(TILES, []):
                tiles(step, 0)
            with act.Fori(0, B - 1) as i:
                for stream, step in BODY:
                    (layer0, layer1, tiles)[stream](step, i if stream == 1 else i + 1)
            for step in LAYER1:
                layer1(step, B - 1)

        @block.gpsimd
        def _(pool):
            g = nc.gpsimd
            steps = [0]

            def then(ins):
                steps[0] += 1
                ins.then_inc(pool_step, 1)
                pool.wait_ge(pool_step, steps[0])

            def set_up(part):
                if part == 0:
                    g.memset(mhalf[:, :], -0.5)
                    then(g.memset(eps_row[:, :], EPS))
                    pool.wait_ge(su_dve, 1)
                    then(g.tensor_scalar(ve[:, 1, 0:1], mv[:, 1, 0, 1:2], EPS, None, ALU.add))
                    g.tensor_tensor(rstd[:, 1, 0:1], ve[:, 1, 0:1], mhalf[:, 0:1], ALU.pow)\
                        .then_inc(su_pool, 1)
                elif part == 1:
                    for tile_ in (rt0, top0, grp, topg, cand, top1):
                        g.memset(tile_[:, :, :], SENT)
                elif part == 2:
                    g.memset(kc[:, :, :, :], 0.0)
                    then(g.memset(vc[:, :, :], 0.0))
                    for j in range(HG):
                        r = D1 * (1 - j % 2)
                        then(g.memset(vc[j * M:(j + 1) * M, j:H1:HG, r:r + D1], 1.0))
                elif part == 3:
                    pool.wait_ge(su_dve, 4)
                    then(g.tensor_tensor(nn[:, 0:H1], ssq[:, 0:H1], mhalf[:, 0:H1], ALU.pow))
                    g.tensor_scalar(rn[:, 0:H1], nn[:, 0:H1], 1.0 / L2_EPS, QS, ALU.min, ALU.mult)\
                        .then_inc(su_pool, 1)
                elif part == 5:
                    pool.wait_ge(su_dve, 6)

            def rsqrt_var(hf, b, n, twice=False):
                pool.wait_ge(stats_ready[hf], b * LNS[hf] + n)
                var = mv[:, hf, :, 1]
                then(g.tensor_tensor(ve[:, hf, :], var, eps_row[:, :], ALU.add))
                ins = g.tensor_tensor(rstd[:, hf, :], ve[:, hf, :], mhalf[:, 0:NT], ALU.pow)
                if twice:
                    then(ins)
                    then(g.tensor_tensor(tmp4[:, :], rstd[:, hf, :], rstd[:, hf, :], ALU.mult))
                    then(g.tensor_tensor(tmp4[:, :], tmp4[:, :], var, ALU.mult))
                    then(g.tensor_tensor(tmp4[:, :], tmp4[:, :], eps_row[:, :], ALU.add))
                    then(g.tensor_tensor(ve[:, hf, :], tmp4[:, :], mhalf[:, 0:NT], ALU.pow))
                    ins = g.tensor_tensor(rstd[:, hf, :], rstd[:, hf, :], ve[:, hf, :], ALU.mult)
                ins.then_inc(rstd_ready[hf], 1)

            def layer0(step, b):
                norms = {"x_stats": 1, "fold_back": 2, "ca_back": 3, "lin2_back": 4, "y_stats": 5, "moe_back": 6}
                if step in norms:
                    rsqrt_var(0, b, norms[step], twice=(step == "moe_back"))
                elif step == "exp0":
                    if isinstance(b, int):
                        pool.wait_ge(su_act, 4)
                    g.tensor_copy(Vp[:, :, :].rearrange("p h f -> p (h f)").unsqueeze(1),
                                  Vp_all[:, bass.ds(b, 1), :, :].rearrange("p o h f -> p o (h f)"))\
                        .then_inc(staged0, 1)
                elif step == "probs":
                    pool.wait_ge(rec_ready, b + 1)
                    p3 = sc.rearrange("p (g m) -> p g m", m=M)
                    g.tensor_tensor(p3, p3, hrec[:, :].unsqueeze(2).broadcast_to([P, NT * H0, M]), ALU.mult)\
                        .then_inc(probs_ready, 1)

            def tiles(step, b):
                name, k = step
                if name == "qk_rows":
                    for a in range(2):
                        half = slice(a * H1, (a + 1) * H1)
                        pool.wait_ge(ssq_ready, 2 * (b * NT + k) + a + 1)
                        then(g.tensor_tensor(nn[:, half], ssq[:, half], mhalf[:, half], ALU.pow))
                        g.tensor_scalar(rn[:, half], nn[:, half], DS / L2_EPS, QS, ALU.min, ALU.mult)\
                            .then_inc(rn_ready, 1)
                    then(g.tensor_copy(kc[:, :, k:H1:HG, k * M:(k + 1) * M].rearrange("p s g m -> p (s g) m")
                                       .unsqueeze(2),
                                       kc_all[:, :, k:H1:HG, bass.ds(b, 1), :].rearrange("p s g o m -> p (s g) o m")))
                    r = D1 * (k % 2)
                    then(g.tensor_copy(vc[k * M:(k + 1) * M, k:H1:HG, r:r + D1].unsqueeze(1),
                                       vc_all[k * M:(k + 1) * M, bass.ds(b, 1), :, :]))
                    if k == NT - 1:
                        g.tensor_copy(mb[:, :], mbias[:, bass.ds(b, 1)]).then_inc(staged1, 1)

            def layer1(step, b):
                name, k = step if isinstance(step, tuple) else (step, 0)
                if name == "wo_back":
                    rsqrt_var(1, b, 1)
                elif name == "z_stats":
                    rsqrt_var(1, b, 2)

            def end_of_pass():
                pool.wait_ge(pool_step, steps[0])
                pool.sem_clear(pool_step)
                steps[0] = 0

            for step in PROLOGUE:
                if step[0] == "set_up":
                    set_up(step[1])
                elif step[0] != "split":
                    layer0(step, 0)
            pool.wait_ge(low_done, len(PIECES))
            then(g.memset(vt[:, :, :, D1:2 * D1].rearrange("p t a d -> p (t a) d"), 1.0))
            for step in sum(TILES, []):
                tiles(step, 0)
            end_of_pass()
            with pool.Fori(0, B - 1) as i:
                for stream, step in BODY:
                    (layer0, layer1, tiles)[stream](step, i if stream == 1 else i + 1)
                end_of_pass()
            for step in LAYER1:
                layer1(step, B - 1)

        @block.vector
        def _(dve):
            v = nc.vector
            steps = [0]

            def then(ins):
                steps[0] += 1
                ins.then_inc(dve_step, 1)
                dve.wait_ge(dve_step, steps[0])

            def swap_halves(dst, src):
                v.tensor_copy(dst[0:D1], src[D1:P])
                return v.tensor_copy(dst[D1:P], src[0:D1])

            def three_parts(parts, value, rest):
                then(v.tensor_copy(parts[0], value))
                then(v.tensor_tensor(rest, value, parts[0], ALU.subtract))
                then(v.tensor_copy(parts[1], rest))
                then(v.tensor_tensor(rest, rest, parts[1], ALU.subtract))
                return v.tensor_copy(parts[2], rest)

            def set_up(part):
                if part == 0:
                    dve.wait_ge(ctx_loaded, 16)
                    then(v.bn_stats(stat[:, 1, 0, :], ctx_tok))
                    v.bn_aggr(mv[:, 1, 0, :], stat[:, 1, 0, :]).then_inc(su_dve, 1)
                    dve.wait_ge(su_dve, 1)
                    dve.wait_ge(su_pool, 1)
                    v.tensor_scalar(ctx_nrm, ctx_tok, mv[:, 1, 0, 0:1], rstd[:, 1, 0:1],
                                    ALU.subtract, ALU.mult).then_inc(su_dve, 1)
                    dve.wait_ge(wa_in, 16)
                    v.tensor_copy(id16[:, :], ident)
                    v.tensor_copy(idb[:, :], ident)
                    at = offsets(SLAB_A)["ln2_g"][0]
                    v.tensor_scalar(scaled[:, :], WA[:, at:at + 4], AS, None, ALU.mult)
                    dve.wait_ge(su_pe, 3)
                    then(v.tensor_scalar(fold_b[:, :], PS[:, 6, 0:1], W("sa_b"), None, ALU.add))
                elif part == 1:
                    dve.wait_ge(su_pe, 4)
                    v.tensor_scalar(kT0, PS[:, 7, 0:P], W("bk"), None, ALU.add)
                    then(v.tensor_scalar(vT0, PS[:, 7, P:2 * P], W("bv"), None, ALU.add))
                    heads = W("head_of_row").unsqueeze(1).unsqueeze(3).broadcast_to([P, B, H0, M])
                    for src, dst in ((kT0, Kb_all[:, :, :].rearrange("p b (h m) -> p b h m", m=M)),
                                     (vT0, Vb_all.rearrange("p (b h m) -> p b h m", b=B, m=M))):
                        last = v.tensor_tensor(dst, src.rearrange("p (b m) -> p b m", m=M).unsqueeze(2).broadcast_to(
                            [P, B, H0, M]), heads, ALU.mult)
                    last.then_inc(su_dve, 1)
                elif part == 3:
                    dve.wait_ge(su_act, 5)
                    v.tensor_reduce(ssq[:, 0:H1], sqc.rearrange("p (h d) -> p h d", d=D1), AX.X, ALU.add)\
                        .then_inc(su_dve, 1)
                elif part == 4:
                    dve.wait_ge(su_pool, 2)
                    k3 = kcn.rearrange("p (h d) -> p h d", d=D1)
                    then(v.tensor_tensor(k3, PS[:, 7, :].rearrange("p (h d) -> p h d", d=D1),
                                         rn[:, 0:H1].unsqueeze(2).broadcast_to([P, H1, D1]), ALU.mult))
                    then(v.tensor_copy(k16[:, :, 0:D1], k3))
                    v.tensor_tensor(k16[:, :, D1:2 * D1], k3, k16[:, :, 0:D1], ALU.subtract).then_inc(su_dve, 1)
                    dve.wait_ge(su_act, 6)
                    vh = vctx.rearrange("p (h d) -> p h d", d=D1)
                    for b in range(B):
                        for j in range(HG):
                            v.tensor_copy(vc_all[j * M:(j + 1) * M, b, :, :], vh[b * M:(b + 1) * M, j:H1:HG, :])
                    dve.wait_ge(small_in, 80)
                    three_parts([b2p[:, s, :] for s in range(PARTS)], b2[:, :], b2r[:, :]).then_inc(b2_ready, 1)
                elif part == 5:
                    dve.wait_ge(small_in, 80)
                    then(v.tensor_tensor(qks_row[:, :], W("qs_row"), W("ks_row"), ALU.mult))
                    then(v.tensor_reduce(shift[:, :], qks_row[:, :], AX.X, ALU.max, apply_absolute_value=True))
                    then(v.tensor_scalar(shift[:, :], shift[:, :], SIM_SCALE, -EXP_ROOM, ALU.mult, ALU.add))
                    v.tensor_scalar(mbias[:, :], maskb[:, :], 1.0, MASKED, ALU.subtract, ALU.mult)
                    then(v.tensor_scalar(shift[:, :], shift[:, :], 0.0, -1.0, ALU.max, ALU.mult))
                    then(v.tensor_scalar(mbias[:, :], mbias[:, :], shift[:, :], None, ALU.add))
                    dve.wait_ge(su_pe, 9)
                    kc2 = kc_all[:, :, :, :, :].rearrange("p s h b m -> p s (h b m)")
                    then(v.tensor_copy(kc2[:, 0, :], PS[:, 5, :].bitcast(F16)))
                    last = swap_halves(kc2[:, 1, :], kc2[:, 0, :])
                    last.then_inc(su_dve, 1)

            def end_of_pass():
                dve.wait_ge(dve_step, steps[0])
                dve.sem_clear(dve_step)
                steps[0] = 0

            def split_low(n):
                nm, c0, cols = PIECES[n]
                at = split_at[nm][0] + c0
                dve.wait_ge(high_done, n + 1)
                v.scalar_tensor_tensor(halves[:, 1, at:at + cols], W(nm)[:, c0:c0 + cols], WS,
                                       halves[:, 0, at:at + cols], ALU.mult, ALU.subtract).then_inc(low_done, 1)

            def by_tile(src):
                return [src[:, t * P:(t + 1) * P] for t in range(NT)]

            def stats(hf, src):
                for t in range(NT):
                    last = v.bn_stats(stat[:, hf, t, :], by_tile(src)[t])
                then(last)
                for t in range(NT):
                    last = v.bn_aggr(mv[:, hf, t, :], stat[:, hf, t, :])
                last.then_inc(stats_ready[hf], 1)

            def normalise(hf, b, n, src):
                dve.wait_ge(stats_ready[hf], b * LNS[hf] + n)
                dve.wait_ge(rstd_ready[hf], b * LNS[hf] + n)
                for t in range(NT):
                    last = v.tensor_scalar(nrm[:, hf, t * P:(t + 1) * P], by_tile(src)[t], mv[:, hf, t, 0:1],
                                           rstd[:, hf, t:t + 1], ALU.subtract, ALU.mult)
                last.then_inc(nrm_ready[hf], 1)

            def with_row(data, row, op):
                d3 = data.rearrange("p (t f) -> p t f", f=P)
                return v.tensor_tensor(d3, d3, W(row).unsqueeze(1).broadcast_to([P, NT, P]), op)

            def add_normalised(hf, b, n, src, gain, base):
                dve.wait_ge(stats_ready[hf], b * LNS[hf] + n)
                for t in range(NT):
                    last = v.scalar_tensor_tensor(nrm[:, hf, t * P:(t + 1) * P], by_tile(src)[t], mv[:, hf, t, 0:1],
                                                  W(gain), ALU.subtract, ALU.mult)
                then(last)
                dve.wait_ge(rstd_ready[hf], b * LNS[hf] + n)
                for t in range(NT):
                    last = v.scalar_tensor_tensor(X[:, hf, t * P:(t + 1) * P], nrm[:, hf, t * P:(t + 1) * P],
                                                  rstd[:, hf, t:t + 1], by_tile(base)[t], ALU.mult, ALU.add)
                return last

            def add_residual(b, n, which, bias):
                dve.wait_ge(prod_psum[0], b * 3 + n)
                v.scalar_tensor_tensor(res[:, 0, :], bank(0, which), bias, feat[:, 0, :], ALU.add, ALU.add)\
                    .then_inc(res_ready[0], 1)

            def low_part(hf, dst, high, ready):
                dve.wait_ge(feat_ready[hf], ready)
                v.scalar_tensor_tensor(dst, feat[:, hf, :], AS, high, ALU.mult, ALU.subtract)\
                    .then_inc(split_ready[hf], 1)

            def pick(k, values, n, mx, top, hit):
                for t in range(NT):
                    last = v.max(mx[:, t, :], values[:, t, 0:n])
                then(last)
                then(v.tensor_copy(top[:, :, 0:k], mx[:, :, 0:k]))
                for t in range(NT):
                    last = v.match_replace(hit[:, t, 0:n + 8 - k], top[:, t, :], values[:, t, 0:n + 8 - k], PICK)
                then(last)

            def layer0(step, b):
                name, k = step if isinstance(step, tuple) else (step, 0)
                if name == "x_stats":
                    dve.wait_ge(x_loaded, 16 * (b + 1))
                    stats(0, X0)
                elif name == "x_norm":
                    normalise(0, b, 1, X0)
                elif name == "fold":
                    add_residual(b, 1, SA, fold_b[:, :])
                elif name == "fold_back":
                    dve.wait_ge(resT_psum[0], b * 4 + 1)
                    stats(0, bank(0, TR))
                elif name == "n1_norm":
                    normalise(0, b, 2, bank(0, TR))
                elif name == "scores":
                    dve.wait_ge(score_psum, b + 1)
                    s3 = PS[:, SA:SA + 2, :].rearrange("p a (g m) -> p (a g) m", m=M)
                    then(v.tensor_reduce(hmax[:, :], s3, AX.X, ALU.max))
                    v.tensor_tensor(sc.rearrange("p (g m) -> p g m", m=M), s3,
                                    hmax[:, :].unsqueeze(2).broadcast_to([P, NT * H0, M]), ALU.subtract)\
                        .then_inc(centred, 1)
                elif name == "exp0":
                    dve.wait_ge(exped, b + 1)
                    then(v.tensor_reduce(hsum[:, :], sc.rearrange("p (g m) -> p g m", m=M), AX.X, ALU.add))
                    v.reciprocal(hrec[:, :], hsum[:, :]).then_inc(rec_ready, 1)
                elif name == "probs_turn":
                    dve.wait_ge(probT_psum, b + 1)
                    v.tensor_copy(pT[:, 1, :], bank(0, SB_)).then_inc(pT1_ready, 1)
                elif name == "ca":
                    add_residual(b, 2, MM, W("mha_b"))
                elif name == "ca_back":
                    dve.wait_ge(resT_psum[0], b * 4 + 2)
                    stats(0, bank(0, TR))
                elif name == "n2_norm":
                    normalise(0, b, 3, bank(0, TR))
                elif name == "n2_turn":
                    low_part(0, xl[:, :], xh[:, :], b * TURNS + 3)
                elif name == "lin1":
                    if k == 0:
                        if isinstance(b, int):
                            dve.wait_ge(small_in, 80)
                        with_row(X0[:, :], "ln3_b", ALU.add)
                elif name == "lin2":
                    add_residual(b, 3, SA, W("lin2_b"))
                elif name == "lin2_back":
                    dve.wait_ge(resT_psum[0], b * 4 + 3)
                    stats(0, bank(0, TR))
                elif name == "n3_norm":
                    add_normalised(0, b, 4, bank(0, TR), "ln3_g", X0).then_inc(x0_free, 1)
                elif name == "y_stats":
                    dve.wait_ge(x0_free, b + 1)
                    stats(0, X[:, 0, :])
                elif name == "y_norm":
                    normalise(0, b, 5, X[:, 0, :])
                elif name == "y_turn":
                    low_part(0, xl[:, :], xh[:, :], b * TURNS + 4)
                elif name == "gate0":
                    dve.wait_ge(gate_psum[0], b + 1)
                    then(v.tensor_tensor(rt0[:, :, 0:E0], bank(0, SA)[:, 0:NT * E0].rearrange(
                        "p (t e) -> p t e", e=E0), W("gate_b").unsqueeze(1).broadcast_to([P, NT, E0]), ALU.add))
                    pick(K0, rt0, E0, mx0, top0, hit0)
                    then(v.scalar_tensor_tensor(comb0[:, :, :], hit0[:, :, 0:E0], PICK, rt0[:, :, 0:E0],
                                                ALU.is_ge, ALU.mult))
                    three_parts([part0[:, :, s, :] for s in range(PARTS)], comb0[:, :, :], hit0[:, :, 0:E0])\
                        .then_inc(comb_ready[0], 1)
                elif name == "expert":
                    dve.wait_ge(relu_ready, b * E0 + k + 1)
                    dve.wait_ge(w0_psum, b * E0 + k + 1)
                    if k >= 2:
                        dve.wait_ge(down_done, b * E0 + k - 1)
                    v.tensor_tensor(er[:, 2 + k % 2, :], bank(0, SA), er[:, k % 2, :], ALU.mult).then_inc(gated, 1)
                elif name == "moe_back":
                    dve.wait_ge(resT_psum[0], b * 4 + 4)
                    then(v.tensor_tensor(X[:, 0, :], bank(0, TR), X[:, 0, :], ALU.add))
                    stats(0, X[:, 0, :])
                elif name == "lat_norm":
                    normalise(0, b, 6, X[:, 0, :])
                elif name == "lat_turn":
                    low_part(0, latl[:, :], lath[:, :], b * TURNS + 5)

            def next_residual():
                then(v.tensor_copy(X[:, 1, :], X[:, 0, :]))

            def tiles(step, b):
                name, k = step
                n = b * NT + k + 1
                q3, k3 = (qk[:, a, :].rearrange("p (h d) -> p h d", d=D1) for a in range(2))
                if name == "qk_rows":
                    for a in range(2):
                        dve.wait_ge(sq_ready, 2 * (n - 1) + a + 1)
                        v.tensor_reduce(ssq[:, a * H1:(a + 1) * H1], sq[:, a, :].rearrange("p (h d) -> p h d", d=D1),
                                        AX.X, ALU.add).then_inc(ssq_ready, 1)
                elif name == "l2norm":
                    for a in range(2):
                        dve.wait_ge(rn_ready, 2 * (n - 1) + a + 1)
                        last = v.tensor_tensor(
                            (q3, k3)[a], bank(0, (MM, SA)[a]).rearrange("p (h d) -> p h d", d=D1),
                            rn[:, a * H1:(a + 1) * H1].unsqueeze(2).broadcast_to([P, H1, D1]), ALU.mult)
                    last.then_inc(qk_used, 1)
                elif name == "halves":
                    dve.wait_ge(qk_used, n)
                    if k > 0:
                        dve.wait_ge(kT_psum, n - 1)
                    v.tensor_copy(k16[:, :, 0:D1], k3)
                    then(v.tensor_tensor(q3, q3, qks_row[:, :].unsqueeze(1).broadcast_to([P, H1, D1]), ALU.mult))
                    v.tensor_tensor(k16[:, :, D1:2 * D1], k3, k16[:, :, 0:D1], ALU.subtract)
                    then(v.tensor_copy(q16[:, :, 0:D1], q3))
                    v.tensor_tensor(q16[:, :, D1:2 * D1], q3, q16[:, :, 0:D1], ALU.subtract).then_inc(low_ready, 1)
                elif name == "turn_A":
                    dve.wait_ge(qT_psum, n)
                    v.tensor_copy(qT[:, :, k * P:(k + 1) * P], bank(0, TR).bitcast(F16).rearrange(
                        "p (h k) -> p h k", k=P)).then_inc(qT_ready, 1)
                elif name == "turn_B":
                    dve.wait_ge(kA_ready, n)
                    swap_halves(*(z[:, :, k * P:(k + 1) * P] for z in (kB, kA))).then_inc(kB_ready, 1)

            s4 = sfc[:, :, :].rearrange("p t (g s) -> p t g s", s=GS)

            def layer1(step, b):
                name, k = step if isinstance(step, tuple) else (step, 0)
                if name == "attn":
                    if k == 1:
                        then(with_row(X[:, 1, :], "lno_b", ALU.add))
                    if k in PAIR_AT:
                        pair = PAIR_AT.index(k)
                        dve.wait_ge(head_out, b * H1 + 2 * pair + 2)
                        rec = den[pair % 2]
                        then(v.reciprocal(rec, rec))
                        v.tensor_tensor(aT[:, pair, :], on[:, pair % 2, :], rec, ALU.mult)\
                            .then_inc(pair_ready, 1)
                elif name == "wo_back":
                    dve.wait_ge(resT_psum[1], b * 2 + 1)
                    stats(1, bank(1, TR))
                elif name == "no_norm":
                    then(add_normalised(1, b, 1, bank(1, TR), "lno_w", X[:, 1, :]))
                elif name == "z_stats":
                    stats(1, X[:, 1, :])
                elif name == "z_norm":
                    normalise(1, b, 2, X[:, 1, :])
                elif name == "z_turn":
                    low_part(1, zl[:, :], zh[:, :], b + 1)
                elif name == "route":
                    dve.wait_ge(sig_ready, b + 1)
                    then(v.tensor_tensor(sfc[:, :, :], scor[:, :, :], W("route_b").unsqueeze(1).broadcast_to(
                        [P, NT, E1]), ALU.add))
                    then(v.tensor_reduce(grp[:, :, 0:NG], s4, AX.X, ALU.max))
                    pick(TG, grp, NG, mx1, topg, hitg)
                elif name == "route_pick":
                    then(v.tensor_scalar(hitg[:, :, 0:NG], hitg[:, :, 0:NG], PICK, None, ALU.is_ge))
                    then(v.tensor_tensor(cand[:, :, 0:E1].rearrange("p t (g s) -> p t g s", s=GS), s4,
                                         hitg[:, :, 0:NG].unsqueeze(3).broadcast_to([P, NT, NG, GS]), ALU.mult))
                    pick(K1, cand, E1, mx1, top1, hit1)
                    then(v.scalar_tensor_tensor(comb1[:, :, :], hit1[:, :, 0:E1], PICK, scor[:, :, :],
                                                ALU.is_ge, ALU.mult))
                    then(v.tensor_reduce(csum[:, :], comb1[:, :, :], AX.X, ALU.add))
                    then(v.tensor_scalar(csum[:, :], csum[:, :], 1e-20, None, ALU.add))
                    then(v.reciprocal(csum[:, :], csum[:, :]))
                    then(v.scalar_tensor_tensor(comb1[:, :, :], comb1[:, :, :], ROUTE_SCALE, csum[:, :].unsqueeze(2)
                                                .broadcast_to([P, NT, E1]), ALU.mult, ALU.mult))
                    three_parts([part1[:, :, s, :] for s in range(PARTS)], comb1[:, :, :], hit1[:, :, 0:E1])\
                        .then_inc(comb_ready[1], 1)
                elif name == "ffn":
                    dve.wait_ge(silu_ready, b * PLANES + k + 1)
                    dve.wait_ge(u_psum, b * PLANES + k + 1)
                    if k >= 2:
                        dve.wait_ge(ffn_down, b * PLANES + k - 1)
                    shared = k == EP
                    ins = v.scalar_tensor_tensor(fr[:, (2 if shared else 0) + k % 2, :], bank(1, MM), DS,
                                                 fr[:, k % 2, :], ALU.mult, ALU.mult)
                    if shared:
                        ins.then_inc(act_ready, 1)
                    else:
                        ins.then_inc(u_gated, 1)
                        dve.wait_ge(u_gated, b * EP + k + 1)
                        dve.wait_ge(w1_psum, b * EP + k + 1)
                        v.tensor_tensor(fr[:, 2 + k % 2, :], bank(1, SA), fr[:, k % 2, :], ALU.mult)\
                            .then_inc(act_ready, 1)
                elif name == "ffn_back":
                    dve.wait_ge(resT_psum[1], b * 2 + 2)
                    last = isinstance(b, int) and b == B - 1
                    if last:
                        dve.wait_ge(stored, 16 * (B - 1))
                    v.tensor_tensor(Y[:, :], bank(1, TR), X[:, 1, :], ALU.add).then_inc(y_ready, 1)
                    if not last:
                        dve.wait_ge(y_ready, b + 1)
                        next_residual()

            for step in PROLOGUE:
                if step[0] == "set_up":
                    set_up(step[1])
                elif step[0] == "split":
                    split_low(step[1])
                else:
                    layer0(step, 0)
            for step in sum(TILES, []):
                tiles(step, 0)
            next_residual()
            end_of_pass()
            with dve.Fori(0, B - 1) as i:
                for stream, step in BODY:
                    (layer0, layer1, tiles)[stream](step, i if stream == 1 else i + 1)
                end_of_pass()
            for step in LAYER1:
                layer1(step, B - 1)


def kernel(**inputs):
    import ml_dtypes
    import numpy as np
    import concourse.bacc as bacc
    from concourse.bass_utils import run_bass_kernel_spmd

    a = {k: np.asarray(v) for k, v in inputs.items()}
    f32, bf16 = np.float32, ml_dtypes.bfloat16

    def col(v):
        return np.ascontiguousarray(np.asarray(v).reshape(-1, P).T)

    def chunks(m):
        return m.reshape(-1, P, m.shape[1]).transpose(1, 0, 2).reshape(P, -1)

    qkv_w, qkv_b, in_w, in_b = (a["L0_xattn_" + n] for n in ("qkv_w", "qkv_b", "in_proj_w", "in_proj_b"))
    gu = a["L1_ffn_experts_gate_up"]
    part = {
        "ident": np.eye(P, dtype=f32),
        "head_of_row": (np.arange(P)[:, None] // D0 == np.arange(H0)[None]).astype(f32),
        "sa_b": col(a["L0_xattn_sa_out_b"]), "sa_bv": col(qkv_b[2 * P:]),
        "ln1_g": col(a["L0_xattn_ln1_g"]), "ln1_b": col(a["L0_xattn_ln1_b"]),
        "bq": col(in_b[:P]), "bk": col(in_b[P:2 * P]), "bv": col(in_b[2 * P:]),
        "mha_b": col(a["L0_xattn_mha_out_b"]),
        "ln2_g": col(a["L0_xattn_ln2_g"]), "ln2_b": col(a["L0_xattn_ln2_b"]),
        "lin1_b": col(a["L0_xattn_lin1_b"]), "lin2_b": col(a["L0_xattn_lin2_b"]),
        "b1": col(a["L0_ffn_b1"]),
        "lnl_w": col(a["L1_xattn_ln_l_w"]), "lnl_b": col(a["L1_xattn_ln_l_b"]),
        "lnx_w": col(a["L1_xattn_ln_x_w"]), "lnx_b": col(a["L1_xattn_ln_x_b"]),
        "sa_wv": qkv_w[2 * P:], "sa_oT": a["L0_xattn_sa_out_w"].T,
        "wqT": in_w[:P].T, "wkT": in_w[P:2 * P].T, "wvT": in_w[2 * P:].T,
        "mha_oT": a["L0_xattn_mha_out_w"].T,
        "lin1T": a["L0_xattn_lin1_w"].T, "lin2T": chunks(a["L0_xattn_lin2_w"].T),
        "Wk": a["L1_xattn_Wkv"][:, :INNER], "Wv": a["L1_xattn_Wkv"][:, INNER:],
        "gate_w": a["L0_ffn_gate_w"],
        "w1": a["L0_ffn_w1"].transpose(1, 0, 2).reshape(P, -1), "w2": a["L0_ffn_w2"].transpose(1, 0, 2).reshape(P, -1),
        "Wq": a["L1_xattn_Wq"], "Wo": chunks(a["L1_xattn_Wo"]),
        "route_wT": a["L1_ffn_gate_weight"].T,
        "gateT": gu[:, :I1].reshape(E1 * I1, P).T, "upT": gu[:, I1:].reshape(E1 * I1, P).T,
        "downT": chunks(a["L1_ffn_experts_down"].transpose(0, 2, 1).reshape(E1 * I1, P)),
        "sh_gateT": a["L1_ffn_shared_gate_w"].T, "sh_upT": a["L1_ffn_shared_up_w"].T,
        "sh_downT": a["L1_ffn_shared_down_w"].T,
        "ln3_g": a["L0_xattn_ln3_g"], "ln3_b": a["L0_xattn_ln3_b"],
        "lno_w": a["L1_xattn_ln_o_w"], "lno_b": a["L1_xattn_ln_o_b"],
        "gate_b": a["L0_ffn_gate_b"], "route_b": a["L1_ffn_e_score_correction_bias"],
        "qs_row": a["L1_xattn_q_scale"], "ks_row": a["L1_xattn_k_scale"],
    }
    slabs = [np.concatenate([part[n] for n, _ in s], axis=1) for s in (SLAB_A, SLAB_B, SLAB_S, SLAB_G, SLAB_H)]
    sel0 = np.arange(E0)[:, None] == np.repeat(np.arange(E0), P)[None]
    sel1 = np.arange(E1)[:, None] == np.repeat(np.arange(E1), I1)[None]
    arrays = {
        "x": a["x"], "ctx": a["ctx_1024"], "mask": np.tile(a["mask_BxS2_bk0"].T, (HG, 1)),
        **dict(zip(("slab_a", "slab_b", "slab_s", "slab_g", "slab_h"), slabs)),
        "rows": np.concatenate([part[n] for n, _ in ROWS])[None], "b2": np.tile(a["L0_ffn_b2"], (PARTS, 1)),
        "sel0": np.tile(sel0, (PARTS, 1)).astype(bf16), "sel1": np.tile(sel1, (PARTS, 1)).astype(bf16),
    }
    nc = bacc.Bacc("TRN2", target_bir_lowering=False, num_devices=1)
    nc.disable_value_cache = True
    arrays = {k: np.ascontiguousarray(v) for k, v in arrays.items()}
    args = [nc.dram_tensor(k, v.shape, mybir.dt.from_np(v.dtype), kind="ExternalInput").ap()
            for k, v in arrays.items()]
    args.append(nc.dram_tensor("out", (B, S, P), F32, kind="ExternalOutput").ap())
    two_layer_kernel(nc, *args)
    return run_bass_kernel_spmd(nc, [arrays], core_ids=[0]).results[0]["out"]
```
